# Optimizing a Trainium2 kernel written in Bass

```python
import numpy as np
import jax
import jax.numpy as jnp

def _softmax(x, axis=-1):
    return jax.nn.softmax(x, axis=axis)

def _gelu(x):
    return jax.nn.gelu(x, approximate=True)

def _silu(x):
    return jax.nn.silu(x)

def _sigmoid(x):
    return jax.nn.sigmoid(x)

def _layernorm(x, axis=-1, eps=1e-05):
    m = jnp.mean(x, axis=axis, keepdims=True)
    v = jnp.var(x, axis=axis, keepdims=True)
    return (x - m) / jnp.sqrt(v + eps)

def _scatter_add(tgt, idx, src, axis=0):
    return tgt.at[idx].add(src)

def _segment_sum(src, seg, n):
    return jax.ops.segment_sum(src, seg, n)
kernel_name = 'mk_perceiver_d2_seqx_r2_989c77'

def setup_inputs(seed: int=0):
    np.random.seed(seed)
    _w = jnp.asarray

    def _rec_inputs():
        import jax
        import jax.numpy as jnp
        _rk = jax.random.key(seed)
        x = 7.22e-05 + 1 * jax.random.normal(jax.random.fold_in(_rk, 1), (1, 512, 512), jnp.float32)
        _lenS = 512 - jax.random.randint(jax.random.fold_in(_rk, 7), (1,), 0, max(1, 512 // 4) + 1, jnp.int32)
        _lenS2 = 8192 - jax.random.randint(jax.random.fold_in(_rk, 8), (1,), 0, max(1, 8192 // 4) + 1, jnp.int32)
        _ctx_1024P = jax.random.normal(jax.random.fold_in(_rk, 11), (1, 16, 512), jnp.float32)
        _ctx_1024c = jax.random.dirichlet(jax.random.fold_in(_rk, 511), 0.3 * jnp.ones((16,), jnp.float32), (1, 8192))
        _ctx_1024t = jnp.einsum('bsk,bkd->bsd', _ctx_1024c, _ctx_1024P)
        _ctx_1024t = _ctx_1024t * jax.lax.rsqrt(jnp.mean(jnp.square(_ctx_1024t)) + 1e-12) * 0.953939
        ctx_1024 = 4.13588e-05 + 0.999923 * (_ctx_1024t + 0.3 * jax.random.normal(jax.random.fold_in(_rk, 611), (1, 8192, 512), jnp.float32))
        return (x, ctx_1024)
    x, ctx_1024 = _rec_inputs()

    def _L0_xattn_setup():
        import jax, jax.numpy as jnp
        import numpy as np
        D_MODEL = 512
        NUM_HEADS = 16
        DEPTH = D_MODEL // NUM_HEADS

        def _split_heads(x):
            B, S, _ = x.shape
            return x.reshape(B, S, NUM_HEADS, DEPTH).transpose(0, 2, 1, 3)
        key = jax.random.key(seed)
        ks = jax.random.split(key, 11)
        B, S = (4, 1024)
        scale = 1.0 / np.sqrt(D_MODEL)
        inp = {'Q': jax.random.normal(ks[0], (B, S, D_MODEL), jnp.float32), 'K': jax.random.normal(ks[1], (B, S, D_MODEL), jnp.float32), 'V': jax.random.normal(ks[2], (B, S, D_MODEL), jnp.float32), 'W_Q': jax.random.normal(ks[3], (D_MODEL, D_MODEL), jnp.float32) * scale, 'b_Q': jnp.zeros((D_MODEL,), jnp.float32), 'W_K': jax.random.normal(ks[4], (D_MODEL, D_MODEL), jnp.float32) * scale, 'b_K': jnp.zeros((D_MODEL,), jnp.float32), 'W_V': jax.random.normal(ks[5], (D_MODEL, D_MODEL), jnp.float32) * scale, 'b_V': jnp.zeros((D_MODEL,), jnp.float32), 'W_O': jax.random.normal(ks[6], (D_MODEL, D_MODEL), jnp.float32) * scale, 'b_O': jnp.zeros((D_MODEL,), jnp.float32)}
        return inp
    _L0_xattn_all = _L0_xattn_setup()
    _L0_xattn_in = {k: v for k, v in _L0_xattn_all.items() if k in ('W_Q', 'b_Q', 'W_K', 'b_K', 'W_V', 'b_V', 'W_O', 'b_O')}
    del _L0_xattn_all

    def _L0_attn_setup():
        import jax, jax.numpy as jnp
        import numpy as np
        DIM = 512
        INNER = DIM // 2
        DSTATE = 8
        KSZ = 3
        DTRANK = max(INNER // 8, 4)
        B, L = (4, 2048)

        def _dwconv_silu(u, kern):
            c = u.shape[-1]
            v = jnp.transpose(u, (0, 2, 1))
            v = jax.lax.conv_general_dilated(v, kern, (1,), [(KSZ // 2, KSZ // 2)], dimension_numbers=('NCH', 'OIH', 'NCH'), feature_group_count=c)
            return jax.nn.silu(jnp.transpose(v, (0, 2, 1)))

        def _forward(x, W_in, Kx, Kz, W_xproj, W_dt, b_dt, A_log, D, W_out):
            h = jnp.einsum('bld,ed->ble', x, W_in)
            xb, zb = jnp.split(h, 2, axis=-1)
            xb = _dwconv_silu(xb, Kx)
            zb = _dwconv_silu(zb, Kz)
            proj = jnp.einsum('blc,oc->blo', xb, W_xproj)
            dt_raw = proj[..., :DTRANK]
            b_raw = proj[..., DTRANK:DTRANK + DSTATE]
            c_raw = proj[..., DTRANK + DSTATE:]
            delta = jnp.clip(jax.nn.softplus(jnp.einsum('blr,cr->blc', dt_raw, W_dt) + b_dt), 0.0001, 1.0)
            b_term = jnp.tanh(b_raw)
            c_term = jnp.tanh(c_raw)
            a = jax.nn.softplus(A_log) + 0.0001
            decay = jnp.clip(jnp.exp(-delta[..., None] * a), 0.0001, 1.0)
            drive = (1.0 - decay) * (b_term[:, :, None, :] * xb[..., None])

            def step(state, inp):
                dec_t, drv_t, c_t, x_t = inp
                state = dec_t * state + drv_t
                y = jnp.sum(state * c_t[:, None, :], axis=-1) + D * x_t
                return (state, y)
            tm = lambda t: jnp.moveaxis(t, 1, 0)
            state0 = jnp.zeros((x.shape[0], INNER, DSTATE), dtype=jnp.float32)
            _, ys = jax.lax.scan(step, state0, (tm(decay), tm(drive), tm(c_term), tm(xb)))
            y = jnp.moveaxis(ys, 0, 1)
            return jnp.einsum('bld,ed->ble', jnp.concatenate([y, zb], axis=-1), W_out)
        key = jax.random.key(seed)
        ks = jax.random.split(key, 8)
        s = 0.02
        x = jax.random.normal(ks[0], (B, L, DIM), dtype=jnp.float32)
        W_in = jax.random.normal(ks[1], (DIM, DIM), dtype=jnp.float32) * s
        Kx = jax.random.normal(ks[2], (INNER, 1, KSZ), dtype=jnp.float32) * 0.1
        Kz = jax.random.normal(ks[3], (INNER, 1, KSZ), dtype=jnp.float32) * 0.1
        W_xproj = jax.random.normal(ks[4], (DTRANK + 2 * DSTATE, INNER), dtype=jnp.float32) * s
        W_dt = jax.random.normal(ks[5], (INNER, DTRANK), dtype=jnp.float32) * s
        dt_init = jnp.exp(jnp.linspace(jnp.log(0.02), jnp.log(0.2), INNER))
        b_dt = jnp.log(jnp.expm1(dt_init)).astype(jnp.float32)
        A_log = jnp.log(jnp.tile(jnp.arange(1, DSTATE + 1, dtype=jnp.float32), (INNER, 1)))
        D = jnp.ones((INNER,), dtype=jnp.float32)
        W_out = jax.random.normal(ks[6], (DIM, DIM), dtype=jnp.float32) * s
        return {'x': x, 'W_in': W_in, 'Kx': Kx, 'Kz': Kz, 'W_xproj': W_xproj, 'W_dt': W_dt, 'b_dt': b_dt, 'A_log': A_log, 'D': D, 'W_out': W_out}
    _L0_attn_all = _L0_attn_setup()
    _L0_attn_in = {k: v for k, v in _L0_attn_all.items() if k in ('W_in', 'Kx', 'Kz', 'W_xproj', 'W_dt', 'b_dt', 'A_log', 'D', 'W_out')}
    del _L0_attn_all

    def _L0_ffn_setup():
        import jax, jax.numpy as jnp
        import numpy as np
        CAPACITY_FACTOR = 1.25
        key = jax.random.key(seed)
        k1, k2, k3, k4 = jax.random.split(key, 4)
        B, T, D, F, E = (4, 2048, 512, 2048, 8)
        s = 0.02
        return {'x': jax.random.normal(k1, (B, T, D), dtype=jnp.float32), 'wg': jax.random.normal(k2, (D, E), dtype=jnp.float32) * s, 'W1': jax.random.normal(k3, (E, D, F), dtype=jnp.float32) * s, 'b1': jnp.zeros((E, F), dtype=jnp.float32), 'W2': jax.random.normal(k4, (E, F, D), dtype=jnp.float32) * s, 'b2': jnp.zeros((E, D), dtype=jnp.float32)}
    _L0_ffn_all = _L0_ffn_setup()
    _L0_ffn_in = {k: v for k, v in _L0_ffn_all.items() if k in ('wg', 'W1', 'b1', 'W2', 'b2')}
    del _L0_ffn_all

    def _L1_xattn_setup():
        import jax, jax.numpy as jnp
        import numpy as np
        EMBED_DIM = 512
        NUM_HEADS = 16
        HEAD_DIM = EMBED_DIM // NUM_HEADS
        B, T, S = (2, 1024, 1024)
        key = jax.random.key(seed)
        ks = jax.random.split(key, 5)
        scale_w = 1.0 / np.sqrt(EMBED_DIM)
        return {'q': jax.random.normal(ks[0], (B, T, EMBED_DIM), dtype=jnp.float32), 'k': jax.random.normal(ks[1], (B, S, EMBED_DIM), dtype=jnp.float32), 'v': jax.random.normal(ks[2], (B, S, EMBED_DIM), dtype=jnp.float32), 'in_proj_weight': jax.random.normal(ks[3], (3 * EMBED_DIM, EMBED_DIM), dtype=jnp.float32) * scale_w, 'in_proj_bias': jnp.zeros((3 * EMBED_DIM,), dtype=jnp.float32), 'out_w': jax.random.normal(ks[4], (EMBED_DIM, EMBED_DIM), dtype=jnp.float32) * scale_w, 'out_b': jnp.zeros((EMBED_DIM,), dtype=jnp.float32)}
    _L1_xattn_all = _L1_xattn_setup()
    _L1_xattn_in = {k: v for k, v in _L1_xattn_all.items() if k in ('in_proj_weight', 'in_proj_bias', 'out_w', 'out_b')}
    del _L1_xattn_all

    def _L1_attn_setup():
        import jax, jax.numpy as jnp
        import numpy as np
        from jax import lax
        B, T, D, H, CONV_K = (4, 1024, 512, 4, 4)
        DH = D // H
        EPS = 1e-05

        def _depthwise_causal_conv(u, w):
            K = w.shape[0]
            u_pad = jnp.pad(u, ((0, 0), (K - 1, 0), (0, 0)))
            kern = w[:, None, :]
            return lax.conv_general_dilated(u_pad, kern, (1,), 'VALID', dimension_numbers=('NWC', 'WIO', 'NWC'), feature_group_count=u.shape[-1])

        def _l2norm(x):
            return x * lax.rsqrt(jnp.sum(x * x, axis=-1, keepdims=True) + 1e-06)

        def _delta_rule(q, k, v, beta):

            def step(S, inp):
                q_t, k_t, v_t, b_t = inp
                kS = jnp.einsum('bhk,bhkv->bhv', k_t, S)
                delta = (v_t - kS) * b_t[..., None]
                S = S + jnp.einsum('bhk,bhv->bhkv', k_t, delta)
                o_t = jnp.einsum('bhk,bhkv->bhv', q_t, S)
                return (S, o_t)
            S0 = jnp.zeros((q.shape[0], q.shape[2], q.shape[3], v.shape[3]), dtype=q.dtype)
            tm = lambda a: jnp.swapaxes(a, 0, 1)
            _, o = lax.scan(step, S0, (tm(q), tm(k), tm(v), jnp.swapaxes(beta, 0, 1)))
            return jnp.swapaxes(o, 0, 1)
        key = jax.random.key(seed)
        ks = jax.random.split(key, 10)
        s = 0.02
        return {'x': jax.random.normal(ks[0], (B, T, D), dtype=jnp.float32), 'Wq': jax.random.normal(ks[1], (D, D), dtype=jnp.float32) * s, 'Wk': jax.random.normal(ks[2], (D, D), dtype=jnp.float32) * s, 'Wv': jax.random.normal(ks[3], (D, D), dtype=jnp.float32) * s, 'Wb': jax.random.normal(ks[4], (D, H), dtype=jnp.float32) * s, 'conv_q': jax.random.normal(ks[5], (CONV_K, D), dtype=jnp.float32) * 0.1, 'conv_k': jax.random.normal(ks[6], (CONV_K, D), dtype=jnp.float32) * 0.1, 'conv_v': jax.random.normal(ks[7], (CONV_K, D), dtype=jnp.float32) * 0.1, 'g_rms': jnp.ones((DH,), dtype=jnp.float32), 'Wo': jax.random.normal(ks[8], (D, D), dtype=jnp.float32) * s, 'ln_g': jnp.ones((D,), dtype=jnp.float32), 'ln_b': jnp.zeros((D,), dtype=jnp.float32)}
    _L1_attn_all = _L1_attn_setup()
    _L1_attn_in = {k: v for k, v in _L1_attn_all.items() if k in ('Wq', 'Wk', 'Wv', 'Wb', 'conv_q', 'conv_k', 'conv_v', 'g_rms', 'Wo', 'ln_g', 'ln_b')}
    del _L1_attn_all

    def _L1_ffn_setup():
        import jax, jax.numpy as jnp
        import numpy as np
        TOP_K = 2
        NUM_EXPERTS = 8
        B, T, H, F = (4, 1024, 512, 2048)
        key = jax.random.key(seed)
        ks = jax.random.split(key, 6)
        s_in = 1.0 / np.sqrt(H)
        s_ff = 1.0 / np.sqrt(F)
        return {'x': jax.random.normal(ks[0], (B, T, H), dtype=jnp.float32), 'router_w': jax.random.normal(ks[1], (NUM_EXPERTS, H), dtype=jnp.float32) * s_in, 'router_b': jax.random.normal(ks[2], (NUM_EXPERTS,), dtype=jnp.float32) * 0.01, 'gate_w': jax.random.normal(ks[3], (NUM_EXPERTS, F, H), dtype=jnp.float32) * s_in, 'up_w': jax.random.normal(ks[4], (NUM_EXPERTS, F, H), dtype=jnp.float32) * s_in, 'down_w': jax.random.normal(ks[5], (NUM_EXPERTS, H, F), dtype=jnp.float32) * s_ff}
    _L1_ffn_all = _L1_ffn_setup()
    _L1_ffn_in = {k: v for k, v in _L1_ffn_all.items() if k in ('router_w', 'router_b', 'gate_w', 'up_w', 'down_w')}
    del _L1_ffn_all
    return {'x': x, 'ctx_1024': ctx_1024, 'L0_xattn_W_Q': _L0_xattn_in['W_Q'], 'L0_xattn_b_Q': _L0_xattn_in['b_Q'], 'L0_xattn_W_K': _L0_xattn_in['W_K'], 'L0_xattn_b_K': _L0_xattn_in['b_K'], 'L0_xattn_W_V': _L0_xattn_in['W_V'], 'L0_xattn_b_V': _L0_xattn_in['b_V'], 'L0_xattn_W_O': _L0_xattn_in['W_O'], 'L0_xattn_b_O': _L0_xattn_in['b_O'], 'L0_attn_W_in': _L0_attn_in['W_in'], 'L0_attn_Kx': _L0_attn_in['Kx'], 'L0_attn_Kz': _L0_attn_in['Kz'], 'L0_attn_W_xproj': _L0_attn_in['W_xproj'], 'L0_attn_W_dt': _L0_attn_in['W_dt'], 'L0_attn_b_dt': _L0_attn_in['b_dt'], 'L0_attn_A_log': _L0_attn_in['A_log'], 'L0_attn_D': _L0_attn_in['D'], 'L0_attn_W_out': _L0_attn_in['W_out'], 'L0_ffn_wg': _L0_ffn_in['wg'], 'L0_ffn_W1': _L0_ffn_in['W1'], 'L0_ffn_b1': _L0_ffn_in['b1'], 'L0_ffn_W2': _L0_ffn_in['W2'], 'L0_ffn_b2': _L0_ffn_in['b2'], 'L1_xattn_in_proj_weight': _L1_xattn_in['in_proj_weight'], 'L1_xattn_in_proj_bias': _L1_xattn_in['in_proj_bias'], 'L1_xattn_out_w': _L1_xattn_in['out_w'], 'L1_xattn_out_b': _L1_xattn_in['out_b'], 'L1_attn_Wq': _L1_attn_in['Wq'], 'L1_attn_Wk': _L1_attn_in['Wk'], 'L1_attn_Wv': _L1_attn_in['Wv'], 'L1_attn_Wb': _L1_attn_in['Wb'], 'L1_attn_conv_q': _L1_attn_in['conv_q'], 'L1_attn_conv_k': _L1_attn_in['conv_k'], 'L1_attn_conv_v': _L1_attn_in['conv_v'], 'L1_attn_g_rms': _L1_attn_in['g_rms'], 'L1_attn_Wo': _L1_attn_in['Wo'], 'L1_attn_ln_g': _L1_attn_in['ln_g'], 'L1_attn_ln_b': _L1_attn_in['ln_b'], 'L1_ffn_router_w': _L1_ffn_in['router_w'], 'L1_ffn_router_b': _L1_ffn_in['router_b'], 'L1_ffn_gate_w': _L1_ffn_in['gate_w'], 'L1_ffn_up_w': _L1_ffn_in['up_w'], 'L1_ffn_down_w': _L1_ffn_in['down_w']}

def reference(x, ctx_1024, L0_xattn_W_Q, L0_xattn_b_Q, L0_xattn_W_K, L0_xattn_b_K, L0_xattn_W_V, L0_xattn_b_V, L0_xattn_W_O, L0_xattn_b_O, L0_attn_W_in, L0_attn_Kx, L0_attn_Kz, L0_attn_W_xproj, L0_attn_W_dt, L0_attn_b_dt, L0_attn_A_log, L0_attn_D, L0_attn_W_out, L0_ffn_wg, L0_ffn_W1, L0_ffn_b1, L0_ffn_W2, L0_ffn_b2, L1_xattn_in_proj_weight, L1_xattn_in_proj_bias, L1_xattn_out_w, L1_xattn_out_b, L1_attn_Wq, L1_attn_Wk, L1_attn_Wv, L1_attn_Wb, L1_attn_conv_q, L1_attn_conv_k, L1_attn_conv_v, L1_attn_g_rms, L1_attn_Wo, L1_attn_ln_g, L1_attn_ln_b, L1_ffn_router_w, L1_ffn_router_b, L1_ffn_gate_w, L1_ffn_up_w, L1_ffn_down_w):
    import jax
    import jax.numpy as jnp

    def _L0_xattn_ref(Q, K, V, W_Q, b_Q, W_K, b_K, W_V, b_V, W_O, b_O):
        import jax, jax.numpy as jnp
        import numpy as np
        D_MODEL = 512
        NUM_HEADS = 16
        DEPTH = D_MODEL // NUM_HEADS

        def _split_heads(x):
            B, S, _ = x.shape
            return x.reshape(B, S, NUM_HEADS, DEPTH).transpose(0, 2, 1, 3)
        q = _split_heads(Q @ W_Q + b_Q)
        k = _split_heads(K @ W_K + b_K)
        v = _split_heads(V @ W_V + b_V)
        scores = jnp.einsum('bhqd,bhkd->bhqk', q, k) / jnp.sqrt(jnp.float32(DEPTH))
        attn = jax.nn.softmax(scores, axis=-1)
        out = jnp.einsum('bhqk,bhkd->bhqd', attn, v)
        B, H, S, d = out.shape
        out = out.transpose(0, 2, 1, 3).reshape(B, S, H * d)
        return out @ W_O + b_O

    def _L0_attn_ref(x, W_in, Kx, Kz, W_xproj, W_dt, b_dt, A_log, D, W_out):
        import jax, jax.numpy as jnp
        import numpy as np
        DIM = 512
        INNER = DIM // 2
        DSTATE = 8
        KSZ = 3
        DTRANK = max(INNER // 8, 4)
        B, L = (4, 2048)

        def _dwconv_silu(u, kern):
            c = u.shape[-1]
            v = jnp.transpose(u, (0, 2, 1))
            v = jax.lax.conv_general_dilated(v, kern, (1,), [(KSZ // 2, KSZ // 2)], dimension_numbers=('NCH', 'OIH', 'NCH'), feature_group_count=c)
            return jax.nn.silu(jnp.transpose(v, (0, 2, 1)))

        def _forward(x, W_in, Kx, Kz, W_xproj, W_dt, b_dt, A_log, D, W_out):
            h = jnp.einsum('bld,ed->ble', x, W_in)
            xb, zb = jnp.split(h, 2, axis=-1)
            xb = _dwconv_silu(xb, Kx)
            zb = _dwconv_silu(zb, Kz)
            proj = jnp.einsum('blc,oc->blo', xb, W_xproj)
            dt_raw = proj[..., :DTRANK]
            b_raw = proj[..., DTRANK:DTRANK + DSTATE]
            c_raw = proj[..., DTRANK + DSTATE:]
            delta = jnp.clip(jax.nn.softplus(jnp.einsum('blr,cr->blc', dt_raw, W_dt) + b_dt), 0.0001, 1.0)
            b_term = jnp.tanh(b_raw)
            c_term = jnp.tanh(c_raw)
            a = jax.nn.softplus(A_log) + 0.0001
            decay = jnp.clip(jnp.exp(-delta[..., None] * a), 0.0001, 1.0)
            drive = (1.0 - decay) * (b_term[:, :, None, :] * xb[..., None])

            def step(state, inp):
                dec_t, drv_t, c_t, x_t = inp
                state = dec_t * state + drv_t
                y = jnp.sum(state * c_t[:, None, :], axis=-1) + D * x_t
                return (state, y)
            tm = lambda t: jnp.moveaxis(t, 1, 0)
            state0 = jnp.zeros((x.shape[0], INNER, DSTATE), dtype=jnp.float32)
            _, ys = jax.lax.scan(step, state0, (tm(decay), tm(drive), tm(c_term), tm(xb)))
            y = jnp.moveaxis(ys, 0, 1)
            return jnp.einsum('bld,ed->ble', jnp.concatenate([y, zb], axis=-1), W_out)
        return _forward(x, W_in, Kx, Kz, W_xproj, W_dt, b_dt, A_log, D, W_out)

    def _L0_ffn_ref(x, wg, W1, b1, W2, b2):
        import jax, jax.numpy as jnp
        import numpy as np
        CAPACITY_FACTOR = 1.25
        B, T, D = x.shape
        E = wg.shape[1]
        N = B * T
        capacity = int(N / E * CAPACITY_FACTOR) + 1
        xf = x.reshape(N, D)
        logits = xf @ wg
        scores = jax.nn.softmax(logits, axis=-1)
        top1 = jnp.argmax(scores, axis=-1)
        combine_w = jnp.take_along_axis(scores, top1[:, None], axis=1)[:, 0]
        oh = jax.nn.one_hot(top1, E, dtype=jnp.int32)
        rank = jnp.take_along_axis(jnp.cumsum(oh, axis=0), top1[:, None], axis=1)[:, 0] - 1
        valid = rank < capacity
        trash = E * capacity
        slot = jnp.where(valid, top1 * capacity + rank, trash)
        buf = jnp.zeros((E * capacity + 1, D), dtype=x.dtype).at[slot].set(xf)
        eb = buf[:E * capacity].reshape(E, capacity, D)
        h = jax.nn.gelu(jnp.einsum('ecd,edf->ecf', eb, W1) + b1[:, None, :], approximate=False)
        y = jnp.einsum('ecf,efd->ecd', h, W2) + b2[:, None, :]
        yf = y.reshape(E * capacity, D)
        gathered = yf[jnp.minimum(slot, E * capacity - 1)]
        out_flat = jnp.where(valid[:, None], gathered, 0.0) * combine_w[:, None]
        return out_flat.reshape(B, T, D)

    def _L1_xattn_ref(q, k, v, in_proj_weight, in_proj_bias, out_w, out_b):
        import jax, jax.numpy as jnp
        import numpy as np
        EMBED_DIM = 512
        NUM_HEADS = 16
        HEAD_DIM = EMBED_DIM // NUM_HEADS
        B, T, S = (2, 1024, 1024)
        H, D = (NUM_HEADS, HEAD_DIM)
        w_q, w_k, w_v = jnp.split(in_proj_weight, 3, axis=0)
        b_q, b_k, b_v = jnp.split(in_proj_bias, 3, axis=0)
        qp = q @ w_q.T + b_q
        kp = k @ w_k.T + b_k
        vp = v @ w_v.T + b_v
        bsz, t, _ = qp.shape
        s = kp.shape[1]
        qh = qp.reshape(bsz, t, H, D).transpose(0, 2, 1, 3)
        kh = kp.reshape(bsz, s, H, D).transpose(0, 2, 1, 3)
        vh = vp.reshape(bsz, s, H, D).transpose(0, 2, 1, 3)
        scale = D ** (-0.5)
        attn = jnp.einsum('bhtd,bhsd->bhts', qh, kh) * scale
        attn = jax.nn.softmax(attn, axis=-1)
        ctx = jnp.einsum('bhts,bhsd->bhtd', attn, vh)
        ctx = ctx.transpose(0, 2, 1, 3).reshape(bsz, t, H * D)
        out = ctx @ out_w.T + out_b
        return out

    def _L1_attn_ref(x, Wq, Wk, Wv, Wb, conv_q, conv_k, conv_v, g_rms, Wo, ln_g, ln_b):
        import jax, jax.numpy as jnp
        import numpy as np
        from jax import lax
        B, T, D, H, CONV_K = (4, 1024, 512, 4, 4)
        DH = D // H
        EPS = 1e-05

        def _depthwise_causal_conv(u, w):
            K = w.shape[0]
            u_pad = jnp.pad(u, ((0, 0), (K - 1, 0), (0, 0)))
            kern = w[:, None, :]
            return lax.conv_general_dilated(u_pad, kern, (1,), 'VALID', dimension_numbers=('NWC', 'WIO', 'NWC'), feature_group_count=u.shape[-1])

        def _l2norm(x):
            return x * lax.rsqrt(jnp.sum(x * x, axis=-1, keepdims=True) + 1e-06)

        def _delta_rule(q, k, v, beta):

            def step(S, inp):
                q_t, k_t, v_t, b_t = inp
                kS = jnp.einsum('bhk,bhkv->bhv', k_t, S)
                delta = (v_t - kS) * b_t[..., None]
                S = S + jnp.einsum('bhk,bhv->bhkv', k_t, delta)
                o_t = jnp.einsum('bhk,bhkv->bhv', q_t, S)
                return (S, o_t)
            S0 = jnp.zeros((q.shape[0], q.shape[2], q.shape[3], v.shape[3]), dtype=q.dtype)
            tm = lambda a: jnp.swapaxes(a, 0, 1)
            _, o = lax.scan(step, S0, (tm(q), tm(k), tm(v), jnp.swapaxes(beta, 0, 1)))
            return jnp.swapaxes(o, 0, 1)
        silu = jax.nn.silu
        q = silu(_depthwise_causal_conv(x @ Wq, conv_q))
        k = silu(_depthwise_causal_conv(x @ Wk, conv_k))
        v = silu(_depthwise_causal_conv(x @ Wv, conv_v))
        beta = jax.nn.sigmoid(x @ Wb)
        hs = lambda a: a.reshape(a.shape[0], a.shape[1], H, DH)
        q, k, v = (_l2norm(hs(q)), _l2norm(hs(k)), hs(v))
        o = _delta_rule(q, k, v, beta)
        o = o * lax.rsqrt(jnp.mean(o * o, axis=-1, keepdims=True) + EPS) * g_rms
        y = o.reshape(x.shape[0], x.shape[1], D) @ Wo
        y = y + x
        mu = jnp.mean(y, axis=-1, keepdims=True)
        var = jnp.mean((y - mu) ** 2, axis=-1, keepdims=True)
        y = (y - mu) * lax.rsqrt(var + EPS) * ln_g + ln_b
        return y

    def _L1_ffn_ref(x, router_w, router_b, gate_w, up_w, down_w):
        import jax, jax.numpy as jnp
        import numpy as np
        TOP_K = 2
        NUM_EXPERTS = 8
        B, T, H, F = (4, 1024, 512, 2048)
        logits = jnp.einsum('bth,eh->bte', x, router_w) + router_b
        topv, topi = jax.lax.top_k(logits, TOP_K)
        gates = jax.nn.softmax(topv, axis=-1)

        def body(acc, inputs):
            e, gw, uw, dw = inputs
            w = jnp.sum(gates * (topi == e), axis=-1)
            h = jax.nn.silu(jnp.einsum('bth,fh->btf', x, gw)) * jnp.einsum('bth,fh->btf', x, uw)
            y = jnp.einsum('btf,hf->bth', h, dw)
            return (acc + y * w[..., None], None)
        init = jnp.zeros_like(x)
        xs = (jnp.arange(NUM_EXPERTS), gate_w, up_w, down_w)
        out, _ = jax.lax.scan(body, init, xs)
        return out
    x = x + _L0_xattn_ref(_layernorm(x, axis=-1), ctx_1024, ctx_1024, L0_xattn_W_Q, L0_xattn_b_Q, L0_xattn_W_K, L0_xattn_b_K, L0_xattn_W_V, L0_xattn_b_V, L0_xattn_W_O, L0_xattn_b_O)
    x = x + _L0_attn_ref(_layernorm(x, axis=-1), L0_attn_W_in, L0_attn_Kx, L0_attn_Kz, L0_attn_W_xproj, L0_attn_W_dt, L0_attn_b_dt, L0_attn_A_log, L0_attn_D, L0_attn_W_out)
    x = x + _L0_ffn_ref(_layernorm(x, axis=-1), L0_ffn_wg, L0_ffn_W1, L0_ffn_b1, L0_ffn_W2, L0_ffn_b2)
    x = x + _L1_xattn_ref(_layernorm(x, axis=-1), ctx_1024, ctx_1024, L1_xattn_in_proj_weight, L1_xattn_in_proj_bias, L1_xattn_out_w, L1_xattn_out_b)
    x = x + _L1_attn_ref(_layernorm(x, axis=-1), L1_attn_Wq, L1_attn_Wk, L1_attn_Wv, L1_attn_Wb, L1_attn_conv_q, L1_attn_conv_k, L1_attn_conv_v, L1_attn_g_rms, L1_attn_Wo, L1_attn_ln_g, L1_attn_ln_b)
    x = x + _L1_ffn_ref(_layernorm(x, axis=-1), L1_ffn_router_w, L1_ffn_router_b, L1_ffn_gate_w, L1_ffn_up_w, L1_ffn_down_w)
    return x

_drawn_inputs = setup_inputs


def setup_inputs(seed=0):
    import zlib

    import numpy as np

    out = dict(_drawn_inputs(seed))
    spreads = {'L0_xattn_b_Q': (0.0, 0.3),
     'L0_xattn_b_K': (0.0, 0.8),
     'L0_xattn_b_V': (0.0, 0.1),
     'L0_xattn_b_O': (0.0, 0.1),
     'L0_attn_D': (1.0, 0.6),
     'L0_ffn_b1': (0.0, 0.587),
     'L0_ffn_b2': (0.0, 0.282),
     'L1_xattn_in_proj_bias': (0.0, 0.1),
     'L1_xattn_out_b': (0.0, 0.1),
     'L1_attn_g_rms': (1.0, 0.2),
     'L1_attn_ln_g': (1.0, 0.2),
     'L1_attn_ln_b': (0.0, 0.1)}
    factors = {'L0_attn_W_xproj': 8.0,
     'L0_attn_W_dt': 8.0,
     'L0_attn_b_dt': 8.0,
     'L0_attn_A_log': 8.0,
     'L1_ffn_router_b': 4.902}
    for name, (base, spread) in spreads.items():
        noise = np.random.default_rng([zlib.crc32(name.encode()), seed]).standard_normal(out[name].shape)
        drawn = base * np.exp(spread * noise) if base else spread * noise
        out[name] = jnp.asarray(drawn.astype(out[name].dtype))
    for name, factor in factors.items():
        out[name] = (out[name] * factor).astype(out[name].dtype)
    return out
```

```python
from contextlib import ExitStack, contextmanager

import concourse.bass as bass
from concourse import mybir

F32 = mybir.dt.float32
F32R = mybir.dt.float32r
I32 = mybir.dt.int32
U32 = mybir.dt.uint32
ALU = mybir.AluOpType
ACT = mybir.ActivationFunctionType
X = mybir.AxisListType.X

P = 128
TOK, D = 512, 512
TT, KD = TOK // P, D // P
KEYS = 8192
CHUNK = 512
NCHUNK = KEYS // CHUNK
KT = KEYS // P
HEADS, DH = 16, 32
EPS = 1e-5
INNER, DSTATE, DTRANK = 256, 8, 32
DHEADS = 4
CONV = 4
EXPERTS, FF = 8, 2048
CAPACITY = int(TOK / EXPERTS * 1.25) + 1
FT = FF // P
FB = FF // 512
LEVELS = 7
TILES1 = (2 * TOK + EXPERTS * (P - 1)) // P


class Mark:

    def __init__(self, lane, n):
        self.lane, self.n, self.terms = lane, n, list(lane.terms)


class Lane:

    def __init__(self, nc, ctx, name, unit=1):
        self.sem = ctx.enter_context(nc.semaphore(name))
        self.name, self.unit, self.n, self.terms = name, unit, 0, []

    def did(self, instruction):
        instruction.then_inc(self.sem, self.unit)
        self.n += self.unit
        return Mark(self, self.n)

    def now(self, open_steps=0):
        return Mark(self, self.n - open_steps * self.unit)


def wait(engine, *marks):
    for m in marks:
        value = m.n
        for register, per_turn in m.terms:
            value = register * per_turn + value
        engine.wait_ge(m.lane.sem, value)


class Core:

    def __init__(self, nc, ctx):
        self.nc, self.ctx = nc, ctx
        self.pe, self.act, self.dve, self.pool, self.sp = nc.tensor, nc.scalar, nc.vector, nc.gpsimd, nc.sync
        self.engines = [self.pe, self.act, self.dve, self.pool, self.sp]
        self.mm = Lane(nc, ctx, "pe_steps")
        self.ac = Lane(nc, ctx, "act_steps")
        self.ve = Lane(nc, ctx, "dve_steps")
        self.go = Lane(nc, ctx, "pool_steps")
        self.in_ = [Lane(nc, ctx, f"load_{k}", 16) for k in range(8)]
        self.out = [Lane(nc, ctx, f"store_{k}", 16) for k in range(8)]
        self.used = Lane(nc, ctx, "pieces_used")
        self.bias = Lane(nc, ctx, "load_biases", 16)
        self.lanes = [self.mm, self.ac, self.ve, self.go, self.used, self.bias, *self.in_, *self.out]
        self.const = {}
        for lane in self.lanes:
            self.sp.sem_inc(lane.sem, 64)
            lane.n = 64
        self.bank = [ctx.enter_context(nc.psum_tensor(f"bank_{b}", [P, 512], F32)) for b in range(8)]

    @contextmanager
    def loop(self, turns, steps):
        before = [lane.n for lane in self.lanes]
        with self.nc.Fori(0, turns) as turn:
            for lane, n in steps.items():
                lane.terms.append((turn, n * lane.unit))
            yield turn
            for lane in steps:
                lane.terms.pop()
        for lane, n in zip(self.lanes, before):
            made = steps.get(lane, 0) * lane.unit
            assert lane.n - n == made, (lane.name, (lane.n - n) // lane.unit, steps.get(lane, 0))
            lane.n = n + turns * made

    def barrier(self):
        for engine in self.engines:
            wait(engine, *[lane.now() for lane in self.lanes])
        self.nc.all_engine_barrier()

    def sb(self, stack, name, shape, dtype=F32):
        return stack.enter_context(self.nc.sbuf_tensor(name, shape, dtype))


def load(c, lane, to, source):
    return lane.did(c.sp.dma_start(to, source))


def project_context(c, A, S):
    with ExitStack() as st:
        wk = c.sb(st, "wk", [P, 2, KD, D])
        wv = c.sb(st, "wv", [P, 2, KD, D])
        bk = c.sb(st, "bk", [P, 2, KD])
        bv = c.sb(st, "bv", [P, 2, D])
        cx = c.sb(st, "cx", [P, 2, KD, CHUNK])
        kparts = c.sb(st, "kparts", [P, 4, 2, CHUNK], F32R)
        vrow = c.sb(st, "vrow", [P, 2, HEADS, CHUNK // P, DH])
        for l in range(2):
            load(c, c.in_[2], wk[:, l], A["wk"][l])
            load(c, c.in_[2], wv[:, l], A["wv"][l])
            load(c, c.in_[2], bk[:, l], A["bk"][l])
            load(c, c.in_[2], bv[:, l], A["bv"][l].partition_broadcast(P))
        weights = c.in_[2].now()
        wait(c.pe, weights)
        wait(c.act, weights)
        wait(c.dve, weights)
        unit = 0
        per_chunk = 2 * 4 + 2 * 4
        steps = {c.mm: 2 * per_chunk, c.ac: 2 * 8, c.ve: 2 * per_chunk, c.in_[0]: 1, c.in_[1]: 1,
                 **{c.out[s]: 2 * 2 * 2 for s in range(4)}, c.out[4]: 2, c.out[5]: 2}
        with c.loop(NCHUNK // 2, steps) as turn:
            for u in range(2):
                wait(c.sp, c.mm.now(per_chunk))
                load(c, c.in_[u], cx[:, u], A["ctx"][bass.ds((turn * 2 + u) * P, P), :].rearrange("p (k n) -> p k n", k=KD))
                wait(c.pe, c.in_[u].now())
                for l in range(2):
                    for b in range(KD):
                        bank = c.bank[unit % 8]
                        wait(c.pe, c.ve.now(7))
                        for k in range(KD):
                            last = c.pe.matmul(bank[:], wk[:, l, k, b * P:(b + 1) * P], cx[:, u, k, :], start=k == 0, stop=k == KD - 1)
                        made = c.mm.did(last)
                        slot = b
                        wait(c.act, made, c.out[slot].now())
                        high = c.ac.did(c.act.activation(kparts[:, slot, 0, :], bank[:], ACT.Identity, bias=bk[:, l, b:b + 1]))
                        wait(c.dve, high)
                        low = c.ve.did(c.dve.scalar_tensor_tensor(kparts[:, slot, 1, :], bank[:], bk[:, l, b:b + 1], kparts[:, slot, 0, :].bitcast(F32), ALU.add, ALU.subtract))
                        wait(c.sp, low)
                        for part in range(2):
                            c.out[slot].did(c.sp.dma_start(S["k"][l, part, b * P:(b + 1) * P, bass.ds((turn * 2 + u) * CHUNK, CHUNK)], kparts[:, slot, part, :].bitcast(F32)))
                        unit += 1
                    wait(c.dve, c.out[4 + l].now())
                    for t in range(CHUNK // P):
                        bank = c.bank[unit % 8]
                        wait(c.pe, c.ve.now(7))
                        for k in range(KD):
                            last = c.pe.matmul(bank[:], cx[:, u, k, t * P:(t + 1) * P], wv[:, l, k, :], start=k == 0, stop=k == KD - 1)
                        made = c.mm.did(last)
                        wait(c.dve, made)
                        c.ve.did(c.dve.tensor_tensor(vrow[:, l, :, t, :], bank[:].rearrange("p (h d) -> p h d", h=HEADS), bv[:, l, :].rearrange("p (h d) -> p h d", h=HEADS), ALU.add))
                        unit += 1
                    wait(c.sp, c.ve.now())
                    c.out[4 + l].did(c.sp.dma_start(
                        S["v"][l].rearrange("h p t d -> p h (t d)")[:, :, bass.ds((turn * 2 + u) * (CHUNK // P) * DH, CHUNK // P * DH)],
                        vrow[:, l].rearrange("p h t d -> p h (t d)")))
        c.barrier()


def normalize(c, st, x, name):
    xn = c.sb(st, name + "_rows", [P, TT, D])
    xt = c.sb(st, name + "_cols", [P, KD, TOK])
    stats = c.sb(st, name + "_stats", [P, TT, 6])
    mv = c.sb(st, name + "_mv", [P, TT, 2])
    std = c.sb(st, name + "_std", [P, TT, 2])
    for t in range(TT):
        m = c.ve.did(c.dve.bn_stats(stats[:, t, :], x[:, t, :]))
    wait(c.dve, m)
    for t in range(TT):
        m = c.ve.did(c.dve.bn_aggr(mv[:, t, :], stats[:, t, :]))
    wait(c.dve, m)
    m = c.ve.did(c.dve.tensor_scalar(std[:, :, 0], mv[:, :, 1], EPS, None, ALU.add))
    wait(c.act, m)
    m = c.ac.did(c.act.activation(std[:, :, 1], std[:, :, 0], ACT.Sqrt))
    wait(c.dve, m)
    m = c.ve.did(c.dve.reciprocal(std[:, :, 0], std[:, :, 1]))
    wait(c.dve, m)
    for t in range(TT):
        m = c.ve.did(c.dve.tensor_scalar(xn[:, t, :], x[:, t, :], mv[:, t, 0:1], std[:, t, 0:1], ALU.subtract, ALU.mult))
    wait(c.pe, m)
    to_columns(c, xt, xn)
    return xn, xt


def to_columns(c, xt, xn):
    for k in range(KD):
        for t in range(TT):
            last = c.pe.transpose(c.bank[k][:, t * P:(t + 1) * P], xn[:, t, k * P:(k + 1) * P], c.ident[:])
        m = c.mm.did(last)
        wait(c.act, m)
        c.ac.did(c.act.copy(xt[:, k, :], c.bank[k][:]))


def linear_t(c, bank, w, xt, b, kd=KD):
    for k in range(kd):
        last = c.pe.matmul(bank, w[:, k, b * P:(b + 1) * P], xt[:, k, :], start=k == 0, stop=k == kd - 1)
    return c.mm.did(last)


def add_rows(c, x, at, w, bias=None, kd=KD):
    for t in range(TT):
        for k in range(kd):
            last = c.pe.matmul(c.bank[t][:], at[:, k, t * P:(t + 1) * P], w[:, k, :], start=k == 0, stop=k == kd - 1)
        m = c.mm.did(last)
        wait(c.dve, m)
        m = c.ve.did(c.dve.tensor_tensor(x[:, t, :], c.bank[t][:], x[:, t, :], ALU.add))
        if bias is not None:
            wait(c.dve, m)
            c.ve.did(c.dve.tensor_tensor(x[:, t, :], x[:, t, :], bias, ALU.add))


def cross_attention(c, A, S, x, l):
    with ExitStack() as st:
        with ExitStack() as st2:
            wq = c.sb(st2, f"wq{l}", [P, KD, D])
            bq = c.sb(st2, f"bq{l}", [P, KD])
            qf = c.sb(st2, f"qf{l}", [P, KD, TOK])
            qparts = c.sb(st2, f"qparts{l}", [P, KD, 2, TOK], F32R)
            load(c, c.in_[0], wq[:], A["wq"][l])
            w_in = load(c, c.in_[0], bq[:], A["bq"][l])
            xn, xt = normalize(c, st2, x, f"ln_a{l}")
            wait(c.pe, c.ac.now(), w_in)
            wait(c.dve, w_in)
            for b in range(KD):
                m = linear_t(c, c.bank[b][:], wq, xt, b)
                wait(c.dve, m)
                m = c.ve.did(c.dve.tensor_scalar(qf[:, b, :], c.bank[b][:], bq[:, b:b + 1], DH ** -0.5, ALU.add, ALU.mult))
                wait(c.dve, m)
                m = c.ve.did(c.dve.tensor_copy(qparts[:, b, 0, :], qf[:, b, :]))
                wait(c.dve, m)
                m = c.ve.did(c.dve.tensor_tensor(qparts[:, b, 1, :], qf[:, b, :], qparts[:, b, 0, :].bitcast(F32), ALU.subtract))
                wait(c.sp, m)
                for part in range(2):
                    c.out[7].did(c.sp.dma_start(S["q"][l, part, b * P:(b + 1) * P, :], qparts[:, b, part, :].bitcast(F32)))
            c.barrier()
        KROWS = 3 * DH + 1
        ks = [c.sb(st, f"ks{l}_{s}", [KROWS, KEYS], F32R) for s in range(2)]
        qs = [c.sb(st, f"qs{l}_{s}", [KROWS, TOK], F32R) for s in range(2)]
        vs = [c.sb(st, f"vs{l}_{s}", [P, KT, DH]) for s in range(2)]
        pt = c.sb(st, f"pt{l}", [P, 4, 2, TOK])
        run_max = c.sb(st, f"run_max{l}", [P, 2, TOK])
        col_max = c.sb(st, f"col_max{l}", [P, TT])
        partial = c.sb(st, f"partial{l}", [P, 2, TOK])
        head_out = c.sb(st, f"head_out{l}", [DH, 2, 2, TOK])
        for s in range(2):
            m = c.ve.did(c.dve.tensor_copy(ks[s][3 * DH:KROWS, :], c.ones[3 * DH:KROWS, 0:1].to_broadcast([1, KEYS])))

        def load_head(h, s):
            for at, part in ((0, 0), (1, 1), (2, 0)):
                c.in_[s].did(c.sp.dma_start(ks[s][at * DH:(at + 1) * DH, :].bitcast(F32), S["k"][l, part, bass.ds(h * DH, DH), :]))
            for at, part in ((0, 0), (1, 0), (2, 1)):
                c.in_[s].did(c.sp.dma_start(qs[s][at * DH:(at + 1) * DH, :].bitcast(F32), S["q"][l, part, bass.ds(h * DH, DH), :]))
            c.in_[s].did(c.sp.dma_start(vs[s][:], S["v"][l].rearrange("h p t d -> (h p) (t d)")[bass.ds(h * P, P), :].rearrange("p (t d) -> p t d", d=DH)))

        def first_pass(s, quad):
            for j in range(4):
                t = 4 * quad + j
                bank = c.bank[4 + t % 2]
                wait(c.pe, c.ve.now(1))
                m = c.mm.did(c.pe.matmul(bank[:], ks[s][0:3 * DH, t * P:(t + 1) * P], qs[s][0:3 * DH, :], start=True, stop=True))
                wait(c.dve, m, c.ve.now(1))
                other = run_max[:, t % 2, :] if t > 1 else bank[:]
                if t > 1:
                    c.ve.did(c.dve.tensor_tensor(run_max[:, t % 2, :], bank[:], run_max[:, t % 2, :], ALU.max))
                else:
                    c.ve.did(c.dve.tensor_copy(run_max[:, t % 2, :], bank[:]))

        def shift_row(s):
            wait(c.dve, c.ve.now())
            m = c.ve.did(c.dve.tensor_tensor(run_max[:, 0, :], run_max[:, 0, :], run_max[:, 1, :], ALU.max))
            wait(c.pe, m)
            for t in range(TT):
                last = c.pe.transpose(c.bank[4][:, t * P:(t + 1) * P], run_max[:, 0, t * P:(t + 1) * P], c.ident[:])
            m = c.mm.did(last)
            wait(c.dve, m)
            m = c.ve.did(c.dve.tensor_reduce(col_max[:], c.bank[4][:].rearrange("p (t n) -> p t n", t=TT), X, ALU.max))
            wait(c.pe, m)
            for t in range(TT):
                last = c.pe.matmul(c.bank[5][3 * DH:KROWS, t * P:(t + 1) * P], col_max[:, t:t + 1], c.ident[:], start=True, stop=True)
            m = c.mm.did(last)
            wait(c.dve, m)
            c.ve.did(c.dve.tensor_scalar(qs[s][3 * DH:KROWS, :], c.bank[5][3 * DH:KROWS, :], -1.0, None, ALU.mult))

        def second_pass(s, quad):
            for pair in range(2):
                g = 2 * quad + pair
                ring = g % 4
                wait(c.pe, c.ac.now(1))
                for j in range(2):
                    t = 2 * g + j
                    last = c.pe.matmul(c.bank[2 * (g % 2) + j][:], ks[s][:, t * P:(t + 1) * P], qs[s][:], start=True, stop=True)
                m = c.mm.did(last)
                wait(c.act, m)
                for j in range(2):
                    last = c.act.activation(pt[:, ring, j, :], c.bank[2 * (g % 2) + j][:], ACT.Exp)
                c.ac.did(last)

        def weigh(s, quad):
            for rhs_is_v, bank in ((True, c.bank[6]), (False, c.bank[7])):
                for j in range(4):
                    t = 4 * quad + j
                    lhs = vs[s][:, t, :] if rhs_is_v else c.ones[:, 0:DH]
                    last = c.pe.matmul(bank[j * DH:(j + 1) * DH, :], lhs, pt[:, (t // 2) % 4, t % 2, :], start=quad == 0, stop=quad == KT // 4 - 1)
            c.mm.did(last)

        def finish_head(h, s):
            wait(c.act, c.mm.now())
            m1 = c.ac.did(c.act.copy(partial[:, 0, :], c.bank[6][:]))
            m2 = c.ac.did(c.act.copy(partial[:, 1, :], c.bank[7][:]))
            wait(c.pe, m2, c.ve.now())
            c.pe.matmul(c.bank[4][0:DH, :], c.fold[:], partial[:, 0, :], start=True, stop=True)
            m = c.mm.did(c.pe.matmul(c.bank[5][0:DH, :], c.fold[:], partial[:, 1, :], start=True, stop=True))
            wait(c.dve, m, c.out[s].now())
            m = c.ve.did(c.dve.reciprocal(head_out[:, s, 1, :], c.bank[5][0:DH, :]))
            wait(c.dve, m)
            m = c.ve.did(c.dve.tensor_tensor(head_out[:, s, 0, :], c.bank[4][0:DH, :], head_out[:, s, 1, :], ALU.mult))
            wait(c.sp, m)
            c.out[s].did(c.sp.dma_start(S["heads"][bass.ds(h * DH, DH), :], head_out[:, s, 0, :]))

        def head(h, s, with_next, load_after):
            n = 1 - s
            if with_next:
                wait(c.pe, c.in_[n].now(), c.ve.now())
            quads = KT // 4
            for quad in range(quads):
                second_pass(s, quad)
                if with_next:
                    first_pass(n, quad)
                if quad:
                    wait(c.pe, c.ac.now(2))
                    weigh(s, quad - 1)
                    wait(c.act, c.mm.now())
            wait(c.pe, c.ac.now())
            weigh(s, quads - 1)
            if load_after is not None:
                wait(c.sp, c.mm.now())
                load_head(load_after, s)
            if with_next:
                shift_row(n)
            finish_head(h, s)

        load_head(0, 0)
        load_head(1, 1)
        wait(c.dve, c.in_[0].now())
        wait(c.pe, c.in_[0].now(), c.ve.now())
        for quad in range(KT // 4):
            first_pass(0, quad)
        shift_row(0)
        wait(c.pe, c.ve.now())
        pairs, quads = KT // 2, KT // 4
        mm_steps = pairs + KT + quads + 2 + 1
        steps = {c.mm: 2 * mm_steps, c.ac: 2 * (pairs + 2), c.ve: 2 * (KT + 3 + 2), c.in_[0]: 7, c.in_[1]: 7, c.out[0]: 1, c.out[1]: 1}
        with c.loop(HEADS // 2 - 1, steps) as turn:
            for u in range(2):
                head(turn * 2 + u, u, True, turn * 2 + u + 2)
        head(HEADS - 2, 0, True, None)
        head(HEADS - 1, 1, False, None)
        c.barrier()
    with ExitStack() as st:
        wo = c.sb(st, f"wo{l}", [P, KD, D])
        bo = c.sb(st, f"bo{l}", [P, D])
        at = c.sb(st, f"heads{l}", [P, KD, TOK])
        load(c, c.in_[0], wo[:], A["wo"][l])
        load(c, c.in_[0], bo[:], A["bo"][l].partition_broadcast(P))
        m = load(c, c.in_[0], at[:], S["heads"].rearrange("(k p) n -> p k n", p=P))
        wait(c.pe, m)
        wait(c.dve, m)
        add_rows(c, x, at, wo, bo[:])
        c.barrier()


def silu_conv(c, out, padded, taps, ntap, scratch):
    m = c.ve.did(c.dve.tensor_scalar(scratch, padded[:, 0:TOK], taps[:, 0:1], None, ALU.mult))
    for j in range(1, ntap):
        wait(c.dve, m)
        m = c.ve.did(c.dve.scalar_tensor_tensor(scratch, padded[:, j:j + TOK], taps[:, j:j + 1], scratch, ALU.mult, ALU.add))
    wait(c.act, m)
    return c.ac.did(c.act.activation(out, scratch, ACT.Silu))


def softplus(c, out, v, tmp):
    m = c.ve.did(c.dve.tensor_scalar(tmp, v, -1.0, None, ALU.mult))
    wait(c.dve, m)
    m = c.ve.did(c.dve.tensor_tensor(tmp, v, tmp, ALU.max))
    wait(c.act, m)
    m = c.ac.did(c.act.activation(tmp, tmp, ACT.Exp, scale=-1.0))
    wait(c.act, m)
    m = c.ac.did(c.act.activation(tmp, tmp, ACT.Ln, bias=1.0))
    wait(c.dve, m)
    return c.ve.did(c.dve.scalar_tensor_tensor(out, v, 0.0, tmp, ALU.max, ALU.add))


def selective_scan(c, A, x):
    CB = INNER // P
    with ExitStack() as st:
        w_in = c.sb(st, "w_in", [P, KD, D])
        w_out = c.sb(st, "w_out", [P, KD, D])
        w_x = c.sb(st, "w_x", [P, CB, DTRANK + 2 * DSTATE])
        w_dt = c.sb(st, "w_dt", [DTRANK, INNER])
        chan = c.sb(st, "chan", [P, KD, 3 + 2 + DSTATE])
        rate = c.sb(st, "rate", [P, CB, 2, DSTATE])
        padded = c.sb(st, "padded", [P, KD, TOK + 2])
        conv = c.sb(st, "conv", [P, KD, TOK])
        tmp = c.sb(st, "tmp", [P, 2, TOK])
        dt_raw = c.sb(st, "dt_raw", [DTRANK, TOK])
        bc = c.sb(st, "bc", [DSTATE, 2, TOK])
        delta = c.sb(st, "delta", [P, CB, TOK])
        cterm = c.sb(st, "cterm", [P, DSTATE, TOK])
        bterm = c.sb(st, "bterm", [P, DSTATE, TOK])
        decay = c.sb(st, "decay", [P, 2, TOK])
        drive = c.sb(st, "drive", [P, 2, TOK])
        state = c.sb(st, "state", [P, 2, TOK])
        y = c.sb(st, "y", [P, CB, TOK])
        for to, name in ((w_in, "w_in"), (w_out, "w_out"), (w_x, "w_xproj"), (w_dt, "w_dt"), (chan, "chan")):
            m = load(c, c.in_[0], to[:], A[name])
        ready = m
        wait(c.dve, ready)
        for b in range(KD):
            for edge in (0, TOK + 1):
                c.ve.did(c.dve.memset(padded[:, b, edge:edge + 1], 0.0))
        _, xt = normalize(c, st, x, "ln_s")
        wait(c.pe, ready, c.ac.now())
        for b in range(KD):
            m = linear_t(c, c.bank[b][:], w_in, xt, b)
            wait(c.dve, m)
            m = c.ve.did(c.dve.tensor_copy(padded[:, b, 1:TOK + 1], c.bank[b][:]))
            wait(c.dve, m)
            if b > 1:
                wait(c.dve, c.ac.now(1))
            silu_conv(c, conv[:, b, :], padded[:, b, :], chan[:, b, 0:3], 3, tmp[:, b % 2, :])
        wait(c.pe, c.ac.now())
        for bank, lo, n in ((4, 0, DTRANK), (5, DTRANK, DSTATE), (6, DTRANK + DSTATE, DSTATE)):
            for k in range(CB):
                last = c.pe.matmul(c.bank[bank][0:n, :], w_x[:, k, lo:lo + n], conv[:, k, :], start=k == 0, stop=k == CB - 1)
            m = c.mm.did(last)
        wait(c.act, m)
        m = c.ac.did(c.act.copy(dt_raw[:], c.bank[4][0:DTRANK, :]))
        c.ac.did(c.act.activation(bc[:, 0, :], c.bank[5][0:DSTATE, :], ACT.Tanh))
        c.ac.did(c.act.activation(bc[:, 1, :], c.bank[6][0:DSTATE, :], ACT.Tanh))
        wait(c.pe, m)
        for b in range(CB):
            m = c.mm.did(c.pe.matmul(c.bank[b][:], w_dt[:, b * P:(b + 1) * P], dt_raw[:], start=True, stop=True))
            wait(c.dve, m, c.ac.now())
            m = c.ve.did(c.dve.tensor_scalar(decay[:, b, :], c.bank[b][:], chan[:, b, 3:4], None, ALU.add))
            wait(c.dve, m)
            m = softplus(c, delta[:, b, :], decay[:, b, :], tmp[:, b, :])
            wait(c.dve, m)
            c.ve.did(c.dve.tensor_scalar(delta[:, b, :], delta[:, b, :], 1e-4, 1.0, ALU.max, ALU.min))
            m = softplus(c, rate[:, b, 0, :], chan[:, b, 5:5 + DSTATE], rate[:, b, 1, :])
            wait(c.dve, m)
            c.ve.did(c.dve.tensor_scalar(rate[:, b, 0, :], rate[:, b, 0, :], -1.0, -1e-4, ALU.mult, ALU.add))
        wait(c.pe, c.ac.now(), c.ve.now())
        for s in range(DSTATE):
            for which, to in ((0, bterm), (1, cterm)):
                bank = c.bank[(2 * s + which) % 4]
                wait(c.pe, c.ac.now(3))
                m = c.mm.did(c.pe.matmul(bank[:], c.pick[0:DSTATE, s * P:(s + 1) * P], bc[:, which, :], start=True, stop=True))
                wait(c.act, m)
                c.ac.did(c.act.copy(to[:, s, :], bank[:]))
        wait(c.act, c.ve.now())
        wait(c.dve, c.ac.now())
        for b in range(CB):
            c.ve.did(c.dve.tensor_scalar(y[:, b, :], conv[:, b, :], chan[:, b, 4:5], None, ALU.mult))
            for s in range(DSTATE):
                r = s % 2
                wait(c.act, c.ve.now())
                m = c.ac.did(c.act.activation(decay[:, r, :], delta[:, b, :], ACT.Exp, scale=rate[:, b, 0, s:s + 1]))
                wait(c.dve, m)
                m1 = c.ve.did(c.dve.tensor_tensor(drive[:, r, :], bterm[:, s, :], conv[:, b, :], ALU.mult))
                m = c.ve.did(c.dve.tensor_scalar(decay[:, r, :], decay[:, r, :], 1e-4, 1.0, ALU.max, ALU.min))
                wait(c.dve, m)
                m = c.ve.did(c.dve.tensor_scalar(tmp[:, r, :], decay[:, r, :], -1.0, 1.0, ALU.mult, ALU.add))
                wait(c.dve, m)
                m = c.ve.did(c.dve.tensor_tensor(drive[:, r, :], tmp[:, r, :], drive[:, r, :], ALU.mult))
                wait(c.dve, m)
                m = c.ve.did(c.dve.tensor_tensor_scan(state[:, r, :], decay[:, r, :], drive[:, r, :], 0.0, ALU.mult, ALU.add))
                wait(c.dve, m)
                m = c.ve.did(c.dve.tensor_tensor(tmp[:, r, :], state[:, r, :], cterm[:, s, :], ALU.mult))
                wait(c.dve, m)
                c.ve.did(c.dve.tensor_tensor(y[:, b, :], y[:, b, :], tmp[:, r, :], ALU.add))
        wait(c.dve, c.ve.now())
        for b in range(CB):
            m = c.ve.did(c.dve.tensor_copy(conv[:, b, :], y[:, b, :]))
        wait(c.pe, m)
        add_rows(c, x, conv, w_out)
        c.barrier()


def route(c, st, A, xt, l, wr, br):
    n = f"route{l}_"
    logits = c.sb(st, n + "logits", [P, TT, EXPERTS])
    best = c.sb(st, n + "best", [P, TT, 8])
    index = c.sb(st, n + "index", [P, TT, 8], U32)
    indexf = c.sb(st, n + "indexf", [P, TT, 8])
    hot = c.sb(st, n + "hot", [P, TT, 2, EXPERTS])
    for t in range(TT):
        for k in range(KD):
            last = c.pe.matmul(c.bank[4][:, t * EXPERTS:(t + 1) * EXPERTS], xt[:, k, t * P:(t + 1) * P], wr[:, k, :], start=k == 0, stop=k == KD - 1)
    m = c.mm.did(last)
    wait(c.dve, m)
    m = c.ve.did(c.dve.tensor_tensor(logits[:], c.bank[4][:, 0:TT * EXPERTS].rearrange("p (t e) -> p t e", t=TT), br, ALU.add))
    wait(c.dve, m)
    for t in range(TT):
        m = c.ve.did(c.dve.max(best[:, t, :], logits[:, t, :]))
    wait(c.dve, m)
    for t in range(TT):
        m = c.ve.did(c.dve.max_index(index[:, t, :], best[:, t, :], logits[:, t, :]))
    wait(c.dve, m)
    m = c.ve.did(c.dve.tensor_copy(indexf[:], index[:]))
    wait(c.dve, m)
    for t in range(TT):
        for j in range(2):
            m = c.ve.did(c.dve.tensor_scalar(hot[:, t, j, :], c.iota[:, 0:EXPERTS], indexf[:, t, j:j + 1], None, ALU.is_equal))
    wait(c.dve, m)
    return logits, best, hot


def ranks(c, st, l, chosen):
    rank = c.sb(st, f"rank{l}", [P, TT, EXPERTS])
    count = c.sb(st, f"count{l}", [P, EXPERTS])
    wait(c.pe, c.ve.now())
    for t in range(TT):
        for s in range(t + 1):
            last = c.pe.matmul(c.bank[5][:, t * EXPERTS:(t + 1) * EXPERTS], c.upto[:] if s == t else c.ones[:], chosen[:, s, :], start=s == 0, stop=s == t)
    for s in range(TT):
        last = c.pe.matmul(c.bank[6][:, 0:EXPERTS], c.ones[:], chosen[:, s, :], start=s == 0, stop=s == TT - 1)
    m = c.mm.did(last)
    wait(c.dve, m)
    c.ve.did(c.dve.tensor_copy(count[:], c.bank[6][:, 0:EXPERTS]))
    m = c.ve.did(c.dve.tensor_copy(rank[:], c.bank[5][:, 0:TT * EXPERTS].rearrange("p (t e) -> p t e", t=TT)))
    wait(c.dve, m)
    return rank, count


def expert_tiles(c, st, A, x, xn, pos, gate, l, tiles, expert_of):
    n = f"moe{l}_"
    two = l == 1
    pieces = (3 if two else 2) * FB
    ring = 6 if two else 8
    used = c.used
    piece = c.sb(st, n + "piece", [P, ring, KD, 512])
    sel = c.sb(st, n + "sel", [P, TT, P])
    selw = c.sb(st, n + "selw", [P, TT, P])
    sel2 = c.sb(st, n + "sel2", [P, TT, P])
    selwt = c.sb(st, n + "selwt", [P, TOK])
    slots = c.sb(st, n + "slots", [P, P])
    xg = c.sb(st, n + "xg", [P, KD, P])
    h = c.sb(st, n + "h", [P, FF])
    ht = c.sb(st, n + "ht", [P, FT, P])
    yrow = c.sb(st, n + "yrow", [P, D])
    if not two:
        bias1 = c.sb(st, n + "bias1", [P, FT])
        bias2 = c.sb(st, n + "bias2", [P, D])
    m = c.ve.did(c.dve.tensor_scalar(slots[:], c.iota[:], -float(P), None, ALU.add))
    ve_turn = 1 + TT * (5 if two else 2) + (FB if two else 0) + 1 + TT
    ac_turn = 2 + FB + (FB if two else FT)
    mm_turn = 2 + FB + (0 if two else 0) + 1
    steps = {c.ve: ve_turn, c.ac: ac_turn, c.mm: mm_turn, used: pieces}
    for r in range(ring):
        steps[c.in_[r]] = pieces // ring
    if not two:
        steps[c.bias] = 2
    with c.loop(tiles, steps) as turn:
        expert = expert_of(turn)
        if not two:
            wait(c.sp, c.ac.now(), c.ve.now())
            load(c, c.bias, bias1[:], A[n + "b1"][bass.ds(expert * P, P), :])
            load(c, c.bias, bias2[:], A[n + "b2"][bass.ds(expert * P, P), :])
            biases = c.bias.now()
        arrived = []
        for w in range(pieces):
            slot = w % ring
            wait(c.sp, used.now(ring - 1 - w))
            arrived.append(load(c, c.in_[slot], piece[:, slot], A[n + "w"][bass.ds((expert * pieces + w) * P, P), :].rearrange("p (k n) -> p k n", k=KD)))
        wait(c.dve, c.mm.now(), c.ve.now())
        m = c.ve.did(c.dve.tensor_scalar(slots[:], slots[:], float(P), None, ALU.add))
        wait(c.dve, m)
        for t in range(TT):
            c.ve.did(c.dve.tensor_scalar(sel[:, t, :], slots[:], pos[0][:, t:t + 1], None, ALU.is_equal))
            m = c.ve.did(c.dve.tensor_scalar(selw[:, t, :], slots[:], pos[0][:, t:t + 1], gate[0][:, t:t + 1], ALU.is_equal, ALU.mult))
            if two:
                wait(c.dve, m)
                c.ve.did(c.dve.scalar_tensor_tensor(sel[:, t, :], slots[:], pos[1][:, t:t + 1], sel[:, t, :], ALU.is_equal, ALU.add))
                m = c.ve.did(c.dve.tensor_scalar(sel2[:, t, :], slots[:], pos[1][:, t:t + 1], gate[1][:, t:t + 1], ALU.is_equal, ALU.mult))
                wait(c.dve, m)
                m = c.ve.did(c.dve.tensor_tensor(selw[:, t, :], selw[:, t, :], sel2[:, t, :], ALU.add))
        wait(c.pe, m, c.ac.now())
        for t in range(TT):
            last = c.pe.transpose(c.bank[4][:, t * P:(t + 1) * P], selw[:, t, :], c.ident[:])
        made = c.mm.did(last)
        for k in range(KD):
            for t in range(TT):
                last = c.pe.matmul(c.bank[5][:, k * P:(k + 1) * P], xn[:, t, k * P:(k + 1) * P], sel[:, t, :], start=t == 0, stop=t == TT - 1)
        gathered = c.mm.did(last)
        wait(c.act, gathered)
        m = c.ac.did(c.act.copy(xg[:], c.bank[5][:].rearrange("p (k n) -> p k n", k=KD)))
        wait(c.act, made)
        c.ac.did(c.act.copy(selwt[:], c.bank[4][:]))
        wait(c.pe, m)

        def hidden(fb):
            outs = []
            for which in range(2 if two else 1):
                w = fb * 2 + which if two else fb
                bank = c.bank[2 * (fb % 2) + which]
                wait(c.pe, arrived[w])
                for k in range(KD):
                    last = c.pe.matmul(bank[:], xg[:, k, :], piece[:, w % ring, k, :], start=k == 0, stop=k == KD - 1)
                outs.append(used.did(last))
            wait(c.act, outs[0])
            part = h[:, fb * 512:(fb + 1) * 512]
            if not two:
                return c.ac.did(c.act.copy(part, c.bank[2 * (fb % 2)][:]))
            m = c.ac.did(c.act.activation(part, c.bank[2 * (fb % 2)][:], ACT.Silu))
            wait(c.dve, m, outs[1])
            return c.ve.did(c.dve.tensor_tensor(part, part, c.bank[2 * (fb % 2) + 1][:], ALU.mult))

        def turn_hidden(fb, made):
            wait(c.pe, made)
            bank = c.bank[6 + fb % 2]
            wait(c.pe, c.ac.now(1) if two else c.ac.now(FT // FB + 1))
            for j in range(FT // FB):
                last = c.pe.transpose(bank[:, j * P:(j + 1) * P], h[:, (fb * (FT // FB) + j) * P:(fb * (FT // FB) + j + 1) * P], c.ident[:])
            m = c.mm.did(last)
            wait(c.act, m)
            if two:
                return c.ac.did(c.act.copy(ht[:, fb * 4:(fb + 1) * 4, :], bank[:].rearrange("p (j n) -> p j n", j=4)))
            if fb == 0:
                wait(c.act, biases)
            for j in range(FT // FB):
                f = fb * (FT // FB) + j
                m = c.ac.did(c.act.activation(ht[:, f, :], bank[:, j * P:(j + 1) * P], ACT.Gelu, bias=bias1[:, f:f + 1]))
            return m

        before = None
        for fb in range(FB):
            if fb >= 2:
                wait(c.pe, c.ve.now(1) if two else c.ac.now(0))
            made = hidden(fb)
            if fb:
                turned = turn_hidden(fb - 1, before)
            before = made
        turned = turn_hidden(FB - 1, before)
        wait(c.pe, turned)
        for db in range(FB):
            w = pieces - FB + db
            wait(c.pe, arrived[w])
            for j in range(4):
                f = db * 4 + j
                last = c.pe.matmul(c.bank[5][:], ht[:, f, :], piece[:, w % ring, j, :], start=f == 0, stop=f == FT - 1)
            m = used.did(last)
        wait(c.dve, m)
        if two:
            m = c.ve.did(c.dve.tensor_copy(yrow[:], c.bank[5][:]))
        else:
            wait(c.dve, biases)
            m = c.ve.did(c.dve.tensor_tensor(yrow[:], c.bank[5][:], bias2[:], ALU.add))
        wait(c.pe, m, c.ac.now())
        for t in range(TT):
            last = c.pe.matmul(c.bank[t][:], selwt[:, t * P:(t + 1) * P], yrow[:], start=True, stop=True)
        m = c.mm.did(last)
        wait(c.dve, m)
        for t in range(TT):
            m = c.ve.did(c.dve.tensor_tensor(x[:, t, :], c.bank[t][:], x[:, t, :], ALU.add))
        wait(c.pe, m)
    c.barrier()


def experts_top1(c, A, x):
    with ExitStack() as st:
        wr = c.sb(st, "wr0", [P, KD, EXPERTS])
        br = c.sb(st, "br0", [P, TT, EXPERTS])
        small = c.sb(st, "small0", [P, 6, TT])
        prod = c.sb(st, "prod0", [P, TT, EXPERTS])
        ready = load(c, c.in_[0], wr[:], A["moe0_router"])
        c.ve.did(c.dve.memset(br[:], 0.0))
        xn, xt = normalize(c, st, x, "ln_m0")
        wait(c.pe, ready, c.ac.now())
        logits, best, hot = route(c, st, A, xt, 0, wr, br[:])
        rank, _ = ranks(c, st, 0, hot[:, :, 0, :])
        for t in range(TT):
            m = c.ve.did(c.dve.tensor_scalar(prod[:, t, :], logits[:, t, :], best[:, t, 0:1], None, ALU.subtract))
        wait(c.act, m)
        m = c.ac.did(c.act.activation(prod[:], prod[:], ACT.Exp))
        wait(c.dve, m)
        total, weight, r, e, valid, slot = (small[:, k, :] for k in range(6))
        m = c.ve.did(c.dve.tensor_reduce(total, prod[:], X, ALU.add))
        wait(c.dve, m)
        c.ve.did(c.dve.reciprocal(weight, total))
        m = c.ve.did(c.dve.tensor_tensor(prod[:], hot[:, :, 0, :], rank[:], ALU.mult))
        wait(c.dve, m)
        m = c.ve.did(c.dve.tensor_reduce(r, prod[:], X, ALU.add))
        wait(c.dve, m)
        m = c.ve.did(c.dve.tensor_tensor(prod[:], hot[:, :, 0, :], c.iota[:, None, 0:EXPERTS].to_broadcast([P, TT, EXPERTS]), ALU.mult))
        wait(c.dve, m)
        m = c.ve.did(c.dve.tensor_reduce(e, prod[:], X, ALU.add))
        c.ve.did(c.dve.tensor_scalar(valid, r, float(CAPACITY), None, ALU.is_le))
        wait(c.dve, c.ve.now())
        m = c.ve.did(c.dve.scalar_tensor_tensor(slot, e, float(P), r, ALU.mult, ALU.add))
        wait(c.dve, m)
        m = c.ve.did(c.dve.tensor_tensor(slot, slot, valid, ALU.mult))
        wait(c.dve, m)
        m = c.ve.did(c.dve.tensor_scalar(slot, slot, -1.0, None, ALU.add))
        wait(c.dve, m)
        expert_tiles(c, st, A, x, xn, [slot], [weight], 0, EXPERTS, lambda turn: turn)


def experts_top2(c, A, x):
    with ExitStack() as st:
        wr = c.sb(st, "wr1", [P, KD, EXPERTS])
        br = c.sb(st, "br1", [P, TT, EXPERTS])
        small = c.sb(st, "small1", [P, 5, TT])
        prod = c.sb(st, "prod1", [P, TT, EXPERTS])
        chosen = c.sb(st, "chosen1", [P, TT, EXPERTS])
        tile_of = c.sb(st, "tile_of", [P, 4, EXPERTS])
        owner = c.sb(st, "owner", [1, TILES1, EXPERTS])
        ownerf = c.sb(st, "ownerf", [1, TILES1])
        owneri = c.sb(st, "owneri", [1, TILES1], I32)
        load(c, c.in_[0], wr[:], A["moe1_router"])
        for t in range(TT):
            ready = load(c, c.in_[0], br[:, t, :], A["moe1_router_b"].partition_broadcast(P))
        xn, xt = normalize(c, st, x, "ln_m1")
        wait(c.pe, ready, c.ac.now())
        wait(c.dve, ready)
        logits, best, hot = route(c, st, A, xt, 1, wr, br[:])
        m = c.ve.did(c.dve.tensor_tensor(chosen[:], hot[:, :, 0, :], hot[:, :, 1, :], ALU.add))
        rank, count = ranks(c, st, 1, chosen)
        d, w1, w2, slot1, slot2 = (small[:, k, :] for k in range(5))
        m = c.ve.did(c.dve.tensor_tensor(d, best[:, :, 1], best[:, :, 0], ALU.subtract))
        wait(c.act, m)
        m = c.ac.did(c.act.activation(d, d, ACT.Exp))
        wait(c.dve, m)
        m = c.ve.did(c.dve.tensor_scalar(w2, d, 1.0, None, ALU.add))
        wait(c.dve, m)
        m = c.ve.did(c.dve.reciprocal(w1, w2))
        wait(c.dve, m)
        c.ve.did(c.dve.tensor_tensor(w2, d, w1, ALU.mult))
        need, end, start, part = (tile_of[:, k, :] for k in range(4))
        m = c.ve.did(c.dve.tensor_scalar(need, count[:], 0.0, None, ALU.is_gt))
        for k in range(1, TT):
            wait(c.dve, m)
            m = c.ve.did(c.dve.scalar_tensor_tensor(need, count[:], float(k * P), need, ALU.is_gt, ALU.add))
        wait(c.dve, m)
        m = c.ve.did(c.dve.tensor_tensor_scan(end, c.ones[:, 0:EXPERTS], need, 0.0, ALU.mult, ALU.add))
        wait(c.dve, m)
        m = c.ve.did(c.dve.tensor_tensor(start, end, need, ALU.subtract))
        wait(c.dve, m)
        m = c.ve.did(c.dve.tensor_scalar(start, start, float(P), -1.0, ALU.mult, ALU.add))
        wait(c.dve, m)
        m = c.ve.did(c.dve.tensor_tensor(chosen[:], rank[:], start[:, None, :].to_broadcast([P, TT, EXPERTS]), ALU.add))
        wait(c.dve, m)
        for j, slot in ((0, slot1), (1, slot2)):
            m = c.ve.did(c.dve.tensor_tensor(prod[:], hot[:, :, j, :], chosen[:], ALU.mult))
            wait(c.dve, m)
            m = c.ve.did(c.dve.tensor_reduce(slot, prod[:], X, ALU.add))
            wait(c.dve, m)
        m = c.ve.did(c.dve.tensor_tensor(owner[:], end[0:1, None, :].to_broadcast([1, TILES1, EXPERTS]),
                                         c.iota[0:1, 0:TILES1, None].to_broadcast([1, TILES1, EXPERTS]), ALU.is_le))
        wait(c.dve, m)
        m = c.ve.did(c.dve.tensor_reduce(ownerf[:], owner[:], X, ALU.add))
        wait(c.dve, m)
        m = c.ve.did(c.dve.tensor_scalar(ownerf[:], ownerf[:], float(EXPERTS - 1), None, ALU.min))
        wait(c.dve, m)
        m = c.ve.did(c.dve.tensor_copy(owneri[:], ownerf[:]))
        wait(c.sp, m)
        expert_tiles(c, st, A, x, xn, [slot1, slot2], [w1, w2], 1, TILES1,
                     lambda turn: c.sp.value_load(owneri[0:1, bass.ds(turn, 1)], min_val=0, max_val=EXPERTS - 1))


def delta_rule(c, A, x):
    with ExitStack() as st:
        w = [c.sb(st, "dw_" + n, [P, KD, D]) for n in "qkvo"]
        wb = c.sb(st, "dw_b", [P, KD, DHEADS])
        taps = c.sb(st, "taps", [P, 3, KD, CONV])
        g_rms = c.sb(st, "g_rms", [P, 1])
        ln = c.sb(st, "ln_gb", [P, 2, D])
        padded = c.sb(st, "dpadded", [P, 2, TOK + CONV - 1])
        feat = [c.sb(st, "feat_" + n, [P, DHEADS, TOK]) for n in "qkv"]
        tmp = c.sb(st, "dtmp", [P, 4, TOK])
        beta = c.sb(st, "beta", [P, TT, DHEADS])
        for to, n in zip(w, "qkvo"):
            load(c, c.in_[0], to[:], A["d_w" + n])
        load(c, c.in_[0], wb[:], A["d_wb"])
        load(c, c.in_[0], taps[:], A["d_taps"])
        load(c, c.in_[0], g_rms[:], A["d_rms"])
        load(c, c.in_[0], ln[:, 0, :], A["d_lng"].partition_broadcast(P))
        ready = load(c, c.in_[0], ln[:, 1, :], A["d_lnb"].partition_broadcast(P))
        c.ve.did(c.dve.memset(padded[:, :, 0:CONV - 1], 0.0))
        xn, xt = normalize(c, st, x, "ln_d")
        wait(c.pe, ready, c.ac.now())
        wait(c.dve, ready)
        for i in range(3):
            for b in range(DHEADS):
                r = b % 2
                wait(c.pe, c.ve.now(2))
                m = linear_t(c, c.bank[r][:], w[i], xt, b)
                wait(c.dve, m)
                m = c.ve.did(c.dve.tensor_copy(padded[:, r, CONV - 1:], c.bank[r][:]))
                wait(c.dve, m, c.ac.now(1))
                silu_conv(c, feat[i][:, b, :], padded[:, r, :], taps[:, i, b, :], CONV, tmp[:, r, :])
        for t in range(TT):
            for k in range(KD):
                last = c.pe.matmul(c.bank[4][:, t * DHEADS:(t + 1) * DHEADS], xt[:, k, t * P:(t + 1) * P], wb[:, k, :], start=k == 0, stop=k == KD - 1)
        m = c.mm.did(last)
        wait(c.act, m)
        c.ac.did(c.act.activation(beta[:], c.bank[4][:, 0:TT * DHEADS].rearrange("p (t h) -> p t h", t=TT), ACT.Sigmoid))
        wait(c.dve, c.ac.now())
        for i in range(2):
            for b in range(DHEADS):
                r = b % 4
                wait(c.dve, c.mm.now())
                m = c.ve.did(c.dve.tensor_tensor(tmp[:, r, :], feat[i][:, b, :], feat[i][:, b, :], ALU.mult))
                wait(c.pe, m)
                m = c.mm.did(c.pe.matmul(c.bank[r][:], c.ones[:], tmp[:, r, :], start=True, stop=True))
                wait(c.dve, m)
                m = c.ve.did(c.dve.tensor_scalar(tmp[:, r, :], c.bank[r][:], 1e-6, None, ALU.add))
                wait(c.act, m)
                m = c.ac.did(c.act.activation(tmp[:, r, :], tmp[:, r, :], ACT.Sqrt))
                wait(c.dve, m)
                m = c.ve.did(c.dve.reciprocal(tmp[:, r, :], tmp[:, r, :]))
                wait(c.dve, m)
                c.ve.did(c.dve.tensor_tensor(feat[i][:, b, :], feat[i][:, b, :], tmp[:, r, :], ALU.mult))
        c.barrier()
        q, k, v = feat
        per = lambda n: c.sb(st, n, [P, TT, DHEADS, P])
        below, below_t, inv, inv_t, qk, vrow, krow = (per("d_" + n) for n in ("below", "below_t", "inv", "inv_t", "qk", "vrow", "krow"))
        lev = c.sb(st, "d_lev", [P, 2, DHEADS, P])
        prod = c.sb(st, "d_prod", [P, 2, DHEADS, P])
        flat = lambda a: a.rearrange("p h n -> p (h n)")
        over_heads = lambda mask: mask[:, None, :].to_broadcast([P, DHEADS, P])
        heads_of = lambda bank: bank[:].rearrange("p (h n) -> p h n", h=DHEADS)

        def four(bank, lhs, rhs):
            for h in range(DHEADS):
                last = c.pe.matmul(bank[:, h * P:(h + 1) * P], lhs(h), rhs(h), start=True, stop=True)
            return c.mm.did(last)

        def four_transposes(bank, of):
            for h in range(DHEADS):
                last = c.pe.transpose(bank[:, h * P:(h + 1) * P], of(h), c.ident[:])
            return c.mm.did(last)

        for t in range(TT):
            at = slice(t * P, (t + 1) * P)
            wait(c.pe, c.ve.now(), c.ac.now())
            m = four(c.bank[0], lambda h: k[:, h, at], lambda h: k[:, h, at])
            wait(c.dve, m)
            for h in range(DHEADS):
                m = c.ve.did(c.dve.scalar_tensor_tensor(below[:, t, h, :], c.bank[0][:, h * P:(h + 1) * P], beta[:, t, h:h + 1], c.lower[:], ALU.mult, ALU.mult))
            m2 = four(c.bank[1], lambda h: k[:, h, at], lambda h: q[:, h, at])
            wait(c.dve, m2)
            c.ve.did(c.dve.tensor_tensor(qk[:, t], heads_of(c.bank[1]), over_heads(c.upto), ALU.mult))
            m2 = four_transposes(c.bank[2], lambda h: v[:, h, at])
            wait(c.act, m2)
            c.ac.did(c.act.copy(flat(vrow[:, t]), c.bank[2][:]))
            m2 = four_transposes(c.bank[3], lambda h: k[:, h, at])
            wait(c.act, m2)
            c.ac.did(c.act.copy(flat(krow[:, t]), c.bank[3][:]))
            wait(c.pe, m)
            m2 = four_transposes(c.bank[4], lambda h: below[:, t, h, :])
            wait(c.dve, m2)
            m = c.ve.did(c.dve.tensor_copy(flat(below_t[:, t]), c.bank[4][:]))
            wait(c.dve, m)
            c.ve.did(c.dve.tensor_tensor(inv[:, t], below[:, t], over_heads(c.level0), ALU.mult))
            c.ve.did(c.dve.tensor_tensor(inv_t[:, t], below_t[:, t], over_heads(c.level_t[0]), ALU.mult))
            wait(c.dve, c.ve.now())
            c.ve.did(c.dve.tensor_tensor(inv[:, t], over_heads(c.ident), inv[:, t], ALU.subtract))
            c.ve.did(c.dve.tensor_tensor(inv_t[:, t], over_heads(c.ident), inv_t[:, t], ALU.subtract))
        for level in range(1, LEVELS):
            for t in range(TT):
                r = t % 2
                wait(c.dve, c.mm.now(), c.ve.now())
                m = c.ve.did(c.dve.tensor_tensor(lev[:, r], below_t[:, t], over_heads(c.level_t[level]), ALU.mult))
                wait(c.pe, m)
                m = four(c.bank[4 * r], lambda h: lev[:, r, h, :], lambda h: inv[:, t, h, :])
                wait(c.act, m)
                m = c.ac.did(c.act.copy(flat(prod[:, r]), c.bank[4 * r][:]))
                wait(c.pe, m)
                m = four(c.bank[4 * r + 1], lambda h: inv_t[:, t, h, :], lambda h: prod[:, r, h, :])
                m2 = four(c.bank[4 * r + 2], lambda h: prod[:, r, h, :], lambda h: inv_t[:, t, h, :])
                wait(c.dve, m2)
                c.ve.did(c.dve.tensor_tensor(inv[:, t], inv[:, t], heads_of(c.bank[4 * r + 1]), ALU.subtract))
                c.ve.did(c.dve.tensor_tensor(inv_t[:, t], inv_t[:, t], heads_of(c.bank[4 * r + 2]), ALU.subtract))
        c.barrier()
        S = c.sb(st, "d_state", [P, DHEADS, P])
        rhs = c.sb(st, "d_rhs", [P, DHEADS, P])
        u = c.sb(st, "d_u", [P, DHEADS, P])
        o = c.sb(st, "d_o", [P, TT, DHEADS, P])
        osq = c.sb(st, "d_osq", [P, TT, DHEADS, P])
        rms = c.sb(st, "d_rms_of", [P, 2, TT, DHEADS])
        m = c.ve.did(c.dve.memset(flat(S[:]), 0.0))
        wait(c.dve, m)
        for t in range(TT):
            at = slice(t * P, (t + 1) * P)
            wait(c.pe, c.ve.now())
            m = four(c.bank[0], lambda h: k[:, h, at], lambda h: S[:, h, :])
            wait(c.dve, m)
            m = c.ve.did(c.dve.tensor_tensor(rhs[:], vrow[:, t], heads_of(c.bank[0]), ALU.subtract))
            wait(c.dve, m)
            m = c.ve.did(c.dve.tensor_tensor(rhs[:], rhs[:], beta[:, t, :, None].to_broadcast([P, DHEADS, P]), ALU.mult))
            wait(c.pe, m)
            m = four(c.bank[1], lambda h: inv_t[:, t, h, :], lambda h: rhs[:, h, :])
            wait(c.dve, m)
            m = c.ve.did(c.dve.tensor_copy(flat(u[:]), c.bank[1][:]))
            wait(c.pe, m)
            for h in range(DHEADS):
                c.pe.matmul(c.bank[2][:, h * P:(h + 1) * P], q[:, h, at], S[:, h, :], start=True, stop=False)
                last = c.pe.matmul(c.bank[2][:, h * P:(h + 1) * P], qk[:, t, h, :], u[:, h, :], start=False, stop=True)
            mo = c.mm.did(last)
            ms = four(c.bank[3], lambda h: krow[:, t, h, :], lambda h: u[:, h, :])
            wait(c.dve, ms)
            c.ve.did(c.dve.tensor_tensor(S[:], S[:], heads_of(c.bank[3]), ALU.add))
            c.ve.did(c.dve.tensor_copy(flat(o[:, t]), c.bank[2][:]))
        wait(c.dve, c.ve.now())
        c.ve.did(c.dve.tensor_tensor(osq[:], o[:], o[:], ALU.mult))
        wait(c.dve, c.ve.now())
        c.ve.did(c.dve.tensor_reduce(rms[:, 0], osq[:], X, ALU.add))
        wait(c.dve, c.ve.now())
        m = c.ve.did(c.dve.tensor_scalar(rms[:, 0], rms[:, 0], 1.0 / P, EPS, ALU.mult, ALU.add))
        wait(c.act, m)
        m = c.ac.did(c.act.activation(rms[:, 1], rms[:, 0], ACT.Sqrt))
        wait(c.dve, m)
        m = c.ve.did(c.dve.reciprocal(rms[:, 0], rms[:, 1]))
        wait(c.dve, m)
        m = c.ve.did(c.dve.tensor_tensor(osq[:], o[:], rms[:, 0, :, :, None].to_broadcast([P, TT, DHEADS, P]), ALU.mult))
        wait(c.pe, m)
        for h in range(DHEADS):
            for t in range(TT):
                last = c.pe.transpose(c.bank[4 + h][:, t * P:(t + 1) * P], osq[:, t, h, :], c.ident[:])
            m = c.mm.did(last)
            wait(c.act, m)
            c.ac.did(c.act.activation(xt[:, h, :], c.bank[4 + h][:], ACT.Identity, scale=g_rms[:, 0:1]))
        wait(c.pe, c.ac.now())
        add_rows(c, xn, xt, w[3])
        wait(c.dve, c.ve.now())
        stats = c.sb(st, "y_stats", [P, TT, 6])
        mv = c.sb(st, "y_mv", [P, TT, 2])
        std = c.sb(st, "y_std", [P, TT, 2])
        for t in range(TT):
            c.ve.did(c.dve.bn_stats(stats[:, t, :], xn[:, t, :]))
        wait(c.dve, c.ve.now())
        for t in range(TT):
            c.ve.did(c.dve.bn_aggr(mv[:, t, :], stats[:, t, :]))
        wait(c.dve, c.ve.now())
        m = c.ve.did(c.dve.tensor_scalar(std[:, :, 0], mv[:, :, 1], EPS, None, ALU.add))
        wait(c.act, m)
        m = c.ac.did(c.act.activation(std[:, :, 1], std[:, :, 0], ACT.Sqrt))
        wait(c.dve, m)
        m = c.ve.did(c.dve.reciprocal(std[:, :, 0], std[:, :, 1]))
        wait(c.dve, m)
        for t in range(TT):
            c.ve.did(c.dve.tensor_scalar(xn[:, t, :], xn[:, t, :], mv[:, t, 0:1], std[:, t, 0:1], ALU.subtract, ALU.mult))
        for which, op in ((0, ALU.mult), (1, ALU.add)):
            wait(c.dve, c.ve.now())
            c.ve.did(c.dve.tensor_tensor(xn[:], xn[:], ln[:, which, None, :].to_broadcast([P, TT, D]), op))
        wait(c.dve, c.ve.now())
        c.ve.did(c.dve.tensor_tensor(x[:], x[:], xn[:], ALU.add))
        c.barrier()


def perceiver(nc, A, out, stages=range(1, 8)):
    with ExitStack() as ctx:
        c = Core(nc, ctx)
        scratch = {
            "k": nc.dram_tensor("k_parts", [2, 2, D, KEYS], F32, kind="Internal").ap(),
            "v": nc.dram_tensor("v_heads", [2, HEADS, P, KT, DH], F32, kind="Internal").ap(),
            "q": nc.dram_tensor("q_parts", [2, 2, D, TOK], F32, kind="Internal").ap(),
            "heads": nc.dram_tensor("head_outputs", [D, TOK], F32, kind="Internal").ap(),
        }
        x = c.sb(ctx, "x_rows", [P, TT, D])
        const = c.sb(ctx, "constants", [P, CONST_COLS])
        for name, (lo, hi) in CONST_AT.items():
            c.const[name] = const[:, lo:hi]
        c.ident, c.ones, c.iota, c.upto, c.lower, c.level0, c.fold, c.pick = (
            c.const[n] for n in ("ident", "ones", "iota", "upto", "lower", "level0", "fold", "pick"))
        c.level_t = [c.const["level_t"][:, k * P:(k + 1) * P] for k in range(LEVELS)]
        load(c, c.in_[0], const[:], A["constants"])
        load(c, c.in_[0], x[:], A["x"].rearrange("(t p) d -> p t d", p=P))
        c.barrier()
        if 1 in stages:
            project_context(c, A, scratch)
        if 2 in stages:
            cross_attention(c, A, scratch, x, 0)
        if 3 in stages:
            selective_scan(c, A, x)
        if 4 in stages:
            experts_top1(c, A, x)
        if 5 in stages:
            cross_attention(c, A, scratch, x, 1)
        if 6 in stages:
            delta_rule(c, A, x)
        if 7 in stages:
            experts_top2(c, A, x)
        c.out[0].did(nc.sync.dma_start(out.rearrange("(t p) d -> p t d", p=P), x[:]))
        wait(nc.sync, c.out[0].now())


CONST_AT, CONST_COLS = {}, 0
for _name, _cols in (("ident", P), ("ones", P), ("iota", P), ("upto", P), ("lower", P), ("level0", P),
                     ("level_t", LEVELS * P), ("fold", DH), ("pick", DSTATE * P)):
    CONST_AT[_name] = (CONST_COLS, CONST_COLS + _cols)
    CONST_COLS += _cols



def constants(np):
    i, j = np.arange(P)[:, None], np.arange(P)[None, :]
    level = [(i // (2 << n) == j // (2 << n)) & ((i >> n) % 2 == 1) & ((j >> n) % 2 == 0) for n in range(LEVELS)]
    parts = {
        "ident": i == j, "ones": i + j >= 0, "iota": j + 0 * i, "upto": i <= j, "lower": i > j, "level0": level[0],
        "level_t": np.concatenate([m.T for m in level], 1),
        "fold": i % DH == j[:, :DH],
        "pick": np.concatenate([(i == s) & (j >= 0) for s in range(DSTATE)], 1),
    }
    return np.concatenate([parts[n].astype(np.float32) for n in CONST_AT], 1)


def arrange(np, x, ctx_1024, **w):
    def rows(a, k=None):
        return a.reshape(-1, P, a.shape[-1]).transpose(1, 0, 2)

    def column(a):
        return a.reshape(-1, P).T

    ipw, ipb = w["L1_xattn_in_proj_weight"], w["L1_xattn_in_proj_bias"]
    g, u, dn = w["L1_ffn_gate_w"], w["L1_ffn_up_w"], w["L1_ffn_down_w"]

    def in_pieces(a):
        return a.reshape(EXPERTS, KD, P, FB, 512).transpose(0, 3, 2, 1, 4).reshape(EXPERTS, FB, P, KD * 512)

    def out_pieces(a):
        return a.reshape(EXPERTS, FB, 4, P, D).transpose(0, 1, 3, 2, 4).reshape(EXPERTS, FB, P, 4 * D)

    gu = np.stack([in_pieces(g.transpose(0, 2, 1)), in_pieces(u.transpose(0, 2, 1))], 2).reshape(EXPERTS, 2 * FB, P, KD * 512)
    A = {
        "constants": constants(np),
        "x": x.reshape(TOK, D),
        "ctx": ctx_1024.reshape(NCHUNK, CHUNK, KD, P).transpose(0, 3, 2, 1).reshape(NCHUNK * P, KD * CHUNK),
        "wq": np.stack([rows(w["L0_xattn_W_Q"]), rows(ipw[0:D].T)]),
        "wk": np.stack([rows(w["L0_xattn_W_K"]), rows(ipw[D:2 * D].T)]),
        "wv": np.stack([rows(w["L0_xattn_W_V"]), rows(ipw[2 * D:].T)]),
        "wo": np.stack([rows(w["L0_xattn_W_O"]), rows(w["L1_xattn_out_w"].T)]),
        "bq": np.stack([column(w["L0_xattn_b_Q"]), column(ipb[0:D])]),
        "bk": np.stack([column(w["L0_xattn_b_K"]), column(ipb[D:2 * D])]),
        "bv": np.stack([w["L0_xattn_b_V"], ipb[2 * D:]]),
        "bo": np.stack([w["L0_xattn_b_O"], w["L1_xattn_out_b"]]),
        "w_in": rows(w["L0_attn_W_in"].T),
        "w_out": rows(w["L0_attn_W_out"].T),
        "w_xproj": rows(w["L0_attn_W_xproj"].T),
        "w_dt": w["L0_attn_W_dt"].T,
        "chan": np.concatenate([
            rows(np.concatenate([w["L0_attn_Kx"], w["L0_attn_Kz"]]).reshape(D, 3)),
            rows(np.concatenate([w["L0_attn_b_dt"]] * 2).reshape(D, 1)),
            rows(np.concatenate([w["L0_attn_D"]] * 2).reshape(D, 1)),
            rows(np.concatenate([w["L0_attn_A_log"]] * 2))], 2),
        "moe0_router": rows(w["L0_ffn_wg"]),
        "moe0_w": np.concatenate([in_pieces(w["L0_ffn_W1"]), out_pieces(w["L0_ffn_W2"])], 1).reshape(-1, KD * 512),
        "moe0_b1": w["L0_ffn_b1"].reshape(EXPERTS, FT, P).transpose(0, 2, 1).reshape(EXPERTS * P, FT),
        "moe0_b2": np.repeat(w["L0_ffn_b2"], P, axis=0),
        "d_wq": rows(w["L1_attn_Wq"]), "d_wk": rows(w["L1_attn_Wk"]), "d_wv": rows(w["L1_attn_Wv"]),
        "d_wo": rows(w["L1_attn_Wo"]), "d_wb": rows(w["L1_attn_Wb"]),
        "d_taps": np.stack([rows(w["L1_attn_conv_" + n].T) for n in "qkv"], 1),
        "d_rms": w["L1_attn_g_rms"].reshape(P, 1),
        "d_lng": w["L1_attn_ln_g"], "d_lnb": w["L1_attn_ln_b"],
        "moe1_router": rows(w["L1_ffn_router_w"].T),
        "moe1_router_b": w["L1_ffn_router_b"],
        "moe1_w": np.concatenate([gu, out_pieces(dn.transpose(0, 2, 1))], 1).reshape(-1, KD * 512),
    }
    return {name: np.ascontiguousarray(a) for name, a in A.items()}


def kernel(**inputs):
    import numpy as np
    import concourse.bacc as bacc
    from concourse.bass_utils import run_bass_kernel_spmd

    arrays = arrange(np, **{k: np.asarray(v) for k, v in inputs.items()})
    nc = bacc.Bacc("TRN2", target_bir_lowering=False, num_devices=1)
    aps = {name: nc.dram_tensor("in_" + name, a.shape, mybir.dt.from_np(a.dtype), kind="ExternalInput").ap() for name, a in arrays.items()}
    out = nc.dram_tensor("out", (TOK, D), F32, kind="ExternalOutput").ap()
    perceiver(nc, aps, out)
    result = run_bass_kernel_spmd(nc, [{"in_" + name: a for name, a in arrays.items()}], core_ids=[0])
    return result.results[0]["out"].reshape(1, TOK, D)
```

```python
from contextlib import ExitStack, contextmanager

import concourse.bass as bass
from concourse import mybir

F32 = mybir.dt.float32
F32R = mybir.dt.float32r
I32 = mybir.dt.int32
U32 = mybir.dt.uint32
ALU = mybir.AluOpType
ACT = mybir.ActivationFunctionType
X = mybir.AxisListType.X

P = 128
TOK, D = 512, 512
TT, KD = TOK // P, D // P
KEYS = 8192
CHUNK = 512
NCHUNK = KEYS // CHUNK
KT = KEYS // P
HEADS, DH = 16, 32
EPS = 1e-5
INNER, DSTATE, DTRANK = 256, 8, 32
DHEADS = 4
CONV = 4
EXPERTS, FF = 8, 2048
CAPACITY = int(TOK / EXPERTS * 1.25) + 1
FT = FF // P
FB = FF // 512
LEVELS = 7
TILES1 = (2 * TOK + EXPERTS * (P - 1)) // P


class Mark:

    def __init__(self, lane, n):
        self.lane, self.n, self.terms = lane, n, list(lane.terms)


class Lane:

    def __init__(self, nc, ctx, name, unit=1):
        self.sem = ctx.enter_context(nc.semaphore(name))
        self.name, self.unit, self.n, self.terms = name, unit, 0, []

    def did(self, instruction):
        instruction.then_inc(self.sem, self.unit)
        self.n += self.unit
        return Mark(self, self.n)

    def now(self, open_steps=0):
        return Mark(self, self.n - open_steps * self.unit)


def wait(engine, *marks):
    for m in marks:
        value = m.n
        for register, per_turn in m.terms:
            value = register * per_turn + value
        engine.wait_ge(m.lane.sem, value)


class Core:

    def __init__(self, nc, ctx):
        self.nc, self.ctx = nc, ctx
        self.pe, self.act, self.dve, self.pool, self.sp = nc.tensor, nc.scalar, nc.vector, nc.gpsimd, nc.sync
        self.engines = [self.pe, self.act, self.dve, self.pool, self.sp]
        self.mm = Lane(nc, ctx, "pe_steps")
        self.ac = Lane(nc, ctx, "act_steps")
        self.ve = Lane(nc, ctx, "dve_steps")
        self.go = Lane(nc, ctx, "pool_steps")
        self.in_ = [Lane(nc, ctx, f"load_{k}", 16) for k in range(8)]
        self.q_in = [Lane(nc, ctx, f"load_q_{k}", 16) for k in range(2)]
        self.v_in = [Lane(nc, ctx, f"load_v_{k}", 16) for k in range(2)]
        self.out = [Lane(nc, ctx, f"store_{k}", 16) for k in range(8)]
        self.used = Lane(nc, ctx, "pieces_used")
        self.cut = Lane(nc, ctx, "pieces_split")
        self.bias = Lane(nc, ctx, "load_biases", 16)
        self.lanes = [self.mm, self.ac, self.ve, self.go, self.used, self.cut, self.bias, *self.q_in, *self.v_in, *self.in_, *self.out]
        self.const = {}
        for lane in self.lanes:
            self.sp.sem_inc(lane.sem, 64)
            lane.n = 64
        self.psum = ctx.enter_context(nc.psum_tensor("psum", [P, 8, 512], F32))
        self.bank = [self.psum[:, b, :] for b in range(8)]

    @contextmanager
    def loop(self, turns, steps):
        before = [lane.n for lane in self.lanes]
        with self.nc.Fori(0, turns) as turn:
            for lane, n in steps.items():
                lane.terms.append((turn, n * lane.unit))
            yield turn
            for lane in steps:
                lane.terms.pop()
        for lane, n in zip(self.lanes, before):
            made = steps.get(lane, 0) * lane.unit
            assert lane.n - n == made, (lane.name, (lane.n - n) // lane.unit, steps.get(lane, 0))
            lane.n = n + turns * made

    def barrier(self):
        for engine in self.engines:
            wait(engine, *[lane.now() for lane in self.lanes])
        self.nc.all_engine_barrier()

    def sb(self, stack, name, shape, dtype=F32):
        return stack.enter_context(self.nc.sbuf_tensor(name, shape, dtype))


def load(c, lane, to, source):
    return lane.did(c.sp.dma_start(to, source))


def split(c, high, low, source):
    m = c.ac.did(c.act.copy(high, source))
    wait(c.dve, m)
    return c.ve.did(c.dve.tensor_tensor(low, source, high.bitcast(F32), ALU.subtract))


def product(c, out, lhs, rhs, start, stop):
    c.pe.matmul(out, lhs[0], rhs[0], start=start, stop=False)
    c.pe.matmul(out, lhs[0], rhs[1], start=False, stop=False)
    return c.pe.matmul(out, lhs[1], rhs[0], start=False, stop=stop)


def project_context(c, A, S):
    with ExitStack() as st:
        raw = c.sb(st, "w_raw", [P, 2, KD, D])
        w = {n: [c.sb(st, f"w{n}_{part}", [P, 2, KD, D], F32R) for part in ("high", "low")] for n in "kv"}
        bk = c.sb(st, "bk", [P, 2, KD])
        bv = c.sb(st, "bv", [P, 2, D])
        cx = c.sb(st, "cx", [P, KD, CHUNK])
        cparts = c.sb(st, "cparts", [P, 2, 2, KD, CHUNK], F32R)
        kparts = c.sb(st, "kparts", [P, 4, 2, CHUNK], F32R)
        vrow = c.sb(st, "vrow", [P, 2, HEADS, CHUNK // P, DH])
        for l in range(2):
            load(c, c.in_[2], bk[:, l], A["bk"][l])
            load(c, c.in_[2], bv[:, l], A["bv"][l].partition_broadcast(P))
        for n, slot in (("k", 0), ("k", 1), ("v", 0), ("v", 1)):
            wait(c.sp, c.ve.now(1))
            m = load(c, c.in_[slot], raw[:, slot], A["w" + n][slot])
            wait(c.act, m)
            wait(c.dve, m)
            split(c, w[n][0][:, slot], w[n][1][:, slot], raw[:, slot])
        wait(c.pe, c.ve.now())
        wait(c.act, c.in_[2].now())
        wait(c.dve, c.in_[2].now())
        per_chunk = 2 * 4 + 2 * 4

        def load_chunk(n, u):
            wait(c.sp, c.go.now())
            load(c, c.in_[4 + u], cx[:], A["ctx"][bass.ds(n * P, P), :].rearrange("p (k n) -> p k n", k=KD))

        def chunk(n, u, has_next=True):
            wait(c.act, c.in_[4 + u].now(), c.mm.now(per_chunk))
            m = c.ac.did(c.act.copy(cparts[:, u, 0], cx[:]))
            wait(c.pool, m)
            m = c.go.did(c.pool.tensor_tensor(cparts[:, u, 1], cx[:], cparts[:, u, 0].bitcast(F32), ALU.subtract))
            wait(c.pe, m)
            for l in range(2):
                for b in range(KD):
                    bank = c.bank[b]
                    wait(c.pe, c.ve.now(7))
                    for k in range(KD):
                        last = product(c, bank, [x[:, l, k, b * P:(b + 1) * P] for x in w["k"]], [cparts[:, u, x, k, :] for x in range(2)], k == 0, k == KD - 1)
                    made = c.mm.did(last)
                    wait(c.act, made, c.out[b].now())
                    high = c.ac.did(c.act.activation(kparts[:, b, 0, :], bank, ACT.Identity, bias=bk[:, l, b:b + 1]))
                    wait(c.dve, high)
                    low = c.ve.did(c.dve.scalar_tensor_tensor(kparts[:, b, 1, :], bank, bk[:, l, b:b + 1], kparts[:, b, 0, :].bitcast(F32), ALU.add, ALU.subtract))
                    wait(c.act, low)
                    for part in range(2):
                        c.out[b].did(c.act.dma_start(S["k"][l, part, b * P:(b + 1) * P, bass.ds(n * CHUNK, CHUNK)], kparts[:, b, part, :].bitcast(F32)))
                if l == 1 and has_next:
                    load_chunk(n + 1, 1 - u)
                wait(c.dve, c.out[4 + l].now())
                for t in range(CHUNK // P):
                    bank = c.bank[4 + t]
                    wait(c.pe, c.ve.now(7))
                    for k in range(KD):
                        last = product(c, bank, [cparts[:, u, x, k, t * P:(t + 1) * P] for x in range(2)], [x[:, l, k, :] for x in w["v"]], k == 0, k == KD - 1)
                    made = c.mm.did(last)
                    wait(c.dve, made)
                    c.ve.did(c.dve.tensor_tensor(vrow[:, l, :, t, :], bank.rearrange("p (h d) -> p h d", h=HEADS), bv[:, l, :].rearrange("p (h d) -> p h d", h=HEADS), ALU.add))
                wait(c.sp, c.ve.now())
                c.out[4 + l].did(c.sp.dma_start(
                    S["v"][l].rearrange("h p t d -> p h (t d)")[:, :, bass.ds(n * (CHUNK // P) * DH, CHUNK // P * DH)],
                    vrow[:, l].rearrange("p h t d -> p h (t d)")))

        load_chunk(0, 0)
        steps = {c.mm: 2 * per_chunk, c.ac: 2 * 9, c.ve: 2 * per_chunk, c.go: 2, c.in_[4]: 1, c.in_[5]: 1,
                 **{c.out[s]: 2 * 2 * 2 for s in range(4)}, c.out[4]: 2, c.out[5]: 2}
        with c.loop(NCHUNK // 2 - 1, steps) as turn:
            for u in range(2):
                chunk(turn * 2 + u, u)
        chunk(NCHUNK - 2, 0)
        chunk(NCHUNK - 1, 1, has_next=False)
        c.barrier()


def normalize(c, st, x, name):
    xn = c.sb(st, name + "_rows", [P, TT, D])
    xt = c.sb(st, name + "_cols", [P, KD, TOK])
    stats = c.sb(st, name + "_stats", [P, TT, 6])
    mv = c.sb(st, name + "_mv", [P, TT, 2])
    std = c.sb(st, name + "_std", [P, TT, 2])
    for t in range(TT):
        m = c.ve.did(c.dve.bn_stats(stats[:, t, :], x[:, t, :]))
    wait(c.dve, m)
    for t in range(TT):
        m = c.ve.did(c.dve.bn_aggr(mv[:, t, :], stats[:, t, :]))
    wait(c.dve, m)
    m = c.ve.did(c.dve.tensor_scalar(std[:, :, 0], mv[:, :, 1], EPS, None, ALU.add))
    wait(c.act, m)
    m = c.ac.did(c.act.activation(std[:, :, 1], std[:, :, 0], ACT.Sqrt))
    wait(c.dve, m)
    m = c.ve.did(c.dve.reciprocal(std[:, :, 0], std[:, :, 1]))
    wait(c.dve, m)
    for t in range(TT):
        m = c.ve.did(c.dve.tensor_scalar(xn[:, t, :], x[:, t, :], mv[:, t, 0:1], std[:, t, 0:1], ALU.subtract, ALU.mult))
    wait(c.pe, m)
    to_columns(c, xt, xn)
    return xn, xt


def to_columns(c, xt, xn):
    for k in range(KD):
        for t in range(TT):
            last = c.pe.transpose(c.bank[k][:, t * P:(t + 1) * P], xn[:, t, k * P:(k + 1) * P], c.ident[:])
        m = c.mm.did(last)
        wait(c.act, m)
        c.ac.did(c.act.copy(xt[:, k, :], c.bank[k][:]))


def linear_t(c, bank, w, xt, b, kd=KD):
    for k in range(kd):
        last = c.pe.matmul(bank, w[:, k, b * P:(b + 1) * P], xt[:, k, :], start=k == 0, stop=k == kd - 1)
    return c.mm.did(last)


def add_rows(c, x, at, w, bias=None, kd=KD):
    for t in range(TT):
        for k in range(kd):
            last = c.pe.matmul(c.bank[t][:], at[:, k, t * P:(t + 1) * P], w[:, k, :], start=k == 0, stop=k == kd - 1)
        m = c.mm.did(last)
        wait(c.dve, m)
        m = c.ve.did(c.dve.tensor_tensor(x[:, t, :], c.bank[t][:], x[:, t, :], ALU.add))
        if bias is not None:
            wait(c.dve, m)
            c.ve.did(c.dve.tensor_tensor(x[:, t, :], x[:, t, :], bias, ALU.add))


def cross_attention(c, A, S, x, l):
    with ExitStack() as st:
        with ExitStack() as st2:
            wq = c.sb(st2, f"wq{l}", [P, KD, D])
            bq = c.sb(st2, f"bq{l}", [P, KD])
            qf = c.sb(st2, f"qf{l}", [P, KD, TOK])
            qparts = c.sb(st2, f"qparts{l}", [P, KD, 2, TOK], F32R)
            load(c, c.in_[0], wq[:], A["wq"][l])
            w_in = load(c, c.in_[0], bq[:], A["bq"][l])
            xn, xt = normalize(c, st2, x, f"ln_a{l}")
            wait(c.pe, c.ac.now(), w_in)
            wait(c.dve, w_in)
            for b in range(KD):
                m = linear_t(c, c.bank[b][:], wq, xt, b)
                wait(c.dve, m)
                m = c.ve.did(c.dve.tensor_scalar(qf[:, b, :], c.bank[b][:], bq[:, b:b + 1], DH ** -0.5, ALU.add, ALU.mult))
                wait(c.dve, m)
                m = c.ve.did(c.dve.tensor_copy(qparts[:, b, 0, :], qf[:, b, :]))
                wait(c.dve, m)
                m = c.ve.did(c.dve.tensor_tensor(qparts[:, b, 1, :], qf[:, b, :], qparts[:, b, 0, :].bitcast(F32), ALU.subtract))
                wait(c.sp, m)
                for part in range(2):
                    c.out[7].did(c.sp.dma_start(S["q"][l, part, b * P:(b + 1) * P, :], qparts[:, b, part, :].bitcast(F32)))
            c.barrier()
        KROWS = 3 * DH + 1
        QUADS, PARTS = KT // 4, 4
        RING = 16
        POOL_QUADS = [q for q in range(QUADS - 2) if q % 3]
        PART = KEYS // PARTS
        ks = [c.sb(st, f"ks{l}_{s}", [KROWS, KEYS], F32R) for s in range(2)]
        qs = [c.sb(st, f"qs{l}_{s}", [KROWS, TOK], F32R) for s in range(2)]
        vs = [c.sb(st, f"vs{l}_{s}", [P, KT, DH]) for s in range(2)]
        pt = c.sb(st, f"pt{l}", [P, RING, TOK])
        pool_sum = c.sb(st, f"pool_sum{l}", [P, TOK])
        run_max = c.sb(st, f"run_max{l}", [P, 2, TOK])
        col_max = c.sb(st, f"col_max{l}", [P, TT])
        partial = c.sb(st, f"partial{l}", [P, 2, TOK])
        total = c.sb(st, f"total{l}", [P, TT])
        rows = c.sb(st, f"head_rows{l}", [P, TT, D])
        wo = c.sb(st, f"wo{l}", [P, KD, D])
        bo = c.sb(st, f"bo{l}", [P, D])
        at = c.sb(st, f"heads{l}", [P, KD, TOK])
        P1_BANK, OUT_BANK, SUM_BANK = 3, 6, 7
        for s in range(2):
            c.ve.did(c.dve.tensor_copy(ks[s][3 * DH:KROWS, :], c.ones[3 * DH:KROWS, 0:1].to_broadcast([1, KEYS])))

        def load_k(h, s, part):
            for at, which in ((0, 0), (1, 1), (2, 0)):
                c.in_[4 * s + part].did(c.sp.dma_start(ks[s][at * DH:(at + 1) * DH, part * PART:(part + 1) * PART].bitcast(F32),
                                                       S["k"][l, which, bass.ds(h * DH, DH), part * PART:(part + 1) * PART]))

        def load_q(h, s):
            for at, which in ((0, 0), (1, 0), (2, 1)):
                c.q_in[s].did(c.sp.dma_start(qs[s][at * DH:(at + 1) * DH, :].bitcast(F32), S["q"][l, which, bass.ds(h * DH, DH), :]))

        def load_v(h, s):
            c.v_in[s].did(c.sp.dma_start(vs[s][:], S["v"][l].rearrange("h p t d -> (h p) (t d)")[bass.ds(h * P, P), :].rearrange("p (t d) -> p t d", d=DH)))

        def first_pass(s, t, read):
            bank = c.bank[P1_BANK + t % 3]
            if t % (KT // PARTS) == 0:
                wait(c.pe, c.in_[4 * s + t // (KT // PARTS)].now())
            wait(c.pe, read[-3])
            m = c.mm.did(c.pe.matmul(bank[:], ks[s][0:3 * DH, t * P:(t + 1) * P], qs[s][0:3 * DH, :], start=True, stop=True))
            wait(c.dve, m, read[-2])
            if t > 1:
                op = c.dve.tensor_tensor(run_max[:, t % 2, :], bank[:], run_max[:, t % 2, :], ALU.max)
            else:
                op = c.dve.tensor_copy(run_max[:, t % 2, :], bank[:])
            read.append(c.ve.did(op))

        def merge_maxima():
            wait(c.dve, c.ve.now())
            return c.ve.did(c.dve.tensor_tensor(run_max[:, 0, :], run_max[:, 0, :], run_max[:, 1, :], ALU.max))

        def shift_columns(merged):
            wait(c.pe, merged)
            for t in range(TT):
                last = c.pe.transpose(c.bank[P1_BANK][:, t * P:(t + 1) * P], run_max[:, 0, t * P:(t + 1) * P], c.ident[:])
            m = c.mm.did(last)
            wait(c.dve, m)
            return c.ve.did(c.dve.tensor_reduce(col_max[:], c.bank[P1_BANK][:].rearrange("p (t n) -> p t n", t=TT), X, ALU.max))

        def shift_row(s, columns):
            wait(c.pe, columns)
            for t in range(TT):
                last = c.pe.matmul(c.bank[P1_BANK + 1][3 * DH:KROWS, t * P:(t + 1) * P], col_max[:, t:t + 1], c.ident[:], start=True, stop=True)
            m = c.mm.did(last)
            wait(c.dve, m)
            return c.ve.did(c.dve.tensor_scalar(qs[s][3 * DH:KROWS, :], c.bank[P1_BANK + 1][3 * DH:KROWS, :], -1.0, None, ALU.mult))

        def second_pass(s, t, exps, summed):
            wait(c.pe, exps[-3])
            bank = c.bank[(t + s) % 3]
            m = c.mm.did(c.pe.matmul(bank[:], ks[s][:, t * P:(t + 1) * P], qs[s][:], start=True, stop=True))
            wait(c.act, m)
            if t - RING in summed:
                wait(c.act, summed[t - RING])
            exps.append(c.ac.did(c.act.activation(pt[:, t % RING, :], bank[:], ACT.Exp)))

        def pool_quad(quad, exp_done, summed):
            wait(c.pool, exp_done)
            tiles = [4 * quad + j for j in range(4)]
            if quad == POOL_QUADS[0]:
                wait(c.pool, c.mm.now())
                t = tiles.pop(0)
                m = c.go.did(c.pool.tensor_tensor(pool_sum[:], pt[:, t % RING, :], pt[:, (t + 1) % RING, :], ALU.add))
                summed[t] = summed[tiles.pop(0)] = m
            for t in tiles:
                wait(c.pool, c.go.now())
                summed[t] = c.go.did(c.pool.tensor_tensor(pool_sum[:], pool_sum[:], pt[:, t % RING, :], ALU.add))

        def weigh(s, quad, exp_done, is_v):
            wait(c.pe, exp_done)
            bank = c.bank[OUT_BANK if is_v else SUM_BANK]
            for j in range(4):
                t = 4 * quad + j
                lhs = vs[s][:, t, :] if is_v else c.ones[:, 0:DH]
                last = c.pe.matmul(bank[j * DH:(j + 1) * DH, :], lhs, pt[:, t % RING, :], start=quad == 0, stop=quad == QUADS - 1)
            return c.mm.did(last)

        def weigh_last(s, exp_done):
            weigh(s, QUADS - 1, exp_done, True)
            wait(c.pe, c.go.now())
            c.pe.matmul(c.bank[SUM_BANK][0:DH, :], c.ones[:, 0:DH], pool_sum[:], start=False, stop=False)
            return weigh(s, QUADS - 1, exp_done, False)

        def take_partials(weighed):
            wait(c.dve, weighed)
            c.ve.did(c.dve.tensor_copy(partial[:, 0, :], c.bank[OUT_BANK][:]))
            return c.ve.did(c.dve.tensor_copy(partial[:, 1, :], c.bank[SUM_BANK][:]))

        def finish_head(h, taken):
            wait(c.pe, taken)
            out, sums = c.bank[P1_BANK][:, 0:TT * DH], c.bank[P1_BANK][:, TT * DH:TT * DH + TT]
            for t in range(TT):
                c.pe.matmul(out[:, t * DH:(t + 1) * DH], partial[:, 0, t * P:(t + 1) * P], c.fold[:], start=True, stop=True)
                last = c.pe.matmul(sums[:, t:t + 1], partial[:, 1, t * P:(t + 1) * P], c.fold[:, 0:1], start=True, stop=True)
            m = c.mm.did(last)
            wait(c.dve, m)
            m = c.ve.did(c.dve.reciprocal(total[:], sums))
            wait(c.dve, m)
            return c.ve.did(c.dve.tensor_tensor(rows[:, :, bass.ds(h * DH, DH)], out.rearrange("p (t d) -> p t d", t=TT),
                                                total[:, :, None].to_broadcast([P, TT, DH]), ALU.mult))

        def head(h, s, has_previous=True, has_next=True, loads=True):
            n = 1 - s
            exps = [c.ac.now(1), c.ac.now(), c.ac.now()]
            last_exp = exps[-1]
            last_pool = [t - KT for q in POOL_QUADS for t in range(4 * q, 4 * q + 4)][1:]
            summed = {t: c.go.now(len(last_pool) - 1 - i) for i, t in enumerate(last_pool)}
            read, columns = [], None
            tiles = list(range(KT)) if has_next else []
            wait(c.pe, c.ve.now(), c.v_in[s].now())

            def next_tiles(count):
                for _ in range(min(count, len(tiles))):
                    first_pass(n, tiles.pop(0), read)

            for quad in range(QUADS):
                weighs = exps[-1]
                second_pass(s, 4 * quad, exps, summed)
                if quad == 0:
                    for t in range(1, 4):
                        second_pass(s, t, exps, summed)
                    if has_previous:
                        taken = take_partials(weigh_last(n, last_exp))
                    if has_next:
                        wait(c.sp, c.mm.now())
                        load_v(h + 1, n)
                    continue
                if quad > 1:
                    next_tiles(1)
                second_pass(s, 4 * quad + 1, exps, summed)
                if quad > 1:
                    next_tiles(1)
                    weigh(s, quad - 1, weighs, True)
                second_pass(s, 4 * quad + 2, exps, summed)
                if quad > 1:
                    next_tiles(1)
                second_pass(s, 4 * quad + 3, exps, summed)
                if loads and (quad + 1) % (QUADS // PARTS) == 0:
                    wait(c.sp, c.mm.now())
                    load_k(h + 2, s, quad // (QUADS // PARTS))
                    if quad == QUADS - 1:
                        load_q(h + 2, s)
                if quad == 1:
                    if has_previous:
                        wait(c.pe, taken)
                    weigh(s, 0, weighs, True)
                    weigh(s, 0, weighs, False)
                    assert 0 not in POOL_QUADS
                    read += 3 * [finish_head(h - 1, taken) if has_previous else c.ve.now()]
                    if has_next:
                        wait(c.pe, c.q_in[n].now())
                    next_tiles(3)
                    continue
                next_tiles(1)
                if quad == QUADS - 1 and has_next:
                    shift_row(n, columns)
                if quad - 1 in POOL_QUADS:
                    pool_quad(quad - 1, weighs, summed)
                else:
                    weigh(s, quad - 1, weighs, False)
                if quad == QUADS - 2 and has_next:
                    columns = shift_columns(merged)
                next_tiles(1)
                if quad == QUADS - 3 and has_next:
                    next_tiles(KT)
                    merged = merge_maxima()

        for s in range(2):
            for part in range(PARTS):
                load_k(s, s, part)
            load_q(s, s)
        load_v(0, 0)
        load(c, c.bias, wo[:], A["wo"][l])
        load(c, c.bias, bo[:], A["bo"][l].partition_broadcast(P))
        read = 3 * [c.ve.now()]
        wait(c.pe, c.q_in[0].now(), c.ve.now())
        for t in range(KT):
            first_pass(0, t, read)
        shift_row(0, shift_columns(merge_maxima()))
        head(0, 0, has_previous=False)
        steps = {c.mm: 2 * (KT + KT + 2 * QUADS - len(POOL_QUADS) + 1 + 2), c.ac: 2 * KT, c.ve: 2 * (2 + 2 + KT + 2 + 1), c.go: 2 * (4 * len(POOL_QUADS) - 1),
                 c.v_in[0]: 1, c.v_in[1]: 1, c.q_in[0]: 3, c.q_in[1]: 3, **{lane: 3 for lane in c.in_}}
        PEELED = 4
        with c.loop((HEADS - PEELED) // 2, steps) as turn:
            for u in range(2):
                head(turn * 2 + 1 + u, 1 - u)
        head(HEADS - 3, 1)
        head(HEADS - 2, 0, loads=False)
        head(HEADS - 1, 1, has_next=False, loads=False)
        finish_head(HEADS - 1, take_partials(weigh_last(1, c.ac.now())))
        wait(c.pe, c.ve.now(), c.bias.now())
        wait(c.dve, c.bias.now())
        to_columns(c, at, rows)
        wait(c.pe, c.ac.now())
        add_rows(c, x, at, wo, bo[:])
        c.barrier()


def silu_conv(c, out, padded, taps, ntap, scratch):
    m = c.ve.did(c.dve.tensor_scalar(scratch, padded[:, 0:TOK], taps[:, 0:1], None, ALU.mult))
    for j in range(1, ntap):
        wait(c.dve, m)
        m = c.ve.did(c.dve.scalar_tensor_tensor(scratch, padded[:, j:j + TOK], taps[:, j:j + 1], scratch, ALU.mult, ALU.add))
    wait(c.act, m)
    return c.ac.did(c.act.activation(out, scratch, ACT.Silu))


def softplus(c, out, v, tmp):
    m = c.ve.did(c.dve.tensor_scalar(tmp, v, -1.0, None, ALU.mult))
    wait(c.dve, m)
    m = c.ve.did(c.dve.tensor_tensor(tmp, v, tmp, ALU.max))
    wait(c.act, m)
    m = c.ac.did(c.act.activation(tmp, tmp, ACT.Exp, scale=-1.0))
    wait(c.act, m)
    m = c.ac.did(c.act.activation(tmp, tmp, ACT.Ln, bias=1.0))
    wait(c.dve, m)
    return c.ve.did(c.dve.scalar_tensor_tensor(out, v, 0.0, tmp, ALU.max, ALU.add))


def selective_scan(c, A, x):
    CB = INNER // P
    with ExitStack() as st:
        w_in = c.sb(st, "w_in", [P, KD, D])
        w_out = c.sb(st, "w_out", [P, KD, D])
        w_x = c.sb(st, "w_x", [P, CB, DTRANK + 2 * DSTATE])
        w_dt = c.sb(st, "w_dt", [DTRANK, INNER])
        chan = c.sb(st, "chan", [P, KD, 3 + 2 + DSTATE])
        rate = c.sb(st, "rate", [P, CB, 2, DSTATE])
        padded = c.sb(st, "padded", [P, KD, TOK + 2])
        conv = c.sb(st, "conv", [P, KD, TOK])
        tmp = c.sb(st, "tmp", [P, 2, TOK])
        dt_raw = c.sb(st, "dt_raw", [DTRANK, TOK])
        bc = c.sb(st, "bc", [DSTATE, 2, TOK])
        delta = c.sb(st, "delta", [P, CB, TOK])
        cterm = c.sb(st, "cterm", [P, DSTATE, TOK])
        bterm = c.sb(st, "bterm", [P, DSTATE, TOK])
        decay = c.sb(st, "decay", [P, 2, TOK])
        drive = c.sb(st, "drive", [P, 2, TOK])
        state = c.sb(st, "state", [P, 2, TOK])
        y = c.sb(st, "y", [P, CB, TOK])
        for to, name in ((w_in, "w_in"), (w_out, "w_out"), (w_x, "w_xproj"), (w_dt, "w_dt"), (chan, "chan")):
            m = load(c, c.in_[0], to[:], A[name])
        ready = m
        wait(c.dve, ready)
        for b in range(KD):
            for edge in (0, TOK + 1):
                c.ve.did(c.dve.memset(padded[:, b, edge:edge + 1], 0.0))
        _, xt = normalize(c, st, x, "ln_s")
        wait(c.pe, ready, c.ac.now())
        for b in range(KD):
            m = linear_t(c, c.bank[b][:], w_in, xt, b)
            wait(c.dve, m)
            m = c.ve.did(c.dve.tensor_copy(padded[:, b, 1:TOK + 1], c.bank[b][:]))
            wait(c.dve, m)
            if b > 1:
                wait(c.dve, c.ac.now(1))
            silu_conv(c, conv[:, b, :], padded[:, b, :], chan[:, b, 0:3], 3, tmp[:, b % 2, :])
        wait(c.pe, c.ac.now())
        for bank, lo, n in ((4, 0, DTRANK), (5, DTRANK, DSTATE), (6, DTRANK + DSTATE, DSTATE)):
            for k in range(CB):
                last = c.pe.matmul(c.bank[bank][0:n, :], w_x[:, k, lo:lo + n], conv[:, k, :], start=k == 0, stop=k == CB - 1)
            m = c.mm.did(last)
        wait(c.act, m)
        m = c.ac.did(c.act.copy(dt_raw[:], c.bank[4][0:DTRANK, :]))
        c.ac.did(c.act.activation(bc[:, 0, :], c.bank[5][0:DSTATE, :], ACT.Tanh))
        c.ac.did(c.act.activation(bc[:, 1, :], c.bank[6][0:DSTATE, :], ACT.Tanh))
        wait(c.pe, m)
        for b in range(CB):
            m = c.mm.did(c.pe.matmul(c.bank[b][:], w_dt[:, b * P:(b + 1) * P], dt_raw[:], start=True, stop=True))
            wait(c.dve, m, c.ac.now())
            m = c.ve.did(c.dve.tensor_scalar(decay[:, b, :], c.bank[b][:], chan[:, b, 3:4], None, ALU.add))
            wait(c.dve, m)
            m = softplus(c, delta[:, b, :], decay[:, b, :], tmp[:, b, :])
            wait(c.dve, m)
            c.ve.did(c.dve.tensor_scalar(delta[:, b, :], delta[:, b, :], 1e-4, 1.0, ALU.max, ALU.min))
            m = softplus(c, rate[:, b, 0, :], chan[:, b, 5:5 + DSTATE], rate[:, b, 1, :])
            wait(c.dve, m)
            c.ve.did(c.dve.tensor_scalar(rate[:, b, 0, :], rate[:, b, 0, :], -1.0, -1e-4, ALU.mult, ALU.add))
        wait(c.pe, c.ac.now(), c.ve.now())
        for s in range(DSTATE):
            for which, to in ((0, bterm), (1, cterm)):
                bank = c.bank[(2 * s + which) % 4]
                wait(c.pe, c.ac.now(3))
                m = c.mm.did(c.pe.matmul(bank[:], c.pick[0:DSTATE, s * P:(s + 1) * P], bc[:, which, :], start=True, stop=True))
                wait(c.act, m)
                c.ac.did(c.act.copy(to[:, s, :], bank[:]))
        wait(c.act, c.ve.now())
        wait(c.dve, c.ac.now())
        for b in range(CB):
            c.ve.did(c.dve.tensor_scalar(y[:, b, :], conv[:, b, :], chan[:, b, 4:5], None, ALU.mult))
            for s in range(DSTATE):
                r = s % 2
                wait(c.act, c.ve.now())
                m = c.ac.did(c.act.activation(decay[:, r, :], delta[:, b, :], ACT.Exp, scale=rate[:, b, 0, s:s + 1]))
                wait(c.dve, m)
                m1 = c.ve.did(c.dve.tensor_tensor(drive[:, r, :], bterm[:, s, :], conv[:, b, :], ALU.mult))
                m = c.ve.did(c.dve.tensor_scalar(decay[:, r, :], decay[:, r, :], 1e-4, 1.0, ALU.max, ALU.min))
                wait(c.dve, m)
                m = c.ve.did(c.dve.tensor_scalar(tmp[:, r, :], decay[:, r, :], -1.0, 1.0, ALU.mult, ALU.add))
                wait(c.dve, m)
                m = c.ve.did(c.dve.tensor_tensor(drive[:, r, :], tmp[:, r, :], drive[:, r, :], ALU.mult))
                wait(c.dve, m)
                m = c.ve.did(c.dve.tensor_tensor_scan(state[:, r, :], decay[:, r, :], drive[:, r, :], 0.0, ALU.mult, ALU.add))
                wait(c.dve, m)
                m = c.ve.did(c.dve.tensor_tensor(tmp[:, r, :], state[:, r, :], cterm[:, s, :], ALU.mult))
                wait(c.dve, m)
                c.ve.did(c.dve.tensor_tensor(y[:, b, :], y[:, b, :], tmp[:, r, :], ALU.add))
        wait(c.dve, c.ve.now())
        for b in range(CB):
            m = c.ve.did(c.dve.tensor_copy(conv[:, b, :], y[:, b, :]))
        wait(c.pe, m)
        add_rows(c, x, conv, w_out)
        c.barrier()


def route(c, st, A, xt, l, wr, br):
    n = f"route{l}_"
    logits = c.sb(st, n + "logits", [P, TT, EXPERTS])
    best = c.sb(st, n + "best", [P, TT, 8])
    index = c.sb(st, n + "index", [P, TT, 8], U32)
    indexf = c.sb(st, n + "indexf", [P, TT, 8])
    hot = c.sb(st, n + "hot", [P, TT, 2, EXPERTS])
    for t in range(TT):
        for k in range(KD):
            last = c.pe.matmul(c.bank[4][:, t * EXPERTS:(t + 1) * EXPERTS], xt[:, k, t * P:(t + 1) * P], wr[:, k, :], start=k == 0, stop=k == KD - 1)
    m = c.mm.did(last)
    wait(c.dve, m)
    m = c.ve.did(c.dve.tensor_tensor(logits[:], c.bank[4][:, 0:TT * EXPERTS].rearrange("p (t e) -> p t e", t=TT), br, ALU.add))
    wait(c.dve, m)
    for t in range(TT):
        m = c.ve.did(c.dve.max(best[:, t, :], logits[:, t, :]))
    wait(c.dve, m)
    for t in range(TT):
        m = c.ve.did(c.dve.max_index(index[:, t, :], best[:, t, :], logits[:, t, :]))
    wait(c.dve, m)
    m = c.ve.did(c.dve.tensor_copy(indexf[:], index[:]))
    wait(c.dve, m)
    for t in range(TT):
        for j in range(2):
            m = c.ve.did(c.dve.tensor_scalar(hot[:, t, j, :], c.iota[:, 0:EXPERTS], indexf[:, t, j:j + 1], None, ALU.is_equal))
    wait(c.dve, m)
    return logits, best, hot


def ranks(c, st, l, chosen):
    rank = c.sb(st, f"rank{l}", [P, TT, EXPERTS])
    count = c.sb(st, f"count{l}", [P, EXPERTS])
    wait(c.pe, c.ve.now())
    for t in range(TT):
        for s in range(t + 1):
            last = c.pe.matmul(c.bank[5][:, t * EXPERTS:(t + 1) * EXPERTS], c.upto[:] if s == t else c.ones[:], chosen[:, s, :], start=s == 0, stop=s == t)
    for s in range(TT):
        last = c.pe.matmul(c.bank[6][:, 0:EXPERTS], c.ones[:], chosen[:, s, :], start=s == 0, stop=s == TT - 1)
    m = c.mm.did(last)
    wait(c.dve, m)
    c.ve.did(c.dve.tensor_copy(count[:], c.bank[6][:, 0:EXPERTS]))
    m = c.ve.did(c.dve.tensor_copy(rank[:], c.bank[5][:, 0:TT * EXPERTS].rearrange("p (t e) -> p t e", t=TT)))
    wait(c.dve, m)
    return rank, count


def expert_tiles(c, st, A, x, xn, pos, gate, l, tiles, expert_of):
    n = f"moe{l}_"
    two = l == 1
    pieces = (3 if two else 2) * FB
    RAW, CUT = (6, 4) if two else (4, 4)
    AHEAD = 3
    OUT_BANK = 2
    JB = FT // FB
    raw = c.sb(st, n + "raw", [P, RAW, KD, 512])
    cut = c.sb(st, n + "cut", [P, CUT, 2, KD, 512], F32R)
    xparts = c.sb(st, n + "xparts", [P, 2, TT, D], F32R)
    sel = c.sb(st, n + "sel", [P, TT, P], F32R)
    selw = c.sb(st, n + "selw", [P, TT, P])
    sel2 = c.sb(st, n + "sel2", [P, TT, P])
    selwt = c.sb(st, n + "selwt", [P, TOK])
    slots = c.sb(st, n + "slots", [P, P])
    xg = c.sb(st, n + "xg", [P, 2, KD, P], F32R)
    h = c.sb(st, n + "h", [P, FF])
    ht = c.sb(st, n + "ht", [P, 2, FT, P], F32R)
    yrow = c.sb(st, n + "yrow", [P, D])
    if not two:
        bias1 = c.sb(st, n + "bias1", [P, FT])
        bias2 = c.sb(st, n + "bias2", [P, D])
        act_out = c.sb(st, n + "act_out", [P, 2, JB, P])
    split(c, xparts[:, 0], xparts[:, 1], xn[:])
    c.ve.did(c.dve.tensor_copy(slots[:], c.iota[:]))
    c.ve.did(c.dve.memset(selwt[:], 0.0))
    c.ve.did(c.dve.memset(yrow[:], 0.0))
    wait(c.dve, c.ve.now())

    def split_piece(w):
        turn_loads = pieces // RAW
        wait(c.act, c.in_[w % RAW].now(turn_loads - (w // RAW + 1)), c.used.now(CUT - AHEAD - 1))
        m = c.ac.did(c.act.copy(cut[:, w % CUT, 0], raw[:, w % RAW]))
        wait(c.dve, m)
        c.cut.did(c.dve.tensor_tensor(cut[:, w % CUT, 1], raw[:, w % RAW], cut[:, w % CUT, 0].bitcast(F32), ALU.subtract))

    def select(t):
        m = c.ve.did(c.dve.tensor_scalar(sel[:, t, :], slots[:], pos[0][:, t:t + 1], None, ALU.is_equal))
        m2 = c.ve.did(c.dve.tensor_scalar(selw[:, t, :], slots[:], pos[0][:, t:t + 1], gate[0][:, t:t + 1], ALU.is_equal, ALU.mult))
        if two:
            m3 = c.ve.did(c.dve.tensor_scalar(sel2[:, t, :], slots[:], pos[1][:, t:t + 1], gate[1][:, t:t + 1], ALU.is_equal, ALU.mult))
            wait(c.dve, m)
            c.ve.did(c.dve.scalar_tensor_tensor(sel[:, t, :], slots[:], pos[1][:, t:t + 1], sel[:, t, :].bitcast(F32), ALU.is_equal, ALU.add))
            wait(c.dve, m3)
            c.ve.did(c.dve.tensor_tensor(selw[:, t, :], selw[:, t, :], sel2[:, t, :], ALU.add))

    def next_slots():
        wait(c.dve, c.ve.now())
        m = c.ve.did(c.dve.tensor_scalar(slots[:], slots[:], float(P), None, ALU.add))
        wait(c.dve, m)

    def gather(*ready):
        wait(c.pe, *ready)
        for part in range(2):
            for k in range(KD):
                for t in range(TT):
                    last = c.pe.matmul(c.bank[6 + part][:, k * P:(k + 1) * P], xparts[:, part, t, k * P:(k + 1) * P], sel[:, t, :], start=t == 0, stop=t == TT - 1)
        wait(c.act, c.mm.did(last))
        for part in range(2):
            m = c.ac.did(c.act.copy(xg[:, part], c.bank[6 + part].rearrange("p (k n) -> p k n", k=KD)))
        return m

    for t in range(TT):
        select(t)
    for w in range(AHEAD):
        split_piece(w + pieces)
    gather(c.ve.now())

    def scatter(t, *ready):
        wait(c.pe, *ready)
        m = c.mm.did(c.pe.matmul(c.bank[6 + t % 2], selwt[:, t * P:(t + 1) * P], yrow[:], start=True, stop=True))
        wait(c.dve, m)
        return c.ve.did(c.dve.tensor_tensor(x[:, t, :], c.bank[6 + t % 2], x[:, t, :], ALU.add))

    def tile(j, has_next):
        expert = expert_of(j)
        before, gathered = c.ve.now(), c.ac.now()
        for w in range(pieces):
            slot = w % RAW
            wait(c.sp, c.cut.now(AHEAD - 1 - w + RAW))
            load(c, c.in_[slot], raw[:, slot], A[n + "w"][bass.ds((expert * pieces + w) * P, P), :].rearrange("p (k n) -> p k n", k=KD))
            if not two and w == RAW - 1:
                wait(c.sp, gathered, before)
                load(c, c.bias, bias1[:], A[n + "b1"][bass.ds(expert * P, P), :])
                load(c, c.bias, bias2[:], A[n + "b2"][bass.ds(expert * P, P), :])
                biases = c.bias.now()
        wait(c.pe, gathered)
        read = {}

        def piece(w, matmuls):
            if has_next or w + AHEAD < pieces:
                split_piece(w + AHEAD)
            wait(c.pe, c.cut.now(AHEAD if has_next else min(AHEAD, pieces - 1 - w)))
            return c.used.did(matmuls([cut[:, w % CUT, part] for part in range(2)]))

        def into_hidden(bank):
            def matmuls(parts):
                for k in range(KD):
                    last = product(c, bank, [xg[:, part, k, :] for part in range(2)], [p[:, k, :] for p in parts], k == 0, k == KD - 1)
                return last
            return matmuls

        def hidden(fb):
            banks = [c.bank[2 * (fb % 2)], c.bank[2 * (fb % 2) + 1]]
            part = h[:, fb * 512:(fb + 1) * 512]
            if fb >= 2:
                wait(c.pe, read[fb - 2])
            if not two:
                m = piece(fb, into_hidden(banks[0]))
                wait(c.act, m)
                read[fb] = c.ac.did(c.act.copy(part, banks[0]))
                return
            m = piece(2 * fb, into_hidden(banks[0]))
            m2 = piece(2 * fb + 1, into_hidden(banks[1]))
            wait(c.act, m)
            m = c.ac.did(c.act.activation(part, banks[0], ACT.Silu))
            wait(c.dve, m, m2)
            read[fb] = c.ve.did(c.dve.tensor_tensor(part, part, banks[1], ALU.mult))

        def turn_hidden(fb):
            bank = c.bank[4 + fb % 2]
            wait(c.pe, read[fb])
            if fb >= 2:
                wait(c.pe, read["t", fb - 2])
            for j in range(JB):
                last = c.pe.transpose(bank[:, j * P:(j + 1) * P], h[:, (fb * JB + j) * P:(fb * JB + j + 1) * P], c.ident[:])
            m = c.mm.did(last)
            wait(c.act, m)
            high, low = (ht[:, part, fb * JB:(fb + 1) * JB, :] for part in range(2))
            source = bank.rearrange("p (j n) -> p j n", j=JB)
            if not two:
                if fb == 0:
                    wait(c.act, biases)
                source = act_out[:, fb % 2]
                for j in range(JB):
                    m = c.ac.did(c.act.activation(source[:, j, :], bank[:, j * P:(j + 1) * P], ACT.Gelu, bias=bias1[:, fb * JB + j:fb * JB + j + 1]))
                wait(c.act, m)
            m = c.ac.did(c.act.copy(high, source))
            wait(c.dve, m)
            read["t", fb] = c.ve.did(c.dve.tensor_tensor(low, source, high.bitcast(F32), ALU.subtract))

        def out_of_hidden(db):
            def matmuls(parts):
                for i in range(JB):
                    f = db * JB + i
                    last = product(c, c.bank[OUT_BANK], [ht[:, part, f, :] for part in range(2)], [p[:, i, :] for p in parts], f == 0, f == FT - 1)
                return last
            return matmuls

        hidden(0)
        added = [scatter(0, before), scatter(1, gathered)]
        hidden(1)
        turn_hidden(0)
        added += [scatter(2, added[0]), scatter(3, added[1])]
        hidden(2)
        turn_hidden(1)
        wait(c.pe, added[3])
        for t in range(TT):
            last = c.pe.transpose(c.bank[7][:, t * P:(t + 1) * P], selw[:, t, :], c.ident[:])
        turned = c.mm.did(last)
        wait(c.act, turned)
        weights = c.ac.did(c.act.copy(selwt[:], c.bank[7]))
        if has_next:
            wait(c.dve, turned)
            next_slots()
            for t in range(TT):
                select(t)
            selected = c.ve.now()
        hidden(3)
        turn_hidden(2)
        if has_next:
            gather(selected, added[2], weights)
        for db in range(FB):
            wait(c.pe, read["t", db], *([read[3]] if db == 0 else []))
            m = piece(pieces - FB + db, out_of_hidden(db))
            if db == 0:
                turn_hidden(3)
        wait(c.dve, m)
        if two:
            c.ve.did(c.dve.tensor_copy(yrow[:], c.bank[OUT_BANK]))
        else:
            wait(c.dve, biases)
            c.ve.did(c.dve.tensor_tensor(yrow[:], c.bank[OUT_BANK], bias2[:], ALU.add))

    steps = {c.mm: 1 + FB + 1 + TT, c.used: pieces, c.cut: pieces,
             c.ac: pieces + 1 + 2 + FB + FB * (1 if two else 1 + JB),
             c.ve: 1 + TT * (5 if two else 2) + (FB if two else 0) + FB + 1 + TT,
             **{c.in_[r]: pieces // RAW for r in range(RAW)}}
    if not two:
        steps[c.bias] = 2
    with c.loop(tiles - 1, steps) as turn:
        tile(turn, True)
    tile(tiles - 1, False)
    for t in range(TT):
        scatter(t, c.ve.now())
    c.barrier()


def experts_top1(c, A, x):
    with ExitStack() as st:
        wr = c.sb(st, "wr0", [P, KD, EXPERTS])
        br = c.sb(st, "br0", [P, TT, EXPERTS])
        small = c.sb(st, "small0", [P, 6, TT])
        prod = c.sb(st, "prod0", [P, TT, EXPERTS])
        ready = load(c, c.in_[7], wr[:], A["moe0_router"])
        c.ve.did(c.dve.memset(br[:], 0.0))
        xn, xt = normalize(c, st, x, "ln_m0")
        wait(c.pe, ready, c.ac.now())
        logits, best, hot = route(c, st, A, xt, 0, wr, br[:])
        rank, _ = ranks(c, st, 0, hot[:, :, 0, :])
        for t in range(TT):
            m = c.ve.did(c.dve.tensor_scalar(prod[:, t, :], logits[:, t, :], best[:, t, 0:1], None, ALU.subtract))
        wait(c.act, m)
        m = c.ac.did(c.act.activation(prod[:], prod[:], ACT.Exp))
        wait(c.dve, m)
        total, weight, r, e, valid, slot = (small[:, k, :] for k in range(6))
        m = c.ve.did(c.dve.tensor_reduce(total, prod[:], X, ALU.add))
        wait(c.dve, m)
        c.ve.did(c.dve.reciprocal(weight, total))
        m = c.ve.did(c.dve.tensor_tensor(prod[:], hot[:, :, 0, :], rank[:], ALU.mult))
        wait(c.dve, m)
        m = c.ve.did(c.dve.tensor_reduce(r, prod[:], X, ALU.add))
        wait(c.dve, m)
        m = c.ve.did(c.dve.tensor_tensor(prod[:], hot[:, :, 0, :], c.iota[:, None, 0:EXPERTS].to_broadcast([P, TT, EXPERTS]), ALU.mult))
        wait(c.dve, m)
        m = c.ve.did(c.dve.tensor_reduce(e, prod[:], X, ALU.add))
        c.ve.did(c.dve.tensor_scalar(valid, r, float(CAPACITY), None, ALU.is_le))
        wait(c.dve, c.ve.now())
        m = c.ve.did(c.dve.scalar_tensor_tensor(slot, e, float(P), r, ALU.mult, ALU.add))
        wait(c.dve, m)
        m = c.ve.did(c.dve.tensor_tensor(slot, slot, valid, ALU.mult))
        wait(c.dve, m)
        m = c.ve.did(c.dve.tensor_scalar(slot, slot, -1.0, None, ALU.add))
        wait(c.dve, m)
        expert_tiles(c, st, A, x, xn, [slot], [weight], 0, EXPERTS, lambda turn: turn)


def experts_top2(c, A, x):
    with ExitStack() as st:
        wr = c.sb(st, "wr1", [P, KD, EXPERTS])
        br = c.sb(st, "br1", [P, TT, EXPERTS])
        small = c.sb(st, "small1", [P, 5, TT])
        prod = c.sb(st, "prod1", [P, TT, EXPERTS])
        chosen = c.sb(st, "chosen1", [P, TT, EXPERTS])
        tile_of = c.sb(st, "tile_of", [P, 4, EXPERTS])
        owner = c.sb(st, "owner", [1, TILES1, EXPERTS])
        ownerf = c.sb(st, "ownerf", [1, TILES1])
        owneri = c.sb(st, "owneri", [1, TILES1], I32)
        load(c, c.in_[7], wr[:], A["moe1_router"])
        for t in range(TT):
            ready = load(c, c.in_[7], br[:, t, :], A["moe1_router_b"].partition_broadcast(P))
        xn, xt = normalize(c, st, x, "ln_m1")
        wait(c.pe, ready, c.ac.now())
        wait(c.dve, ready)
        logits, best, hot = route(c, st, A, xt, 1, wr, br[:])
        m = c.ve.did(c.dve.tensor_tensor(chosen[:], hot[:, :, 0, :], hot[:, :, 1, :], ALU.add))
        rank, count = ranks(c, st, 1, chosen)
        d, w1, w2, slot1, slot2 = (small[:, k, :] for k in range(5))
        m = c.ve.did(c.dve.tensor_tensor(d, best[:, :, 1], best[:, :, 0], ALU.subtract))
        wait(c.act, m)
        m = c.ac.did(c.act.activation(d, d, ACT.Exp))
        wait(c.dve, m)
        m = c.ve.did(c.dve.tensor_scalar(w2, d, 1.0, None, ALU.add))
        wait(c.dve, m)
        m = c.ve.did(c.dve.reciprocal(w1, w2))
        wait(c.dve, m)
        c.ve.did(c.dve.tensor_tensor(w2, d, w1, ALU.mult))
        need, end, start, part = (tile_of[:, k, :] for k in range(4))
        m = c.ve.did(c.dve.tensor_scalar(need, count[:], 0.0, None, ALU.is_gt))
        for k in range(1, TT):
            wait(c.dve, m)
            m = c.ve.did(c.dve.scalar_tensor_tensor(need, count[:], float(k * P), need, ALU.is_gt, ALU.add))
        wait(c.dve, m)
        m = c.ve.did(c.dve.tensor_tensor_scan(end, c.ones[:, 0:EXPERTS], need, 0.0, ALU.mult, ALU.add))
        wait(c.dve, m)
        m = c.ve.did(c.dve.tensor_tensor(start, end, need, ALU.subtract))
        wait(c.dve, m)
        m = c.ve.did(c.dve.tensor_scalar(start, start, float(P), -1.0, ALU.mult, ALU.add))
        wait(c.dve, m)
        m = c.ve.did(c.dve.tensor_tensor(chosen[:], rank[:], start[:, None, :].to_broadcast([P, TT, EXPERTS]), ALU.add))
        wait(c.dve, m)
        for j, slot in ((0, slot1), (1, slot2)):
            m = c.ve.did(c.dve.tensor_tensor(prod[:], hot[:, :, j, :], chosen[:], ALU.mult))
            wait(c.dve, m)
            m = c.ve.did(c.dve.tensor_reduce(slot, prod[:], X, ALU.add))
            wait(c.dve, m)
        m = c.ve.did(c.dve.tensor_tensor(owner[:], end[0:1, None, :].to_broadcast([1, TILES1, EXPERTS]),
                                         c.iota[0:1, 0:TILES1, None].to_broadcast([1, TILES1, EXPERTS]), ALU.is_le))
        wait(c.dve, m)
        m = c.ve.did(c.dve.tensor_reduce(ownerf[:], owner[:], X, ALU.add))
        wait(c.dve, m)
        m = c.ve.did(c.dve.tensor_scalar(ownerf[:], ownerf[:], float(EXPERTS - 1), None, ALU.min))
        wait(c.dve, m)
        m = c.ve.did(c.dve.tensor_copy(owneri[:], ownerf[:]))
        wait(c.sp, m)
        expert_tiles(c, st, A, x, xn, [slot1, slot2], [w1, w2], 1, TILES1,
                     lambda turn: c.sp.value_load(owneri[0:1, bass.ds(turn, 1)], min_val=0, max_val=EXPERTS - 1))


def delta_rule(c, A, x):
    with ExitStack() as st:
        w = [c.sb(st, "dw_" + n, [P, KD, D]) for n in "qkvo"]
        wb = c.sb(st, "dw_b", [P, KD, DHEADS])
        taps = c.sb(st, "taps", [P, 3, KD, CONV])
        g_rms = c.sb(st, "g_rms", [P, 1])
        ln = c.sb(st, "ln_gb", [P, 2, D])
        padded = c.sb(st, "dpadded", [P, 2, TOK + CONV - 1])
        feat = [c.sb(st, "feat_" + n, [P, DHEADS, TOK]) for n in "qkv"]
        tmp = c.sb(st, "dtmp", [P, 4, TOK])
        beta = c.sb(st, "beta", [P, TT, DHEADS])
        for to, n in zip(w, "qkvo"):
            load(c, c.in_[0], to[:], A["d_w" + n])
        load(c, c.in_[0], wb[:], A["d_wb"])
        load(c, c.in_[0], taps[:], A["d_taps"])
        load(c, c.in_[0], g_rms[:], A["d_rms"])
        load(c, c.in_[0], ln[:, 0, :], A["d_lng"].partition_broadcast(P))
        ready = load(c, c.in_[0], ln[:, 1, :], A["d_lnb"].partition_broadcast(P))
        c.ve.did(c.dve.memset(padded[:, :, 0:CONV - 1], 0.0))
        xn, xt = normalize(c, st, x, "ln_d")
        wait(c.pe, ready, c.ac.now())
        wait(c.dve, ready)
        for i in range(3):
            for b in range(DHEADS):
                r = b % 2
                wait(c.pe, c.ve.now(2))
                m = linear_t(c, c.bank[r][:], w[i], xt, b)
                wait(c.dve, m)
                m = c.ve.did(c.dve.tensor_copy(padded[:, r, CONV - 1:], c.bank[r][:]))
                wait(c.dve, m, c.ac.now(1))
                silu_conv(c, feat[i][:, b, :], padded[:, r, :], taps[:, i, b, :], CONV, tmp[:, r, :])
        for t in range(TT):
            for k in range(KD):
                last = c.pe.matmul(c.bank[4][:, t * DHEADS:(t + 1) * DHEADS], xt[:, k, t * P:(t + 1) * P], wb[:, k, :], start=k == 0, stop=k == KD - 1)
        m = c.mm.did(last)
        wait(c.act, m)
        c.ac.did(c.act.activation(beta[:], c.bank[4][:, 0:TT * DHEADS].rearrange("p (t h) -> p t h", t=TT), ACT.Sigmoid))
        wait(c.dve, c.ac.now())
        for i in range(2):
            for b in range(DHEADS):
                r = b % 4
                wait(c.dve, c.mm.now())
                m = c.ve.did(c.dve.tensor_tensor(tmp[:, r, :], feat[i][:, b, :], feat[i][:, b, :], ALU.mult))
                wait(c.pe, m)
                m = c.mm.did(c.pe.matmul(c.bank[r][:], c.ones[:], tmp[:, r, :], start=True, stop=True))
                wait(c.dve, m)
                m = c.ve.did(c.dve.tensor_scalar(tmp[:, r, :], c.bank[r][:], 1e-6, None, ALU.add))
                wait(c.act, m)
                m = c.ac.did(c.act.activation(tmp[:, r, :], tmp[:, r, :], ACT.Sqrt))
                wait(c.dve, m)
                m = c.ve.did(c.dve.reciprocal(tmp[:, r, :], tmp[:, r, :]))
                wait(c.dve, m)
                c.ve.did(c.dve.tensor_tensor(feat[i][:, b, :], feat[i][:, b, :], tmp[:, r, :], ALU.mult))
        c.barrier()
        q, k, v = feat
        per = lambda n: c.sb(st, n, [P, TT, DHEADS, P])
        below, below_t, inv, inv_t, qk, vrow, krow = (per("d_" + n) for n in ("below", "below_t", "inv", "inv_t", "qk", "vrow", "krow"))
        lev = c.sb(st, "d_lev", [P, 2, DHEADS, P])
        prod = c.sb(st, "d_prod", [P, 2, DHEADS, P])
        flat = lambda a: a.rearrange("p h n -> p (h n)")
        over_heads = lambda mask: mask[:, None, :].to_broadcast([P, DHEADS, P])
        heads_of = lambda bank: bank[:].rearrange("p (h n) -> p h n", h=DHEADS)

        def four(bank, lhs, rhs):
            for h in range(DHEADS):
                last = c.pe.matmul(bank[:, h * P:(h + 1) * P], lhs(h), rhs(h), start=True, stop=True)
            return c.mm.did(last)

        def four_transposes(bank, of):
            for h in range(DHEADS):
                last = c.pe.transpose(bank[:, h * P:(h + 1) * P], of(h), c.ident[:])
            return c.mm.did(last)

        for t in range(TT):
            at = slice(t * P, (t + 1) * P)
            wait(c.pe, c.ve.now(), c.ac.now())
            m = four(c.bank[0], lambda h: k[:, h, at], lambda h: k[:, h, at])
            wait(c.dve, m)
            for h in range(DHEADS):
                m = c.ve.did(c.dve.scalar_tensor_tensor(below[:, t, h, :], c.bank[0][:, h * P:(h + 1) * P], beta[:, t, h:h + 1], c.lower[:], ALU.mult, ALU.mult))
            m2 = four(c.bank[1], lambda h: k[:, h, at], lambda h: q[:, h, at])
            wait(c.dve, m2)
            c.ve.did(c.dve.tensor_tensor(qk[:, t], heads_of(c.bank[1]), over_heads(c.upto), ALU.mult))
            m2 = four_transposes(c.bank[2], lambda h: v[:, h, at])
            wait(c.act, m2)
            c.ac.did(c.act.copy(flat(vrow[:, t]), c.bank[2][:]))
            m2 = four_transposes(c.bank[3], lambda h: k[:, h, at])
            wait(c.act, m2)
            c.ac.did(c.act.copy(flat(krow[:, t]), c.bank[3][:]))
            wait(c.pe, m)
            m2 = four_transposes(c.bank[4], lambda h: below[:, t, h, :])
            wait(c.dve, m2)
            m = c.ve.did(c.dve.tensor_copy(flat(below_t[:, t]), c.bank[4][:]))
            wait(c.dve, m)
            c.ve.did(c.dve.tensor_tensor(inv[:, t], below[:, t], over_heads(c.level0), ALU.mult))
            c.ve.did(c.dve.tensor_tensor(inv_t[:, t], below_t[:, t], over_heads(c.level_t[0]), ALU.mult))
            wait(c.dve, c.ve.now())
            c.ve.did(c.dve.tensor_tensor(inv[:, t], over_heads(c.ident), inv[:, t], ALU.subtract))
            c.ve.did(c.dve.tensor_tensor(inv_t[:, t], over_heads(c.ident), inv_t[:, t], ALU.subtract))
        for level in range(1, LEVELS):
            for t in range(TT):
                r = t % 2
                wait(c.dve, c.mm.now(), c.ve.now())
                m = c.ve.did(c.dve.tensor_tensor(lev[:, r], below_t[:, t], over_heads(c.level_t[level]), ALU.mult))
                wait(c.pe, m)
                m = four(c.bank[4 * r], lambda h: lev[:, r, h, :], lambda h: inv[:, t, h, :])
                wait(c.act, m)
                m = c.ac.did(c.act.copy(flat(prod[:, r]), c.bank[4 * r][:]))
                wait(c.pe, m)
                m = four(c.bank[4 * r + 1], lambda h: inv_t[:, t, h, :], lambda h: prod[:, r, h, :])
                m2 = four(c.bank[4 * r + 2], lambda h: prod[:, r, h, :], lambda h: inv_t[:, t, h, :])
                wait(c.dve, m2)
                c.ve.did(c.dve.tensor_tensor(inv[:, t], inv[:, t], heads_of(c.bank[4 * r + 1]), ALU.subtract))
                c.ve.did(c.dve.tensor_tensor(inv_t[:, t], inv_t[:, t], heads_of(c.bank[4 * r + 2]), ALU.subtract))
        c.barrier()
        S = c.sb(st, "d_state", [P, DHEADS, P])
        rhs = c.sb(st, "d_rhs", [P, DHEADS, P])
        u = c.sb(st, "d_u", [P, DHEADS, P])
        o = c.sb(st, "d_o", [P, TT, DHEADS, P])
        osq = c.sb(st, "d_osq", [P, TT, DHEADS, P])
        rms = c.sb(st, "d_rms_of", [P, 2, TT, DHEADS])
        m = c.ve.did(c.dve.memset(flat(S[:]), 0.0))
        wait(c.dve, m)
        for t in range(TT):
            at = slice(t * P, (t + 1) * P)
            wait(c.pe, c.ve.now())
            m = four(c.bank[0], lambda h: k[:, h, at], lambda h: S[:, h, :])
            wait(c.dve, m)
            m = c.ve.did(c.dve.tensor_tensor(rhs[:], vrow[:, t], heads_of(c.bank[0]), ALU.subtract))
            wait(c.dve, m)
            m = c.ve.did(c.dve.tensor_tensor(rhs[:], rhs[:], beta[:, t, :, None].to_broadcast([P, DHEADS, P]), ALU.mult))
            wait(c.pe, m)
            m = four(c.bank[1], lambda h: inv_t[:, t, h, :], lambda h: rhs[:, h, :])
            wait(c.dve, m)
            m = c.ve.did(c.dve.tensor_copy(flat(u[:]), c.bank[1][:]))
            wait(c.pe, m)
            for h in range(DHEADS):
                c.pe.matmul(c.bank[2][:, h * P:(h + 1) * P], q[:, h, at], S[:, h, :], start=True, stop=False)
                last = c.pe.matmul(c.bank[2][:, h * P:(h + 1) * P], qk[:, t, h, :], u[:, h, :], start=False, stop=True)
            mo = c.mm.did(last)
            ms = four(c.bank[3], lambda h: krow[:, t, h, :], lambda h: u[:, h, :])
            wait(c.dve, ms)
            c.ve.did(c.dve.tensor_tensor(S[:], S[:], heads_of(c.bank[3]), ALU.add))
            c.ve.did(c.dve.tensor_copy(flat(o[:, t]), c.bank[2][:]))
        wait(c.dve, c.ve.now())
        c.ve.did(c.dve.tensor_tensor(osq[:], o[:], o[:], ALU.mult))
        wait(c.dve, c.ve.now())
        c.ve.did(c.dve.tensor_reduce(rms[:, 0], osq[:], X, ALU.add))
        wait(c.dve, c.ve.now())
        m = c.ve.did(c.dve.tensor_scalar(rms[:, 0], rms[:, 0], 1.0 / P, EPS, ALU.mult, ALU.add))
        wait(c.act, m)
        m = c.ac.did(c.act.activation(rms[:, 1], rms[:, 0], ACT.Sqrt))
        wait(c.dve, m)
        m = c.ve.did(c.dve.reciprocal(rms[:, 0], rms[:, 1]))
        wait(c.dve, m)
        m = c.ve.did(c.dve.tensor_tensor(osq[:], o[:], rms[:, 0, :, :, None].to_broadcast([P, TT, DHEADS, P]), ALU.mult))
        wait(c.pe, m)
        for h in range(DHEADS):
            for t in range(TT):
                last = c.pe.transpose(c.bank[4 + h][:, t * P:(t + 1) * P], osq[:, t, h, :], c.ident[:])
            m = c.mm.did(last)
            wait(c.act, m)
            c.ac.did(c.act.activation(xt[:, h, :], c.bank[4 + h][:], ACT.Identity, scale=g_rms[:, 0:1]))
        wait(c.pe, c.ac.now())
        add_rows(c, xn, xt, w[3])
        wait(c.dve, c.ve.now())
        stats = c.sb(st, "y_stats", [P, TT, 6])
        mv = c.sb(st, "y_mv", [P, TT, 2])
        std = c.sb(st, "y_std", [P, TT, 2])
        for t in range(TT):
            c.ve.did(c.dve.bn_stats(stats[:, t, :], xn[:, t, :]))
        wait(c.dve, c.ve.now())
        for t in range(TT):
            c.ve.did(c.dve.bn_aggr(mv[:, t, :], stats[:, t, :]))
        wait(c.dve, c.ve.now())
        m = c.ve.did(c.dve.tensor_scalar(std[:, :, 0], mv[:, :, 1], EPS, None, ALU.add))
        wait(c.act, m)
        m = c.ac.did(c.act.activation(std[:, :, 1], std[:, :, 0], ACT.Sqrt))
        wait(c.dve, m)
        m = c.ve.did(c.dve.reciprocal(std[:, :, 0], std[:, :, 1]))
        wait(c.dve, m)
        for t in range(TT):
            c.ve.did(c.dve.tensor_scalar(xn[:, t, :], xn[:, t, :], mv[:, t, 0:1], std[:, t, 0:1], ALU.subtract, ALU.mult))
        for which, op in ((0, ALU.mult), (1, ALU.add)):
            wait(c.dve, c.ve.now())
            c.ve.did(c.dve.tensor_tensor(xn[:], xn[:], ln[:, which, None, :].to_broadcast([P, TT, D]), op))
        wait(c.dve, c.ve.now())
        c.ve.did(c.dve.tensor_tensor(x[:], x[:], xn[:], ALU.add))
        c.barrier()


def perceiver(nc, A, out, stages=range(1, 8)):
    with ExitStack() as ctx:
        c = Core(nc, ctx)
        scratch = {
            "k": nc.dram_tensor("k_parts", [2, 2, D, KEYS], F32, kind="Internal").ap(),
            "v": nc.dram_tensor("v_heads", [2, HEADS, P, KT, DH], F32, kind="Internal").ap(),
            "q": nc.dram_tensor("q_parts", [2, 2, D, TOK], F32, kind="Internal").ap(),
            "heads": nc.dram_tensor("head_outputs", [D, TOK], F32, kind="Internal").ap(),
        }
        x = c.sb(ctx, "x_rows", [P, TT, D])
        const = c.sb(ctx, "constants", [P, CONST_COLS])
        for name, (lo, hi) in CONST_AT.items():
            c.const[name] = const[:, lo:hi]
        c.ident, c.ones, c.iota, c.upto, c.lower, c.level0, c.fold, c.pick = (
            c.const[n] for n in ("ident", "ones", "iota", "upto", "lower", "level0", "fold", "pick"))
        c.level_t = [c.const["level_t"][:, k * P:(k + 1) * P] for k in range(LEVELS)]
        load(c, c.in_[0], const[:], A["constants"])
        load(c, c.in_[0], x[:], A["x"].rearrange("(t p) d -> p t d", p=P))
        c.barrier()
        if 1 in stages:
            project_context(c, A, scratch)
        if 2 in stages:
            cross_attention(c, A, scratch, x, 0)
        if 3 in stages:
            selective_scan(c, A, x)
        if 4 in stages:
            experts_top1(c, A, x)
        if 5 in stages:
            cross_attention(c, A, scratch, x, 1)
        if 6 in stages:
            delta_rule(c, A, x)
        if 7 in stages:
            experts_top2(c, A, x)
        c.out[0].did(nc.sync.dma_start(out.rearrange("(t p) d -> p t d", p=P), x[:]))
        wait(nc.sync, c.out[0].now())


CONST_AT, CONST_COLS = {}, 0
for _name, _cols in (("ident", P), ("ones", P), ("iota", P), ("upto", P), ("lower", P), ("level0", P),
                     ("level_t", LEVELS * P), ("fold", DH), ("pick", DSTATE * P)):
    CONST_AT[_name] = (CONST_COLS, CONST_COLS + _cols)
    CONST_COLS += _cols



def constants(np):
    i, j = np.arange(P)[:, None], np.arange(P)[None, :]
    level = [(i // (2 << n) == j // (2 << n)) & ((i >> n) % 2 == 1) & ((j >> n) % 2 == 0) for n in range(LEVELS)]
    parts = {
        "ident": i == j, "ones": i + j >= 0, "iota": j + 0 * i, "upto": i <= j, "lower": i > j, "level0": level[0],
        "level_t": np.concatenate([m.T for m in level], 1),
        "fold": i % DH == j[:, :DH],
        "pick": np.concatenate([(i == s) & (j >= 0) for s in range(DSTATE)], 1),
    }
    return np.concatenate([parts[n].astype(np.float32) for n in CONST_AT], 1)


def arrange(np, x, ctx_1024, **w):
    def rows(a, k=None):
        return a.reshape(-1, P, a.shape[-1]).transpose(1, 0, 2)

    def column(a):
        return a.reshape(-1, P).T

    ipw, ipb = w["L1_xattn_in_proj_weight"], w["L1_xattn_in_proj_bias"]
    g, u, dn = w["L1_ffn_gate_w"], w["L1_ffn_up_w"], w["L1_ffn_down_w"]

    def in_pieces(a):
        return a.reshape(EXPERTS, KD, P, FB, 512).transpose(0, 3, 2, 1, 4).reshape(EXPERTS, FB, P, KD * 512)

    def out_pieces(a):
        return a.reshape(EXPERTS, FB, 4, P, D).transpose(0, 1, 3, 2, 4).reshape(EXPERTS, FB, P, 4 * D)

    gu = np.stack([in_pieces(g.transpose(0, 2, 1)), in_pieces(u.transpose(0, 2, 1))], 2).reshape(EXPERTS, 2 * FB, P, KD * 512)
    A = {
        "constants": constants(np),
        "x": x.reshape(TOK, D),
        "ctx": ctx_1024.reshape(NCHUNK, CHUNK, KD, P).transpose(0, 3, 2, 1).reshape(NCHUNK * P, KD * CHUNK),
        "wq": np.stack([rows(w["L0_xattn_W_Q"]), rows(ipw[0:D].T)]),
        "wk": np.stack([rows(w["L0_xattn_W_K"]), rows(ipw[D:2 * D].T)]),
        "wv": np.stack([rows(w["L0_xattn_W_V"]), rows(ipw[2 * D:].T)]),
        "wo": np.stack([rows(w["L0_xattn_W_O"]), rows(w["L1_xattn_out_w"].T)]),
        "bq": np.stack([column(w["L0_xattn_b_Q"]), column(ipb[0:D])]),
        "bk": np.stack([column(w["L0_xattn_b_K"]), column(ipb[D:2 * D])]),
        "bv": np.stack([w["L0_xattn_b_V"], ipb[2 * D:]]),
        "bo": np.stack([w["L0_xattn_b_O"], w["L1_xattn_out_b"]]),
        "w_in": rows(w["L0_attn_W_in"].T),
        "w_out": rows(w["L0_attn_W_out"].T),
        "w_xproj": rows(w["L0_attn_W_xproj"].T),
        "w_dt": w["L0_attn_W_dt"].T,
        "chan": np.concatenate([
            rows(np.concatenate([w["L0_attn_Kx"], w["L0_attn_Kz"]]).reshape(D, 3)),
            rows(np.concatenate([w["L0_attn_b_dt"]] * 2).reshape(D, 1)),
            rows(np.concatenate([w["L0_attn_D"]] * 2).reshape(D, 1)),
            rows(np.concatenate([w["L0_attn_A_log"]] * 2))], 2),
        "moe0_router": rows(w["L0_ffn_wg"]),
        "moe0_w": np.concatenate([in_pieces(w["L0_ffn_W1"]), out_pieces(w["L0_ffn_W2"])], 1).reshape(-1, KD * 512),
        "moe0_b1": w["L0_ffn_b1"].reshape(EXPERTS, FT, P).transpose(0, 2, 1).reshape(EXPERTS * P, FT),
        "moe0_b2": np.repeat(w["L0_ffn_b2"], P, axis=0),
        "d_wq": rows(w["L1_attn_Wq"]), "d_wk": rows(w["L1_attn_Wk"]), "d_wv": rows(w["L1_attn_Wv"]),
        "d_wo": rows(w["L1_attn_Wo"]), "d_wb": rows(w["L1_attn_Wb"]),
        "d_taps": np.stack([rows(w["L1_attn_conv_" + n].T) for n in "qkv"], 1),
        "d_rms": w["L1_attn_g_rms"].reshape(P, 1),
        "d_lng": w["L1_attn_ln_g"], "d_lnb": w["L1_attn_ln_b"],
        "moe1_router": rows(w["L1_ffn_router_w"].T),
        "moe1_router_b": w["L1_ffn_router_b"],
        "moe1_w": np.concatenate([gu, out_pieces(dn.transpose(0, 2, 1))], 1).reshape(-1, KD * 512),
    }
    return {name: np.ascontiguousarray(a) for name, a in A.items()}


def kernel(**inputs):
    import numpy as np
    import concourse.bacc as bacc
    from concourse.bass_utils import run_bass_kernel_spmd

    arrays = arrange(np, **{k: np.asarray(v) for k, v in inputs.items()})
    nc = bacc.Bacc("TRN2", target_bir_lowering=False, num_devices=1)
    aps = {name: nc.dram_tensor("in_" + name, a.shape, mybir.dt.from_np(a.dtype), kind="ExternalInput").ap() for name, a in arrays.items()}
    out = nc.dram_tensor("out", (TOK, D), F32, kind="ExternalOutput").ap()
    perceiver(nc, aps, out)
    result = run_bass_kernel_spmd(nc, [{"in_" + name: a for name, a in arrays.items()}], core_ids=[0])
    return result.results[0]["out"].reshape(1, TOK, D)
```

```python
from contextlib import ExitStack, contextmanager

import concourse.bass as bass
from concourse import mybir

F32 = mybir.dt.float32
F32R = mybir.dt.float32r
I32 = mybir.dt.int32
U32 = mybir.dt.uint32
ALU = mybir.AluOpType
ACT = mybir.ActivationFunctionType
X = mybir.AxisListType.X

P = 128
TOK, D = 512, 512
TT, KD = TOK // P, D // P
KEYS = 8192
CHUNK = 512
NCHUNK = KEYS // CHUNK
KT = KEYS // P
HEADS, DH = 16, 32
EPS = 1e-5
INNER, DSTATE, DTRANK = 256, 8, 32
DHEADS = 4
CONV = 4
EXPERTS, FF = 8, 2048
CAPACITY = int(TOK / EXPERTS * 1.25) + 1
FT = FF // P
FB = FF // 512
LEVELS = 7
BY_POOL_0, BY_POOL_1 = (5,), (8, 10)
TILES1 = (2 * TOK + EXPERTS * (P - 1)) // P


class Mark:

    def __init__(self, lane, n):
        self.lane, self.n, self.terms = lane, n, list(lane.terms)


class Lane:

    def __init__(self, nc, ctx, name, unit=1):
        self.sem = ctx.enter_context(nc.semaphore(name))
        self.name, self.unit, self.n, self.terms = name, unit, 0, []

    def did(self, instruction):
        instruction.then_inc(self.sem, self.unit)
        self.n += self.unit
        return Mark(self, self.n)

    def now(self, open_steps=0):
        return Mark(self, self.n - open_steps * self.unit)


def wait(engine, *marks):
    for m in marks:
        value = m.n
        for register, per_turn in m.terms:
            value = register * per_turn + value
        engine.wait_ge(m.lane.sem, value)


class Core:

    def __init__(self, nc, ctx):
        self.nc, self.ctx = nc, ctx
        self.pe, self.act, self.dve, self.pool, self.sp = nc.tensor, nc.scalar, nc.vector, nc.gpsimd, nc.sync
        self.engines = [self.pe, self.act, self.dve, self.pool, self.sp]
        self.mm = Lane(nc, ctx, "pe_steps")
        self.ac = Lane(nc, ctx, "act_steps")
        self.ve = Lane(nc, ctx, "dve_steps")
        self.go = Lane(nc, ctx, "pool_steps")
        self.in_ = [Lane(nc, ctx, f"load_{k}", 16) for k in range(8)]
        self.q_in = [Lane(nc, ctx, f"load_q_{k}", 16) for k in range(2)]
        self.first_q_in = Lane(nc, ctx, "load_q_of_first_pass", 16)
        self.v_in = [Lane(nc, ctx, f"load_v_{k}", 16) for k in range(2)]
        self.out = [Lane(nc, ctx, f"store_{k}", 16) for k in range(8)]
        self.used = Lane(nc, ctx, "pieces_used")
        self.cut = Lane(nc, ctx, "pieces_split")
        self.cut_pool = Lane(nc, ctx, "pieces_split_by_pool")
        self.bias = Lane(nc, ctx, "load_biases", 16)
        self.lanes = [self.mm, self.ac, self.ve, self.go, self.used, self.cut, self.cut_pool, self.bias, self.first_q_in, *self.q_in, *self.v_in, *self.in_, *self.out]
        self.const = {}
        for lane in self.lanes:
            self.sp.sem_inc(lane.sem, 64)
            lane.n = 64
        self.psum = ctx.enter_context(nc.psum_tensor("psum", [P, 8, 512], F32))
        self.bank = [self.psum[:, b, :] for b in range(8)]

    @contextmanager
    def loop(self, turns, steps):
        before = [lane.n for lane in self.lanes]
        with self.nc.Fori(0, turns) as turn:
            for lane, n in steps.items():
                lane.terms.append((turn, n * lane.unit))
            yield turn
            for lane in steps:
                lane.terms.pop()
        for lane, n in zip(self.lanes, before):
            made = steps.get(lane, 0) * lane.unit
            assert lane.n - n == made, (lane.name, (lane.n - n) // lane.unit, steps.get(lane, 0))
            lane.n = n + turns * made

    def barrier(self):
        for engine in self.engines:
            wait(engine, *[lane.now() for lane in self.lanes])
        self.nc.all_engine_barrier()

    def sb(self, stack, name, shape, dtype=F32):
        return stack.enter_context(self.nc.sbuf_tensor(name, shape, dtype))


def load(c, lane, to, source):
    return lane.did(c.sp.dma_start(to, source))


def split(c, high, low, source):
    m = c.ac.did(c.act.copy(high, source))
    wait(c.dve, m)
    return c.ve.did(c.dve.tensor_tensor(low, source, high.bitcast(F32), ALU.subtract))


def product(c, out, lhs, rhs, start, stop):
    c.pe.matmul(out, lhs[0], rhs[0], start=start, stop=False)
    c.pe.matmul(out, lhs[0], rhs[1], start=False, stop=False)
    return c.pe.matmul(out, lhs[1], rhs[0], start=False, stop=stop)


def project_context(c, A, S, x, const):
    with ExitStack() as st:
        raw = c.sb(st, "w_raw", [P, 2, KD, D])
        w = {n: [c.sb(st, f"w{n}_{part}", [P, 2, KD, D], F32R) for part in ("high", "low")] for n in "kv"}
        bk = c.sb(st, "bk", [P, 2, KD])
        bv = c.sb(st, "bv", [P, 2, D])
        cx = c.sb(st, "cx", [P, KD, CHUNK])
        cparts = c.sb(st, "cparts", [P, 2, 2, KD, CHUNK], F32R)
        kparts = c.sb(st, "kparts", [P, 4, 2, CHUNK], F32R)
        vrow = c.sb(st, "vrow", [P, 2, HEADS, CHUNK // P, DH])
        per_chunk = 2 * 4 + 2 * 4

        def load_chunk(n, u):
            wait(c.sp, c.go.now())
            load(c, c.in_[4 + u], cx[:], A["ctx"][bass.ds(n * P, P), :].rearrange("p (k n) -> p k n", k=KD))

        def split_chunk(u):
            wait(c.act, c.in_[4 + u].now(), c.mm.now(per_chunk))
            m = c.ac.did(c.act.copy(cparts[:, u, 0], cx[:]))
            wait(c.pool, m)
            c.go.did(c.pool.tensor_tensor(cparts[:, u, 1], cx[:], cparts[:, u, 0].bitcast(F32), ALU.subtract))

        load_chunk(0, 0)
        weights_split = {}
        for i, (n, l) in enumerate((("k", 0), ("v", 0), ("k", 1), ("v", 1))):
            wait(c.sp, c.ve.now(1))
            m = load(c, c.in_[i], raw[:, i % 2], A["w" + n][l])
            wait(c.act, m)
            wait(c.dve, m)
            weights_split[n, l] = split(c, w[n][0][:, l], w[n][1][:, l], raw[:, i % 2])
            if i == 0:
                split_chunk(0)
            if i == 1:
                for layer in range(2):
                    load(c, c.bias, bk[:, layer], A["bk"][layer])
                    biases_in = load(c, c.bias, bv[:, layer], A["bv"][layer].partition_broadcast(P))
        load(c, c.in_[6], const[:], A["constants"])
        load(c, c.in_[6], x[:], A["x"].rearrange("(t p) d -> p t d", p=P))
        wait(c.act, biases_in)
        wait(c.dve, biases_in)
        def chunk(n, u, has_next=True):
            wait(c.pe, c.go.now())
            for l in range(2):
                wait(c.pe, weights_split["k", l])
                for b in range(KD):
                    bank = c.bank[b]
                    wait(c.pe, c.ve.now(7))
                    for k in range(KD):
                        last = product(c, bank, [x[:, l, k, b * P:(b + 1) * P] for x in w["k"]], [cparts[:, u, x, k, :] for x in range(2)], k == 0, k == KD - 1)
                    made = c.mm.did(last)
                    wait(c.act, made, c.out[b].now())
                    high = c.ac.did(c.act.activation(kparts[:, b, 0, :], bank, ACT.Identity, bias=bk[:, l, b:b + 1]))
                    wait(c.dve, high)
                    low = c.ve.did(c.dve.scalar_tensor_tensor(kparts[:, b, 1, :], bank, bk[:, l, b:b + 1], kparts[:, b, 0, :].bitcast(F32), ALU.add, ALU.subtract))
                    wait(c.act, low)
                    for part in range(2):
                        c.out[b].did(c.act.dma_start(S["k"][l, part, b * P:(b + 1) * P, bass.ds(n * CHUNK, CHUNK)], kparts[:, b, part, :].bitcast(F32)))
                if l == 1 and has_next:
                    load_chunk(n + 1, 1 - u)
                wait(c.dve, c.out[4 + l].now())
                wait(c.pe, weights_split["v", l])
                for t in range(CHUNK // P):
                    bank = c.bank[4 + t]
                    wait(c.pe, c.ve.now(7))
                    for k in range(KD):
                        last = product(c, bank, [cparts[:, u, x, k, t * P:(t + 1) * P] for x in range(2)], [x[:, l, k, :] for x in w["v"]], k == 0, k == KD - 1)
                    made = c.mm.did(last)
                    wait(c.dve, made)
                    c.ve.did(c.dve.tensor_tensor(vrow[:, l, :, t, :], bank.rearrange("p (h d) -> p h d", h=HEADS), bv[:, l, :].rearrange("p (h d) -> p h d", h=HEADS), ALU.add))
                wait(c.sp, c.ve.now())
                c.out[4 + l].did(c.sp.dma_start(
                    S["v"][l].rearrange("h p t d -> p h (t d)")[:, :, bass.ds(n * (CHUNK // P) * DH, CHUNK // P * DH)],
                    vrow[:, l].rearrange("p h t d -> p h (t d)")))
            if has_next:
                split_chunk(1 - u)

        steps = {c.mm: 2 * per_chunk, c.ac: 2 * 9, c.ve: 2 * per_chunk, c.go: 2, c.in_[4]: 1, c.in_[5]: 1,
                 **{c.out[s]: 2 * 2 * 2 for s in range(4)}, c.out[4]: 2, c.out[5]: 2}
        with c.loop(NCHUNK // 2 - 1, steps) as turn:
            for u in range(2):
                chunk(turn * 2 + u, u)
        chunk(NCHUNK - 2, 0)
        chunk(NCHUNK - 1, 1, has_next=False)
        c.barrier()


def normalize(c, st, x, name):
    xn = c.sb(st, name + "_rows", [P, TT, D])
    xt = c.sb(st, name + "_cols", [P, KD, TOK])
    stats = c.sb(st, name + "_stats", [P, TT, 6])
    mv = c.sb(st, name + "_mv", [P, TT, 2])
    std = c.sb(st, name + "_std", [P, TT, 2])
    for t in range(TT):
        m = c.ve.did(c.dve.bn_stats(stats[:, t, :], x[:, t, :]))
    wait(c.dve, m)
    for t in range(TT):
        m = c.ve.did(c.dve.bn_aggr(mv[:, t, :], stats[:, t, :]))
    wait(c.dve, m)
    m = c.ve.did(c.dve.tensor_scalar(std[:, :, 0], mv[:, :, 1], EPS, None, ALU.add))
    wait(c.act, m)
    m = c.ac.did(c.act.activation(std[:, :, 1], std[:, :, 0], ACT.Sqrt))
    wait(c.dve, m)
    m = c.ve.did(c.dve.reciprocal(std[:, :, 0], std[:, :, 1]))
    wait(c.dve, m)
    for t in range(TT):
        m = c.ve.did(c.dve.tensor_scalar(xn[:, t, :], x[:, t, :], mv[:, t, 0:1], std[:, t, 0:1], ALU.subtract, ALU.mult))
    wait(c.pe, m)
    to_columns(c, xt, xn)
    return xn, xt


def to_columns(c, xt, xn):
    for k in range(KD):
        for t in range(TT):
            last = c.pe.transpose(c.bank[k][:, t * P:(t + 1) * P], xn[:, t, k * P:(k + 1) * P], c.ident[:])
        m = c.mm.did(last)
        wait(c.act, m)
        c.ac.did(c.act.copy(xt[:, k, :], c.bank[k][:]))


def linear_t(c, bank, w, xt, b, kd=KD):
    for k in range(kd):
        last = c.pe.matmul(bank, w[:, k, b * P:(b + 1) * P], xt[:, k, :], start=k == 0, stop=k == kd - 1)
    return c.mm.did(last)


def add_rows(c, x, at, w, bias=None, kd=KD):
    for t in range(TT):
        for k in range(kd):
            last = c.pe.matmul(c.bank[t][:], at[:, k, t * P:(t + 1) * P], w[:, k, :], start=k == 0, stop=k == kd - 1)
        m = c.mm.did(last)
        wait(c.dve, m)
        m = c.ve.did(c.dve.tensor_tensor(x[:, t, :], c.bank[t][:], x[:, t, :], ALU.add))
        if bias is not None:
            wait(c.dve, m)
            c.ve.did(c.dve.tensor_tensor(x[:, t, :], x[:, t, :], bias, ALU.add))


def cross_attention(c, A, S, x, l):
    with ExitStack() as st:
        KROWS = 3 * DH + 1
        QUADS, PARTS = KT // 4, 4
        RING = 16
        POOL_QUADS = [q for q in range(QUADS - 3) if q % 3]
        PART = KEYS // PARTS
        ks = [c.sb(st, f"ks{l}_{s}", [KROWS, KEYS], F32R) for s in range(2)]
        vs = [c.sb(st, f"vs{l}_{s}", [P, KT, DH]) for s in range(2)]

        def load_k(h, s, part):
            for at, which in ((0, 0), (1, 1), (2, 0)):
                c.in_[4 * s + part].did(c.sp.dma_start(ks[s][at * DH:(at + 1) * DH, part * PART:(part + 1) * PART].bitcast(F32),
                                                       S["k"][l, which, bass.ds(h * DH, DH), part * PART:(part + 1) * PART]))

        def load_v(h, s):
            c.v_in[s].did(c.sp.dma_start(vs[s][:], S["v"][l].rearrange("h p t d -> (h p) (t d)")[bass.ds(h * P, P), :].rearrange("p (t d) -> p t d", d=DH)))

        with ExitStack() as st2:
            wq = c.sb(st2, f"wq{l}", [P, KD, D])
            bq = c.sb(st2, f"bq{l}", [P, KD])
            qf = c.sb(st2, f"qf{l}", [P, KD, TOK])
            qparts = c.sb(st2, f"qparts{l}", [P, KD, 2, TOK], F32R)
            load(c, c.q_in[0], wq[:], A["wq"][l])
            w_in = load(c, c.q_in[0], bq[:], A["bq"][l])
            for s in range(2):
                for part in range(PARTS):
                    load_k(s, s, part)
            load_v(0, 0)
            xn, xt = normalize(c, st2, x, f"ln_a{l}")
            wait(c.pe, c.ac.now(), w_in)
            wait(c.dve, w_in)
            for b in range(KD):
                m = linear_t(c, c.bank[b][:], wq, xt, b)
                wait(c.dve, m)
                m = c.ve.did(c.dve.tensor_scalar(qf[:, b, :], c.bank[b][:], bq[:, b:b + 1], DH ** -0.5, ALU.add, ALU.mult))
                wait(c.dve, m)
                m = c.ve.did(c.dve.tensor_copy(qparts[:, b, 0, :], qf[:, b, :]))
                wait(c.dve, m)
                m = c.ve.did(c.dve.tensor_tensor(qparts[:, b, 1, :], qf[:, b, :], qparts[:, b, 0, :].bitcast(F32), ALU.subtract))
                wait(c.sp, m)
                for part in range(2):
                    c.out[7].did(c.sp.dma_start(S["q"][l, part, b * P:(b + 1) * P, :], qparts[:, b, part, :].bitcast(F32)))
            c.barrier()
        qs = [c.sb(st, f"qs{l}_{s}", [KROWS, TOK], F32R) for s in range(2)]
        first_q = c.sb(st, f"first_q{l}", [3 * DH, TOK], F32R)
        pt = c.sb(st, f"pt{l}", [P, RING, TOK])
        pool_sum = c.sb(st, f"pool_sum{l}", [P, TOK])
        run_max = c.sb(st, f"run_max{l}", [P, 2, TOK])
        col_max = c.sb(st, f"col_max{l}", [P, TT])
        partial = c.sb(st, f"partial{l}", [P, 2, TOK])
        total = c.sb(st, f"total{l}", [P, TT])
        rows = c.sb(st, f"head_rows{l}", [P, TT, D])
        wo = c.sb(st, f"wo{l}", [P, KD, D])
        bo = c.sb(st, f"bo{l}", [P, D])
        at = c.sb(st, f"heads{l}", [P, KD, TOK])
        P1_BANK, OUT_BANK, SUM_BANK = 3, 6, 7
        for s in range(2):
            c.ac.did(c.act.copy(ks[s][3 * DH:KROWS, :], c.ones[3 * DH:KROWS, 0:1].to_broadcast([1, KEYS])))

        def load_q(h, lane, to):
            for at, which in ((0, 0), (1, 0), (2, 1)):
                lane.did(c.sp.dma_start(to[at * DH:(at + 1) * DH, :].bitcast(F32), S["q"][l, which, bass.ds(h * DH, DH), :]))

        def load_first_q(h):
            wait(c.sp, c.mm.now())
            load_q(h, c.first_q_in, first_q)

        def first_pass(s, t, read):
            bank = c.bank[P1_BANK + (t + 1) % 3]
            if t % (KT // PARTS) == 0:
                wait(c.pe, c.in_[4 * s + t // (KT // PARTS)].now())
            wait(c.pe, read[-3])
            m = c.mm.did(c.pe.matmul(bank[:], ks[s][0:3 * DH, t * P:(t + 1) * P], first_q[:], start=True, stop=True))
            wait(c.dve, m, read[-2])
            if t > 1:
                op = c.dve.tensor_tensor(run_max[:, t % 2, :], bank[:], run_max[:, t % 2, :], ALU.max)
            else:
                op = c.dve.tensor_copy(run_max[:, t % 2, :], bank[:])
            read.append(c.ve.did(op))

        def merge_maxima():
            wait(c.dve, c.ve.now())
            return c.ve.did(c.dve.tensor_tensor(run_max[:, 0, :], run_max[:, 0, :], run_max[:, 1, :], ALU.max))

        def shift_columns(merged):
            wait(c.pe, merged)
            for t in range(TT):
                last = c.pe.transpose(c.bank[P1_BANK][:, t * P:(t + 1) * P], run_max[:, 0, t * P:(t + 1) * P], c.ident[:])
            m = c.mm.did(last)
            wait(c.dve, m)
            return c.ve.did(c.dve.tensor_reduce(col_max[:], c.bank[P1_BANK][:].rearrange("p (t n) -> p t n", t=TT), X, ALU.max))

        def shift_row(s, columns):
            wait(c.pe, columns)
            for t in range(TT):
                last = c.pe.matmul(c.bank[P1_BANK + 1][3 * DH:KROWS, t * P:(t + 1) * P], col_max[:, t:t + 1], c.ident[:], start=True, stop=True)
            m = c.mm.did(last)
            wait(c.dve, m)
            return c.ve.did(c.dve.tensor_scalar(qs[s][3 * DH:KROWS, :], c.bank[P1_BANK + 1][3 * DH:KROWS, :], -1.0, None, ALU.mult))

        def second_pass(s, t, exps, summed, banks):
            wait(c.pe, exps[-banks])
            bank = c.bank[(t + s) % 3 if banks == 3 else t % banks]
            m = c.mm.did(c.pe.matmul(bank[:], ks[s][:, t * P:(t + 1) * P], qs[s][:], start=True, stop=True))
            wait(c.act, m)
            if t - RING in summed:
                wait(c.act, summed[t - RING])
            exps.append(c.ac.did(c.act.activation(pt[:, t % RING, :], bank[:], ACT.Exp)))

        def pool_quad(quad, exp_done, summed):
            wait(c.pool, exp_done)
            tiles = [4 * quad + j for j in range(4)]
            if quad == POOL_QUADS[0]:
                wait(c.pool, c.mm.now())
                t = tiles.pop(0)
                m = c.go.did(c.pool.tensor_tensor(pool_sum[:], pt[:, t % RING, :], pt[:, (t + 1) % RING, :], ALU.add))
                summed[t] = summed[tiles.pop(0)] = m
            for t in tiles:
                wait(c.pool, c.go.now())
                summed[t] = c.go.did(c.pool.tensor_tensor(pool_sum[:], pool_sum[:], pt[:, t % RING, :], ALU.add))

        def weigh(s, quad, exp_done, is_v):
            wait(c.pe, exp_done)
            bank = c.bank[OUT_BANK if is_v else SUM_BANK]
            for j in range(4):
                t = 4 * quad + j
                lhs = vs[s][:, t, :] if is_v else c.ones[:, 0:DH]
                last = c.pe.matmul(bank[j * DH:(j + 1) * DH, :], lhs, pt[:, t % RING, :], start=quad == 0, stop=quad == QUADS - 1)
            return c.mm.did(last)

        def weigh_last(s, exp_done):
            weigh(s, QUADS - 1, exp_done, True)
            wait(c.pe, c.go.now())
            c.pe.matmul(c.bank[SUM_BANK][0:DH, :], c.ones[:, 0:DH], pool_sum[:], start=False, stop=False)
            return weigh(s, QUADS - 1, exp_done, False)

        def take_partials(weighed):
            wait(c.dve, weighed)
            c.ve.did(c.dve.tensor_copy(partial[:, 0, :], c.bank[OUT_BANK][:]))
            return c.ve.did(c.dve.tensor_copy(partial[:, 1, :], c.bank[SUM_BANK][:]))

        def finish_head(h, taken):
            wait(c.pe, taken)
            out, sums = c.bank[SUM_BANK][:, 0:TT * DH], c.bank[SUM_BANK][:, TT * DH:TT * DH + TT]
            for t in range(TT):
                c.pe.matmul(out[:, t * DH:(t + 1) * DH], partial[:, 0, t * P:(t + 1) * P], c.fold[:], start=True, stop=True)
                last = c.pe.matmul(sums[:, t:t + 1], partial[:, 1, t * P:(t + 1) * P], c.fold[:, 0:1], start=True, stop=True)
            m = c.mm.did(last)
            wait(c.dve, m)
            m = c.ve.did(c.dve.reciprocal(total[:], sums))
            wait(c.dve, m)
            return c.ve.did(c.dve.tensor_tensor(rows[:, :, bass.ds(h * DH, DH)], out.rearrange("p (t d) -> p t d", t=TT),
                                                total[:, :, None].to_broadcast([P, TT, DH]), ALU.mult))

        def head(h, s, has_previous=True, has_next=True, loads=True):
            n = 1 - s
            banks = 3 if has_next else 6
            pool_quads = POOL_QUADS if has_next else POOL_QUADS[:1]
            exps = [c.ac.now(1), c.ac.now(), c.ac.now()] if has_next else banks * [c.ac.now()]
            last_exp = exps[-1]
            last_pool = [t - KT for q in POOL_QUADS for t in range(4 * q, 4 * q + 4)][1:]
            summed = {t: c.go.now(len(last_pool) - 1 - i) for i, t in enumerate(last_pool)}
            read, columns = 3 * [c.ve.now()], None
            tiles = list(range(KT)) if has_next else []
            wait(c.pe, c.ve.now(), c.v_in[s].now(), c.q_in[s].now())

            def next_tiles(count):
                for _ in range(min(count, len(tiles))):
                    first_pass(n, tiles.pop(0), read)

            for quad in range(QUADS):
                weighs = exps[-1]
                by_pool = quad - 1 in pool_quads
                second_pass(s, 4 * quad, exps, summed, banks)
                if quad == 0:
                    for t in range(1, 4):
                        second_pass(s, t, exps, summed, banks)
                        if t == 2 and has_next:
                            wait(c.pe, c.first_q_in.now())
                        if t > 1:
                            next_tiles(1)
                    if has_previous:
                        taken = take_partials(weigh_last(n, last_exp))
                    if has_next:
                        wait(c.sp, c.mm.now())
                        load_v(h + 1, n)
                        load_q(h + 1, c.q_in[n], qs[n])
                    continue
                if quad > 1:
                    next_tiles(1)
                second_pass(s, 4 * quad + 1, exps, summed, banks)
                if quad > 1:
                    next_tiles(1)
                    weigh(s, quad - 1, weighs, True)
                    next_tiles(0 if by_pool else 1)
                second_pass(s, 4 * quad + 2, exps, summed, banks)
                if quad > 1:
                    next_tiles(1)
                second_pass(s, 4 * quad + 3, exps, summed, banks)
                if loads and (quad + 1) % (QUADS // PARTS) == 0:
                    wait(c.sp, c.mm.now())
                    load_k(h + 2, s, quad // (QUADS // PARTS))
                if quad == 1:
                    if has_previous:
                        wait(c.pe, taken)
                    weigh(s, 0, weighs, True)
                    if has_previous:
                        finished = finish_head(h - 1, taken)
                    next_tiles(3)
                    if has_previous:
                        wait(c.pe, finished)
                    assert 0 not in POOL_QUADS
                    weigh(s, 0, weighs, False)
                    continue
                next_tiles(1)
                if quad == QUADS - 1 and has_next:
                    shift_row(n, columns)
                if by_pool:
                    pool_quad(quad - 1, weighs, summed)
                else:
                    weigh(s, quad - 1, weighs, False)
                    next_tiles(1)
                if quad == QUADS - 2 and has_next:
                    columns = shift_columns(merged)
                if quad == QUADS - 3 and has_next:
                    next_tiles(KT)
                    merged = merge_maxima()
                    if loads:
                        load_first_q(h + 2)

        load_q(0, c.first_q_in, first_q)
        load_q(0, c.q_in[0], qs[0])
        load(c, c.bias, wo[:], A["wo"][l])
        load(c, c.bias, bo[:], A["bo"][l].partition_broadcast(P))
        read = 3 * [c.ve.now()]
        wait(c.pe, c.first_q_in.now(), c.ve.now())
        for t in range(KT):
            first_pass(0, t, read)
        load_first_q(1)
        shift_row(0, shift_columns(merge_maxima()))
        wait(c.pe, c.ac.now())
        head(0, 0, has_previous=False)
        steps = {c.mm: 2 * (KT + KT + 2 * QUADS - len(POOL_QUADS) + 1 + 2), c.ac: 2 * KT, c.ve: 2 * (2 + 2 + KT + 2 + 1), c.go: 2 * (4 * len(POOL_QUADS) - 1),
                 c.v_in[0]: 1, c.v_in[1]: 1, c.q_in[0]: 3, c.q_in[1]: 3, c.first_q_in: 6, **{lane: 3 for lane in c.in_}}
        PEELED = 4
        with c.loop((HEADS - PEELED) // 2, steps) as turn:
            for u in range(2):
                head(turn * 2 + 1 + u, 1 - u)
        head(HEADS - 3, 1)
        head(HEADS - 2, 0, loads=False)
        head(HEADS - 1, 1, has_next=False, loads=False)
        finish_head(HEADS - 1, take_partials(weigh_last(1, c.ac.now())))
        wait(c.pe, c.ve.now(), c.bias.now())
        wait(c.dve, c.bias.now())
        to_columns(c, at, rows)
        wait(c.pe, c.ac.now())
        add_rows(c, x, at, wo, bo[:])
        c.barrier()


def softplus(c, out, v, tmp):
    m = c.ve.did(c.dve.scalar_tensor_tensor(tmp, v, -1.0, v, ALU.mult, ALU.max))
    wait(c.act, m)
    m = c.ac.did(c.act.activation(tmp, tmp, ACT.Exp, scale=-1.0))
    wait(c.act, m)
    m = c.ac.did(c.act.activation(tmp, tmp, ACT.Ln, bias=1.0))
    wait(c.dve, m)
    return c.ve.did(c.dve.scalar_tensor_tensor(out, v, 0.0, tmp, ALU.max, ALU.add))


def selective_scan(c, A, x):
    CB, TAPS, RING = INNER // P, 3, 3
    with ExitStack() as st:
        w_in = c.sb(st, "w_in", [P, KD, D])
        w_out = c.sb(st, "w_out", [P, KD, D])
        w_x = c.sb(st, "w_x", [P, CB, DTRANK + 2 * DSTATE])
        w_dt = c.sb(st, "w_dt", [DTRANK, INNER])
        chan = c.sb(st, "chan", [P, KD, TAPS + 2 + DSTATE])
        padded = c.sb(st, "padded", [P, KD, TOK + 2])
        summed = c.sb(st, "conv_sum", [P, KD, TOK])
        conv = c.sb(st, "conv", [P, KD, TOK])
        dt_raw = c.sb(st, "dt_raw", [DTRANK, TOK])
        bc = c.sb(st, "bc", [DSTATE, 2, TOK])
        both = c.sb(st, "softplus_in", [P, CB * (TOK + DSTATE)])
        soft = c.sb(st, "softplus_out", [P, CB * (TOK + DSTATE)])
        soft_tmp = c.sb(st, "softplus_tmp", [P, CB * (TOK + DSTATE)])
        terms = c.sb(st, "bc_terms", [P, 2, DSTATE, TOK])
        decay = c.sb(st, "decay", [P, RING, TOK])
        rest = c.sb(st, "one_minus_decay", [P, RING, TOK])
        drive = c.sb(st, "drive", [P, RING, TOK])
        state = c.sb(st, "state", [P, RING, TOK])
        part = c.sb(st, "state_part", [P, RING, TOK])
        delta = [soft[:, b * TOK:(b + 1) * TOK] for b in range(CB)]
        rate = soft[:, CB * TOK:].rearrange("p (b s) -> p b s", b=CB)
        load(c, c.in_[0], chan[:], A["chan"])
        chan_in = load(c, c.in_[0], w_x[:], A["w_xproj"])
        w_in_in = load(c, c.in_[1], w_in[:], A["w_in"])
        w_dt_in = load(c, c.in_[2], w_dt[:], A["w_dt"])
        w_out_in = load(c, c.in_[3], w_out[:], A["w_out"])
        for b in range(KD):
            for edge in (0, TOK + 1):
                c.ve.did(c.dve.memset(padded[:, b, edge:edge + 1], 0.0))
        _, xt = normalize(c, st, x, "ln_s")
        wait(c.pe, w_in_in, c.ac.now())
        wait(c.dve, chan_in)
        convolved, silued = {}, {}
        for b in range(KD):
            wait(c.act, linear_t(c, c.bank[b][:], w_in, xt, b))
            copied = c.ac.did(c.act.copy(padded[:, b, 1:TOK + 1], c.bank[b][:]))
            wait(c.dve, copied)
            m = c.ve.did(c.dve.tensor_scalar(summed[:, b, :], padded[:, b, 0:TOK], chan[:, b, 0:1], None, ALU.mult))
            for j in range(1, TAPS):
                wait(c.dve, m)
                m = c.ve.did(c.dve.scalar_tensor_tensor(summed[:, b, :], padded[:, b, j:j + TOK], chan[:, b, j:j + 1], summed[:, b, :], ALU.mult, ALU.add))
            convolved[b] = m
            if b:
                wait(c.act, convolved[b - 1])
                silued[b - 1] = c.ac.did(c.act.activation(conv[:, b - 1, :], summed[:, b - 1, :], ACT.Silu))
        wait(c.pe, silued[CB - 1], chan_in)
        wait(c.act, convolved[KD - 1])
        for bank, lo, n in ((4, 0, DTRANK), (5, DTRANK, DSTATE), (6, DTRANK + DSTATE, DSTATE)):
            for k in range(CB):
                last = c.pe.matmul(c.bank[bank][0:n, :], w_x[:, k, lo:lo + n], conv[:, k, :], start=k == 0, stop=k == CB - 1)
            m = c.mm.did(last)
            if bank == 4:
                dt_made = m
        silued[KD - 1] = c.ac.did(c.act.activation(conv[:, KD - 1, :], summed[:, KD - 1, :], ACT.Silu))
        wait(c.act, dt_made)
        dt_done = c.ac.did(c.act.copy(dt_raw[:], c.bank[4][0:DTRANK, :]))
        wait(c.act, m)
        for which in range(2):
            bc_done = c.ac.did(c.act.activation(bc[:, which, :], c.bank[5 + which][0:DSTATE, :], ACT.Tanh))
        wait(c.pe, dt_done, w_dt_in)
        for b in range(CB):
            m = c.mm.did(c.pe.matmul(c.bank[b][:], w_dt[:, b * P:(b + 1) * P], dt_raw[:], start=True, stop=True))
            wait(c.dve, m)
            c.ve.did(c.dve.tensor_scalar(both[:, b * TOK:(b + 1) * TOK], c.bank[b][:], chan[:, b, 3:4], None, ALU.add))
            c.ve.did(c.dve.tensor_copy(both[:, CB * TOK + b * DSTATE:CB * TOK + (b + 1) * DSTATE], chan[:, b, 5:5 + DSTATE]))
        wait(c.dve, c.ve.now())
        m = softplus(c, soft[:], both[:], soft_tmp[:])
        wait(c.dve, m)
        for b in range(CB):
            c.ve.did(c.dve.tensor_scalar(delta[b], delta[b], 1e-4, 1.0, ALU.max, ALU.min))
        rates_done = c.ve.did(c.dve.tensor_scalar(rate, rate, -1.0, -1e-4, ALU.mult, ALU.add))
        wait(c.pe, bc_done, w_out_in)

        def output_part(t, blocks):
            for k in blocks:
                last = c.pe.matmul(c.bank[4 + t][:], conv[:, k, t * P:(t + 1) * P], w_out[:, k, :], start=k == CB, stop=k == CB - 1)
            return c.mm.did(last)

        spread = {}
        decayed, driven, scanned, weighed, added = {}, {}, {}, {}, {}
        steps = [(s, b) for s in range(DSTATE) for b in range(CB)]

        def spread_terms(s):
            for which in range(2):
                wait(c.pe, spread[s - 1, which] if s else rates_done)
                m = c.mm.did(c.pe.matmul(c.bank[which][:], c.pick[0:DSTATE, s * P:(s + 1) * P], bc[:, which, :], start=True, stop=True))
                wait(c.act, m)
                spread[s, which] = c.ac.did(c.act.copy(terms[:, which, s, :], c.bank[which][:]))

        def start_step(i):
            s, b = steps[i]
            r = i % RING
            if i >= RING:
                wait(c.act, scanned[i - RING])
                wait(c.pool, scanned[i - RING])
            decayed[i] = c.ac.did(c.act.activation(decay[:, r, :], delta[b], ACT.Exp, scale=rate[:, b, s:s + 1]))
            wait(c.pool, spread[s, 0])
            driven[i] = c.go.did(c.pool.tensor_tensor(drive[:, r, :], terms[:, 0, s, :], conv[:, b, :], ALU.mult))

        def scan_step(i):
            s, b = steps[i]
            r = i % RING
            wait(c.dve, decayed[i])
            m = c.ve.did(c.dve.tensor_scalar(decay[:, r, :], decay[:, r, :], 1e-4, 1.0, ALU.max, ALU.min))
            wait(c.dve, m)
            m = c.ve.did(c.dve.tensor_scalar(rest[:, r, :], decay[:, r, :], -1.0, 1.0, ALU.mult, ALU.add))
            wait(c.dve, m, driven[i])
            m = c.ve.did(c.dve.tensor_tensor(drive[:, r, :], rest[:, r, :], drive[:, r, :], ALU.mult))
            wait(c.dve, m)
            if i >= RING:
                wait(c.dve, weighed[i - RING])
            scanned[i] = c.ve.did(c.dve.tensor_tensor_scan(state[:, r, :], decay[:, r, :], drive[:, r, :], 0.0, ALU.mult, ALU.add))

        def weigh_step(i):
            s, b = steps[i]
            r = i % RING
            wait(c.pool, scanned[i], spread[s, 1])
            if i >= RING:
                wait(c.pool, added[i - RING])
            weighed[i] = c.go.did(c.pool.tensor_tensor(part[:, r, :], state[:, r, :], terms[:, 1, s, :], ALU.mult))
            wait(c.pe, weighed[i])
            added[i] = c.mm.did(c.pe.matmul(c.bank[2 + b][:], c.ident[:], part[:, r, :], start=s == 0, stop=s == DSTATE - 1))

        spread_terms(0)
        wait(c.act, rates_done)
        wait(c.pool, silued[KD - 1])
        start_step(0)
        spread_terms(1)
        wait(c.pe, silued[KD - 1])
        for t in range(TT):
            output_part(t, range(CB, KD))
        for i in range(len(steps)):
            if i + 1 < len(steps):
                start_step(i + 1)
            if i % CB == 0 and i // CB + 2 < DSTATE:
                spread_terms(i // CB + 2)
            scan_step(i)
            if i:
                weigh_step(i - 1)
        weigh_step(len(steps) - 1)
        for b in range(CB):
            wait(c.dve, added[len(steps) - CB + b])
            m = c.ve.did(c.dve.scalar_tensor_tensor(conv[:, b, :], conv[:, b, :], chan[:, b, 4:5], c.bank[2 + b][:], ALU.mult, ALU.add))
        wait(c.pe, m)
        for t in range(TT):
            wait(c.dve, output_part(t, range(CB)))
            c.ve.did(c.dve.tensor_tensor(x[:, t, :], c.bank[4 + t][:], x[:, t, :], ALU.add))
        c.barrier()


def route(c, st, A, xt, l, wr, br):
    n = f"route{l}_"
    logits = c.sb(st, n + "logits", [P, TT, EXPERTS])
    best = c.sb(st, n + "best", [P, TT, 8])
    index = c.sb(st, n + "index", [P, TT, 8], U32)
    indexf = c.sb(st, n + "indexf", [P, TT, 8])
    hot = c.sb(st, n + "hot", [P, TT, 2, EXPERTS])
    for t in range(TT):
        for k in range(KD):
            last = c.pe.matmul(c.bank[4][:, t * EXPERTS:(t + 1) * EXPERTS], xt[:, k, t * P:(t + 1) * P], wr[:, k, :], start=k == 0, stop=k == KD - 1)
    m = c.mm.did(last)
    wait(c.dve, m)
    m = c.ve.did(c.dve.tensor_tensor(logits[:], c.bank[4][:, 0:TT * EXPERTS].rearrange("p (t e) -> p t e", t=TT), br, ALU.add))
    wait(c.dve, m)
    for t in range(TT):
        m = c.ve.did(c.dve.max(best[:, t, :], logits[:, t, :]))
    wait(c.dve, m)
    for t in range(TT):
        m = c.ve.did(c.dve.max_index(index[:, t, :], best[:, t, :], logits[:, t, :]))
    wait(c.dve, m)
    m = c.ve.did(c.dve.tensor_copy(indexf[:], index[:]))
    wait(c.dve, m)
    for t in range(TT):
        for j in range(2):
            m = c.ve.did(c.dve.tensor_scalar(hot[:, t, j, :], c.iota[:, 0:EXPERTS], indexf[:, t, j:j + 1], None, ALU.is_equal))
    wait(c.dve, m)
    return logits, best, hot


def ranks(c, st, l, chosen):
    rank = c.sb(st, f"rank{l}", [P, TT, EXPERTS])
    count = c.sb(st, f"count{l}", [P, EXPERTS])
    wait(c.pe, c.ve.now())
    for t in range(TT):
        for s in range(t + 1):
            last = c.pe.matmul(c.bank[5][:, t * EXPERTS:(t + 1) * EXPERTS], c.upto[:] if s == t else c.ones[:], chosen[:, s, :], start=s == 0, stop=s == t)
    for s in range(TT):
        last = c.pe.matmul(c.bank[6][:, 0:EXPERTS], c.ones[:], chosen[:, s, :], start=s == 0, stop=s == TT - 1)
    m = c.mm.did(last)
    wait(c.dve, m)
    c.ve.did(c.dve.tensor_copy(count[:], c.bank[6][:, 0:EXPERTS]))
    m = c.ve.did(c.dve.tensor_copy(rank[:], c.bank[5][:, 0:TT * EXPERTS].rearrange("p (t e) -> p t e", t=TT)))
    wait(c.dve, m)
    return rank, count


def expert_tiles(c, st, A, x, xn, pos, gate, l, tiles, expert_of):
    n = f"moe{l}_"
    two = l == 1
    pieces = (3 if two else 2) * FB
    RAW, CUT = (6, 4) if two else (4, 4)
    AHEAD = 3
    OUT_BANK = 2
    JB = FT // FB
    BY_POOL = BY_POOL_1 if two else BY_POOL_0
    raw = c.sb(st, n + "raw", [P, RAW, KD, 512])
    cut = c.sb(st, n + "cut", [P, CUT, 2, KD, 512], F32R)
    xparts = c.sb(st, n + "xparts", [P, 2, TT, D], F32R)
    sel = c.sb(st, n + "sel", [P, TT, P], F32R)
    selw = c.sb(st, n + "selw", [P, TT, P])
    sel2 = c.sb(st, n + "sel2", [P, TT, P])
    selwt = c.sb(st, n + "selwt", [P, TOK])
    slots = c.sb(st, n + "slots", [P, P])
    xg = c.sb(st, n + "xg", [P, 2, KD, P], F32R)
    h = c.sb(st, n + "h", [P, FF])
    ht = c.sb(st, n + "ht", [P, 2, FT, P], F32R)
    yrow = c.sb(st, n + "yrow", [P, D])
    if not two:
        bias1 = c.sb(st, n + "bias1", [P, FT])
        bias2 = c.sb(st, n + "bias2", [P, D])
        act_out = c.sb(st, n + "act_out", [P, 2, JB, P])
    split(c, xparts[:, 0], xparts[:, 1], xn[:])
    c.ve.did(c.dve.tensor_copy(slots[:], c.iota[:]))
    c.ve.did(c.dve.memset(selwt[:], 0.0))
    c.ve.did(c.dve.memset(yrow[:], 0.0))
    wait(c.dve, c.ve.now())

    def split_piece(w):
        turn_loads = pieces // RAW
        wait(c.act, c.in_[w % RAW].now(turn_loads - (w // RAW + 1)), c.used.now(CUT - AHEAD - 1))
        m = c.ac.did(c.act.copy(cut[:, w % CUT, 0], raw[:, w % RAW]))
        engine, lane = (c.pool, c.cut_pool) if w % pieces in BY_POOL else (c.dve, c.cut)
        wait(engine, m)
        lane.did(engine.tensor_tensor(cut[:, w % CUT, 1], raw[:, w % RAW], cut[:, w % CUT, 0].bitcast(F32), ALU.subtract))

    def is_split(w, start):
        by_pool = w % pieces in BY_POOL
        same = lambda v: (v % pieces in BY_POOL) == by_pool
        ahead = sum(same(v) for v in range(AHEAD, w + 1)) - sum(same(v) for v in range(w + 1, AHEAD))
        lane = c.cut_pool if by_pool else c.cut
        return Mark(lane, start[by_pool] + ahead * lane.unit)

    def select(t):
        m = c.ve.did(c.dve.tensor_scalar(sel[:, t, :], slots[:], pos[0][:, t:t + 1], None, ALU.is_equal))
        m2 = c.ve.did(c.dve.tensor_scalar(selw[:, t, :], slots[:], pos[0][:, t:t + 1], gate[0][:, t:t + 1], ALU.is_equal, ALU.mult))
        if two:
            m3 = c.ve.did(c.dve.tensor_scalar(sel2[:, t, :], slots[:], pos[1][:, t:t + 1], gate[1][:, t:t + 1], ALU.is_equal, ALU.mult))
            wait(c.dve, m)
            c.ve.did(c.dve.scalar_tensor_tensor(sel[:, t, :], slots[:], pos[1][:, t:t + 1], sel[:, t, :].bitcast(F32), ALU.is_equal, ALU.add))
            wait(c.dve, m3)
            c.ve.did(c.dve.tensor_tensor(selw[:, t, :], selw[:, t, :], sel2[:, t, :], ALU.add))

    def next_slots():
        wait(c.dve, c.ve.now())
        m = c.ve.did(c.dve.tensor_scalar(slots[:], slots[:], float(P), None, ALU.add))
        wait(c.dve, m)

    def gather(*ready):
        wait(c.pe, *ready)
        for part in range(2):
            for k in range(KD):
                for t in range(TT):
                    last = c.pe.matmul(c.bank[6 + part][:, k * P:(k + 1) * P], xparts[:, part, t, k * P:(k + 1) * P], sel[:, t, :], start=t == 0, stop=t == TT - 1)
        wait(c.act, c.mm.did(last))
        for part in range(2):
            m = c.ac.did(c.act.copy(xg[:, part], c.bank[6 + part].rearrange("p (k n) -> p k n", k=KD)))
        return m

    for t in range(TT):
        select(t)
    for w in range(AHEAD):
        split_piece(w + pieces)
    gather(c.ve.now())

    def scatter(t, *ready):
        wait(c.pe, *ready)
        m = c.mm.did(c.pe.matmul(c.bank[6 + t % 2], selwt[:, t * P:(t + 1) * P], yrow[:], start=True, stop=True))
        wait(c.dve, m)
        return c.ve.did(c.dve.tensor_tensor(x[:, t, :], c.bank[6 + t % 2], x[:, t, :], ALU.add))

    def tile(j, has_next):
        expert = expert_of(j)
        before, gathered = c.ve.now(), c.ac.now()
        start = (c.cut.n, c.cut_pool.n)
        for w in range(pieces):
            slot = w % RAW
            wait(c.sp, is_split(w - RAW, start))
            load(c, c.in_[slot], raw[:, slot], A[n + "w"][bass.ds((expert * pieces + w) * P, P), :].rearrange("p (k n) -> p k n", k=KD))
        wait(c.pe, gathered)
        read = {}

        def piece(w, matmuls):
            if has_next or w + AHEAD < pieces:
                split_piece(w + AHEAD)
            wait(c.pe, is_split(w, start))
            return c.used.did(matmuls([cut[:, w % CUT, part] for part in range(2)]))

        def into_hidden(bank):
            def matmuls(parts):
                for k in range(KD):
                    last = product(c, bank, [xg[:, part, k, :] for part in range(2)], [p[:, k, :] for p in parts], k == 0, k == KD - 1)
                return last
            return matmuls

        def hidden(fb, then=lambda: None):
            banks = [c.bank[2 * (fb % 2)], c.bank[2 * (fb % 2) + 1]]
            part = h[:, fb * 512:(fb + 1) * 512]
            if fb >= 2:
                wait(c.pe, read[fb - 2])
            if not two:
                m = piece(fb, into_hidden(banks[0]))
                wait(c.act, m)
                read[fb] = c.ac.did(c.act.copy(part, banks[0]))
                return then()
            m = piece(2 * fb, into_hidden(banks[0]))
            then()
            m2 = piece(2 * fb + 1, into_hidden(banks[1]))
            wait(c.act, m)
            m = c.ac.did(c.act.activation(part, banks[0], ACT.Silu))
            wait(c.dve, m, m2)
            read[fb] = c.ve.did(c.dve.tensor_tensor(part, part, banks[1], ALU.mult))

        def turn_hidden(fb):
            bank = c.bank[4 + fb % 2]
            wait(c.pe, read[fb])
            if fb >= 2:
                wait(c.pe, read["t", fb - 2])
            for j in range(JB):
                last = c.pe.transpose(bank[:, j * P:(j + 1) * P], h[:, (fb * JB + j) * P:(fb * JB + j + 1) * P], c.ident[:])
            m = c.mm.did(last)
            wait(c.act, m)
            high, low = (ht[:, part, fb * JB:(fb + 1) * JB, :] for part in range(2))
            source = bank.rearrange("p (j n) -> p j n", j=JB)
            if not two:
                if fb == 0:
                    wait(c.act, biases)
                source = act_out[:, fb % 2]
                for j in range(JB):
                    m = c.ac.did(c.act.activation(source[:, j, :], bank[:, j * P:(j + 1) * P], ACT.Gelu, bias=bias1[:, fb * JB + j:fb * JB + j + 1]))
                wait(c.act, m)
            m = c.ac.did(c.act.copy(high, source))
            wait(c.dve, m)
            read["t", fb] = c.ve.did(c.dve.tensor_tensor(low, source, high.bitcast(F32), ALU.subtract))

        def out_of_hidden(db):
            def matmuls(parts):
                for i in range(JB):
                    f = db * JB + i
                    last = product(c, c.bank[OUT_BANK], [ht[:, part, f, :] for part in range(2)], [p[:, i, :] for p in parts], f == 0, f == FT - 1)
                return last
            return matmuls

        hidden(0)
        if not two:
            wait(c.act, gathered, before)
            for to, name in ((bias1, "b1"), (bias2, "b2")):
                c.bias.did(c.act.dma_start(to[:], A[n + name][bass.ds(expert * P, P), :]))
            biases = c.bias.now()
        added = [scatter(0, before), scatter(1, gathered)]
        hidden(1)
        turn_hidden(0)
        added += [scatter(2, added[0]), scatter(3, added[1])]
        def turn_weights():
            wait(c.pe, added[3])
            for t in range(TT):
                last = c.pe.transpose(c.bank[7][:, t * P:(t + 1) * P], selw[:, t, :], c.ident[:])
            turned = c.mm.did(last)
            wait(c.act, turned)
            marks["weights"] = c.ac.did(c.act.copy(selwt[:], c.bank[7]))
            if has_next:
                wait(c.dve, turned)
                next_slots()
                for t in range(TT):
                    select(t)
                marks["selected"] = c.ve.now()

        marks = {}
        hidden(2, turn_weights)
        turn_hidden(1)
        hidden(3)
        turn_hidden(2)
        if has_next:
            gather(marks["selected"], added[2], marks["weights"])
        for db in range(FB):
            wait(c.pe, read["t", db], *([read[3]] if db == 0 else []))
            m = piece(pieces - FB + db, out_of_hidden(db))
            if db == 0:
                turn_hidden(3)
        wait(c.dve, m)
        if two:
            c.ve.did(c.dve.tensor_copy(yrow[:], c.bank[OUT_BANK]))
        else:
            wait(c.dve, biases)
            c.ve.did(c.dve.tensor_tensor(yrow[:], c.bank[OUT_BANK], bias2[:], ALU.add))

    steps = {c.mm: 1 + FB + 1 + TT, c.used: pieces, c.cut: pieces - len(BY_POOL), c.cut_pool: len(BY_POOL),
             c.ac: pieces + 1 + 2 + FB + FB * (1 if two else 1 + JB),
             c.ve: 1 + TT * (5 if two else 2) + (FB if two else 0) + FB + 1 + TT,
             **{c.in_[r]: pieces // RAW for r in range(RAW)}}
    if not two:
        steps[c.bias] = 2
    with c.loop(tiles - 1, steps) as turn:
        tile(turn, True)
    tile(tiles - 1, False)
    added = [c.ve.now(), c.ac.now()]
    for t in range(TT):
        added.append(scatter(t, added[t]))
    c.barrier()


def experts_top1(c, A, x):
    with ExitStack() as st:
        wr = c.sb(st, "wr0", [P, KD, EXPERTS])
        br = c.sb(st, "br0", [P, TT, EXPERTS])
        small = c.sb(st, "small0", [P, 6, TT])
        prod = c.sb(st, "prod0", [P, TT, EXPERTS])
        ready = load(c, c.in_[7], wr[:], A["moe0_router"])
        c.ve.did(c.dve.memset(br[:], 0.0))
        xn, xt = normalize(c, st, x, "ln_m0")
        wait(c.pe, ready, c.ac.now())
        logits, best, hot = route(c, st, A, xt, 0, wr, br[:])
        rank, _ = ranks(c, st, 0, hot[:, :, 0, :])
        for t in range(TT):
            m = c.ve.did(c.dve.tensor_scalar(prod[:, t, :], logits[:, t, :], best[:, t, 0:1], None, ALU.subtract))
        wait(c.act, m)
        m = c.ac.did(c.act.activation(prod[:], prod[:], ACT.Exp))
        wait(c.dve, m)
        total, weight, r, e, valid, slot = (small[:, k, :] for k in range(6))
        m = c.ve.did(c.dve.tensor_reduce(total, prod[:], X, ALU.add))
        wait(c.dve, m)
        c.ve.did(c.dve.reciprocal(weight, total))
        m = c.ve.did(c.dve.tensor_tensor(prod[:], hot[:, :, 0, :], rank[:], ALU.mult))
        wait(c.dve, m)
        m = c.ve.did(c.dve.tensor_reduce(r, prod[:], X, ALU.add))
        wait(c.dve, m)
        m = c.ve.did(c.dve.tensor_tensor(prod[:], hot[:, :, 0, :], c.iota[:, None, 0:EXPERTS].to_broadcast([P, TT, EXPERTS]), ALU.mult))
        wait(c.dve, m)
        m = c.ve.did(c.dve.tensor_reduce(e, prod[:], X, ALU.add))
        c.ve.did(c.dve.tensor_scalar(valid, r, float(CAPACITY), None, ALU.is_le))
        wait(c.dve, c.ve.now())
        m = c.ve.did(c.dve.scalar_tensor_tensor(slot, e, float(P), r, ALU.mult, ALU.add))
        wait(c.dve, m)
        m = c.ve.did(c.dve.tensor_tensor(slot, slot, valid, ALU.mult))
        wait(c.dve, m)
        m = c.ve.did(c.dve.tensor_scalar(slot, slot, -1.0, None, ALU.add))
        wait(c.dve, m)
        expert_tiles(c, st, A, x, xn, [slot], [weight], 0, EXPERTS, lambda turn: turn)


def experts_top2(c, A, x):
    with ExitStack() as st:
        wr = c.sb(st, "wr1", [P, KD, EXPERTS])
        br = c.sb(st, "br1", [P, TT, EXPERTS])
        small = c.sb(st, "small1", [P, 5, TT])
        prod = c.sb(st, "prod1", [P, TT, EXPERTS])
        chosen = c.sb(st, "chosen1", [P, TT, EXPERTS])
        tile_of = c.sb(st, "tile_of", [P, 4, EXPERTS])
        owner = c.sb(st, "owner", [1, TILES1, EXPERTS])
        ownerf = c.sb(st, "ownerf", [1, TILES1])
        owneri = c.sb(st, "owneri", [1, TILES1], I32)
        load(c, c.in_[7], wr[:], A["moe1_router"])
        for t in range(TT):
            ready = load(c, c.in_[7], br[:, t, :], A["moe1_router_b"].partition_broadcast(P))
        xn, xt = normalize(c, st, x, "ln_m1")
        wait(c.pe, ready, c.ac.now())
        wait(c.dve, ready)
        logits, best, hot = route(c, st, A, xt, 1, wr, br[:])
        m = c.ve.did(c.dve.tensor_tensor(chosen[:], hot[:, :, 0, :], hot[:, :, 1, :], ALU.add))
        rank, count = ranks(c, st, 1, chosen)
        d, w1, w2, slot1, slot2 = (small[:, k, :] for k in range(5))
        m = c.ve.did(c.dve.tensor_tensor(d, best[:, :, 1], best[:, :, 0], ALU.subtract))
        wait(c.act, m)
        m = c.ac.did(c.act.activation(d, d, ACT.Exp))
        wait(c.dve, m)
        m = c.ve.did(c.dve.tensor_scalar(w2, d, 1.0, None, ALU.add))
        wait(c.dve, m)
        m = c.ve.did(c.dve.reciprocal(w1, w2))
        wait(c.dve, m)
        c.ve.did(c.dve.tensor_tensor(w2, d, w1, ALU.mult))
        need, end, start, part = (tile_of[:, k, :] for k in range(4))
        m = c.ve.did(c.dve.tensor_scalar(need, count[:], 0.0, None, ALU.is_gt))
        for k in range(1, TT):
            wait(c.dve, m)
            m = c.ve.did(c.dve.scalar_tensor_tensor(need, count[:], float(k * P), need, ALU.is_gt, ALU.add))
        wait(c.dve, m)
        m = c.ve.did(c.dve.tensor_tensor_scan(end, c.ones[:, 0:EXPERTS], need, 0.0, ALU.mult, ALU.add))
        wait(c.dve, m)
        m = c.ve.did(c.dve.tensor_tensor(start, end, need, ALU.subtract))
        wait(c.dve, m)
        m = c.ve.did(c.dve.tensor_scalar(start, start, float(P), -1.0, ALU.mult, ALU.add))
        wait(c.dve, m)
        m = c.ve.did(c.dve.tensor_tensor(chosen[:], rank[:], start[:, None, :].to_broadcast([P, TT, EXPERTS]), ALU.add))
        wait(c.dve, m)
        for j, slot in ((0, slot1), (1, slot2)):
            m = c.ve.did(c.dve.tensor_tensor(prod[:], hot[:, :, j, :], chosen[:], ALU.mult))
            wait(c.dve, m)
            m = c.ve.did(c.dve.tensor_reduce(slot, prod[:], X, ALU.add))
            wait(c.dve, m)
        m = c.ve.did(c.dve.tensor_tensor(owner[:], end[0:1, None, :].to_broadcast([1, TILES1, EXPERTS]),
                                         c.iota[0:1, 0:TILES1, None].to_broadcast([1, TILES1, EXPERTS]), ALU.is_le))
        wait(c.dve, m)
        m = c.ve.did(c.dve.tensor_reduce(ownerf[:], owner[:], X, ALU.add))
        wait(c.dve, m)
        m = c.ve.did(c.dve.tensor_scalar(ownerf[:], ownerf[:], float(EXPERTS - 1), None, ALU.min))
        wait(c.dve, m)
        m = c.ve.did(c.dve.tensor_copy(owneri[:], ownerf[:]))
        wait(c.sp, m)
        expert_tiles(c, st, A, x, xn, [slot1, slot2], [w1, w2], 1, TILES1,
                     lambda turn: c.sp.value_load(owneri[0:1, bass.ds(turn, 1)], min_val=0, max_val=EXPERTS - 1))


def delta_rule(c, A, x):
    with ExitStack() as st:
        w = [c.sb(st, "dw_" + n, [P, KD, D]) for n in "qkvo"]
        wb = c.sb(st, "dw_b", [P, KD, DHEADS])
        taps = c.sb(st, "taps", [P, 3, KD, CONV])
        g_rms = c.sb(st, "g_rms", [P, 1])
        ln = c.sb(st, "ln_gb", [P, 2, D])
        padded = c.sb(st, "dpadded", [P, 2, TOK + CONV - 1])
        feat = [c.sb(st, "feat_" + n, [P, DHEADS, TOK]) for n in "qkv"]
        conv = c.sb(st, "dconv", [P, 2, TOK])
        square = c.sb(st, "dsquare", [P, 2, TOK])
        beta = c.sb(st, "beta", [P, TT, DHEADS])
        lengths = c.sb(st, "lengths", [P, 2 * DHEADS * TT])
        diag = c.sb(st, "diag", [P, 2, TT, P])
        small = {}
        for to, n in zip(w, "qkvo"):
            small[n] = load(c, c.in_["qkvo".index(n)], to[:], A["d_w" + n])
        load(c, c.in_[4], taps[:], A["d_taps"])
        load(c, c.in_[4], wb[:], A["d_wb"])
        load(c, c.in_[4], g_rms[:], A["d_rms"])
        load(c, c.in_[4], ln[:, 0, :], A["d_lng"].partition_broadcast(P))
        ready = load(c, c.in_[4], ln[:, 1, :], A["d_lnb"].partition_broadcast(P))
        m = c.ve.did(c.dve.memset(padded[:, :, 0:CONV - 1], 0.0))
        wait(c.act, m)
        xn, xt = normalize(c, st, x, "ln_d")
        wait(c.pe, c.ac.now())
        wait(c.dve, ready)
        wait(c.pool, c.ve.now(), ready)
        for t in range(TT):
            x_ready = c.go.did(c.pool.tensor_tensor(x[:, t, :], x[:, t, :], ln[:, 1, :], ALU.add))
        copied, convolved, silued, squared, summed = {}, {}, {}, {}, {}

        def silu(n):
            wait(c.act, convolved[n])
            silued[n] = c.ac.did(c.act.activation(feat[n // DHEADS][:, n % DHEADS, :], conv[:, n % 2, :], ACT.Silu))
            if n < 2 * DHEADS:
                wait(c.pool, silued[n])
                if n > 1:
                    wait(c.pool, summed[n - 2])
                of = feat[n // DHEADS][:, n % DHEADS, :]
                squared[n] = c.go.did(c.pool.tensor_tensor(square[:, n % 2, :], of, of, ALU.mult))

        def sum_squares(n):
            wait(c.pe, squared[n])
            for t in range(TT):
                last = c.pe.matmul(c.bank[4][:, n * TT + t:n * TT + t + 1], square[:, n % 2, t * P:(t + 1) * P], c.ones[:, 0:1], start=True, stop=True)
            summed[n] = c.mm.did(last)

        for n in range(3 * DHEADS):
            i, b, r = n // DHEADS, n % DHEADS, n % 2
            if b == 0:
                wait(c.pe, small["qkv"[i]])
            if n > 1:
                wait(c.pe, copied[n - 2])
            m = linear_t(c, c.bank[r][:], w[i], xt, b)
            wait(c.act, m)
            if n > 1:
                wait(c.act, convolved[n - 2])
            copied[n] = c.ac.did(c.act.copy(padded[:, r, CONV - 1:], c.bank[r][:]))
            if 2 < n < 2 * DHEADS + 3:
                sum_squares(n - 3)
            if n > 0:
                silu(n - 1)
            wait(c.dve, copied[n])
            if n > 1:
                wait(c.dve, silued[n - 2])
            m = c.ve.did(c.dve.tensor_scalar(conv[:, r, :], padded[:, r, 0:TOK], taps[:, i, b, 0:1], None, ALU.mult))
            for j in range(1, CONV):
                wait(c.dve, m)
                m = c.ve.did(c.dve.scalar_tensor_tensor(conv[:, r, :], padded[:, r, j:j + TOK], taps[:, i, b, j:j + 1], conv[:, r, :], ALU.mult, ALU.add))
            convolved[n] = m
        wait(c.pe, ready)
        for t in range(TT):
            for k in range(KD):
                last = c.pe.matmul(c.bank[5][:, t * DHEADS:(t + 1) * DHEADS], xt[:, k, t * P:(t + 1) * P], wb[:, k, :], start=k == 0, stop=k == KD - 1)
        m = c.mm.did(last)
        silu(3 * DHEADS - 1)
        wait(c.act, m)
        beta_done = c.ac.did(c.act.activation(beta[:], c.bank[5][:, 0:TT * DHEADS].rearrange("p (t h) -> p t h", t=TT), ACT.Sigmoid))
        wait(c.dve, summed[2 * DHEADS - 1])
        m = c.ve.did(c.dve.tensor_scalar(lengths[:], c.bank[4][:, 0:2 * DHEADS * TT], 1e-6, None, ALU.add))
        wait(c.act, m)
        m = c.ac.did(c.act.activation(lengths[:], lengths[:], ACT.Sqrt))
        wait(c.dve, m)
        m = c.ve.did(c.dve.reciprocal(lengths[:], lengths[:]))
        wait(c.pool, m)
        spread, unit = {}, {}
        for n in [*range(DHEADS, 2 * DHEADS), *range(DHEADS)]:
            i, b = n // DHEADS, n % DHEADS
            r = b % 2
            if len(spread) > 1:
                wait(c.pool, list(spread.values())[-2])
            m = c.go.did(c.pool.tensor_tensor(diag[:, r], c.ident[:, None, :].to_broadcast([P, TT, P]),
                                              lengths[:, n * TT:(n + 1) * TT, None].to_broadcast([P, TT, P]), ALU.mult))
            wait(c.pe, m)
            if len(unit) > 1:
                wait(c.pe, list(unit.values())[-2])
            spread[n] = c.mm.did(c.pe.matmul(c.bank[6 + r][:], c.ones[:], diag[:, r].rearrange("p t n -> p (t n)"), start=True, stop=True))
            wait(c.dve, spread[n])
            unit[n] = c.ve.did(c.dve.tensor_tensor(feat[i][:, b, :], feat[i][:, b, :], c.bank[6 + r][:], ALU.mult))
        k_unit, q_unit = unit[2 * DHEADS - 1], unit[DHEADS - 1]
        q, k, v = feat
        per = lambda n: c.sb(st, n, [P, TT, DHEADS, P])
        below, below_t, inv, inv_t, qk, vrow, krow = (per("d_" + n) for n in ("below", "below_t", "inv", "inv_t", "qk", "vrow", "krow"))
        lev = diag
        prod = c.sb(st, "d_prod", [P, 2, DHEADS, P])
        flat = lambda a: a.rearrange("p h n -> p (h n)")
        over_heads = lambda mask: mask[:, None, :].to_broadcast([P, DHEADS, P])
        heads_of = lambda bank: bank[:].rearrange("p (h n) -> p h n", h=DHEADS)

        def four(bank, lhs, rhs):
            for h in range(DHEADS):
                last = c.pe.matmul(bank[:, h * P:(h + 1) * P], lhs(h), rhs(h), start=True, stop=True)
            return c.mm.did(last)

        def four_transposes(bank, of):
            for h in range(DHEADS):
                last = c.pe.transpose(bank[:, h * P:(h + 1) * P], of(h), c.ident[:])
            return c.mm.did(last)

        below_done, qk_done, v_done, k_done, t_done = {}, {}, {}, {}, {}
        inv_t_done, inv_done = {}, {}

        def gram(t):
            at = slice(t * P, (t + 1) * P)
            wait(c.pe, below_done[t - 2] if t > 1 else k_unit)
            m = four(c.bank[t % 2], lambda h: k[:, h, at], lambda h: k[:, h, at])
            wait(c.dve, m)
            for h in range(DHEADS):
                m = c.ve.did(c.dve.scalar_tensor_tensor(below[:, t, h, :], c.bank[t % 2][:, h * P:(h + 1) * P], beta[:, t, h:h + 1], c.lower[:], ALU.mult, ALU.mult))
            below_done[t] = m

        wait(c.dve, beta_done)
        wait(c.pe, silued[3 * DHEADS - 1])
        gram(0)
        gram(1)
        for t in range(TT):
            at = slice(t * P, (t + 1) * P)
            wait(c.pe, qk_done[t - 1] if t else q_unit)
            m = four(c.bank[2], lambda h: k[:, h, at], lambda h: q[:, h, at])
            wait(c.dve, m)
            qk_done[t] = c.ve.did(c.dve.tensor_tensor(qk[:, t], heads_of(c.bank[2]), over_heads(c.upto), ALU.mult))
            if t:
                wait(c.pe, k_done[t - 1])
            m = four_transposes(c.bank[3], lambda h: v[:, h, at])
            wait(c.act, m)
            v_done[t] = c.ac.did(c.act.copy(flat(vrow[:, t]), c.bank[3][:]))
            m = four_transposes(c.bank[4], lambda h: k[:, h, at])
            wait(c.act, m)
            k_done[t] = c.ac.did(c.act.copy(flat(krow[:, t]), c.bank[4][:]))
            wait(c.pe, below_done[t])
            if t > 1:
                wait(c.pe, t_done[t - 2])
            m = four_transposes(c.bank[5 + t % 2], lambda h: below[:, t, h, :])
            wait(c.act, m)
            t_done[t] = c.ac.did(c.act.copy(flat(below_t[:, t]), c.bank[5 + t % 2][:]))
            if t + 2 < TT:
                gram(t + 2)
            wait(c.pool, below_done[t])
            m = c.go.did(c.pool.tensor_tensor(inv[:, t], below[:, t], over_heads(c.level0), ALU.mult))
            wait(c.pool, m)
            inv_done[t] = c.go.did(c.pool.tensor_tensor(inv[:, t], over_heads(c.ident), inv[:, t], ALU.subtract))
            wait(c.dve, t_done[t])
            m = c.ve.did(c.dve.tensor_tensor(inv_t[:, t], below_t[:, t], over_heads(c.level_t[0]), ALU.mult))
            wait(c.dve, m)
            inv_t_done[t] = c.ve.did(c.dve.tensor_tensor(inv_t[:, t], over_heads(c.ident), inv_t[:, t], ALU.subtract))
        STEPS = (LEVELS - 1) * TT
        masked, first, product_copied = {}, {}, {}

        def mask_level(i):
            t = i % TT
            if i > 1:
                wait(c.dve, first[i - 2])
            else:
                wait(c.dve, c.mm.now(), t_done[t])
            masked[i] = c.ve.did(c.dve.tensor_tensor(lev[:, i % 2], below_t[:, t], over_heads(c.level_t[1 + i // TT]), ALU.mult))

        def first_product(i):
            t = i % TT
            wait(c.pe, masked[i], inv_done[t], inv_t_done[t])
            if i > 1:
                wait(c.pe, product_copied[i - 2])
            else:
                wait(c.pe, c.ve.now())
            first[i] = four(c.bank[i % 2], lambda h: lev[:, i % 2, h, :], lambda h: inv[:, t, h, :])
            wait(c.act, first[i])
            product_copied[i] = c.ac.did(c.act.copy(flat(prod[:, i % 2]), c.bank[i % 2][:]))

        def second_products(i):
            t, r = i % TT, i % 2
            banks = c.bank[2 + 2 * (i % 3):4 + 2 * (i % 3)]
            wait(c.pe, product_copied[i])
            if i < 3:
                wait(c.pe, k_done[TT - 1], t_done[TT - 1], qk_done[TT - 1])
            else:
                wait(c.pe, inv_t_done[(i - 3) % TT])
            m = four(banks[1], lambda h: prod[:, r, h, :], lambda h: inv_t[:, t, h, :])
            if i < STEPS - TT:
                m = four(banks[0], lambda h: inv_t[:, t, h, :], lambda h: prod[:, r, h, :])
            wait(c.dve, m)
            if i < STEPS - TT:
                inv_done[t] = c.ve.did(c.dve.tensor_tensor(inv[:, t], inv[:, t], heads_of(banks[0]), ALU.subtract))
            inv_t_done[t] = c.ve.did(c.dve.tensor_tensor(inv_t[:, t], inv_t[:, t], heads_of(banks[1]), ALU.subtract))

        mask_level(0)
        mask_level(1)
        first_product(0)
        for i in range(1, STEPS):
            if i + 1 < STEPS:
                mask_level(i + 1)
            first_product(i)
            second_products(i - 1)
        second_products(STEPS - 1)
        S = c.sb(st, "d_state", [P, 2, DHEADS, P])
        rhs = c.sb(st, "d_rhs", [P, DHEADS, P])
        u = c.sb(st, "d_u", [P, 2, DHEADS, P])
        o = c.sb(st, "d_o", [P, TT, DHEADS, P])
        osq = qk
        rms = c.sb(st, "d_rms_of", [P, 2, TT, DHEADS])
        state = c.ve.did(c.dve.memset(flat(S[:, 0]), 0.0))
        outputs, u_done = {}, {}

        def chunk_output(t):
            at = slice(t * P, (t + 1) * P)
            bank = c.bank[4 + t % 2]
            if t > 1:
                wait(c.pe, outputs[t - 2])
            for h in range(DHEADS):
                c.pe.matmul(bank[:, h * P:(h + 1) * P], q[:, h, at], S[:, t % 2, h, :], start=True, stop=False)
                last = c.pe.matmul(bank[:, h * P:(h + 1) * P], qk[:, t, h, :], u[:, t % 2, h, :], start=False, stop=True)
            m = c.mm.did(last)
            wait(c.act, m)
            outputs[t] = c.ac.did(c.act.copy(flat(o[:, t]), bank[:]))
            wait(c.pool, outputs[t])
            return c.go.did(c.pool.tensor_tensor(osq[:, t], o[:, t], o[:, t], ALU.mult))

        for t in range(TT):
            at = slice(t * P, (t + 1) * P)
            s = t % 2
            wait(c.pe, state)
            m = four(c.bank[0], lambda h: k[:, h, at], lambda h: S[:, s, h, :])
            wait(c.dve, m, v_done[t])
            m = c.ve.did(c.dve.tensor_tensor(rhs[:], vrow[:, t], heads_of(c.bank[0]), ALU.subtract))
            wait(c.dve, m)
            rhs_done = c.ve.did(c.dve.tensor_tensor(rhs[:], rhs[:], beta[:, t, :, None].to_broadcast([P, DHEADS, P]), ALU.mult))
            if t:
                squares = chunk_output(t - 1)
            wait(c.pe, rhs_done, inv_t_done[t])
            m = four(c.bank[1], lambda h: inv_t[:, t, h, :], lambda h: rhs[:, h, :])
            wait(c.act, m)
            u_done[t] = c.ac.did(c.act.copy(flat(u[:, s]), c.bank[1][:]))
            wait(c.pe, u_done[t])
            if t + 1 < TT:
                m = four(c.bank[2], lambda h: krow[:, t, h, :], lambda h: u[:, s, h, :])
                wait(c.dve, m)
                state = c.ve.did(c.dve.tensor_tensor(S[:, 1 - s], S[:, s], heads_of(c.bank[2]), ALU.add))
            if t:
                wait(c.dve, squares)
                c.ve.did(c.dve.tensor_reduce(rms[:, 0, t - 1], osq[:, t - 1], X, ALU.add))
        squares = chunk_output(TT - 1)
        wait(c.dve, squares)
        m = c.ve.did(c.dve.tensor_reduce(rms[:, 0, TT - 1], osq[:, TT - 1], X, ALU.add))
        wait(c.dve, m)
        m = c.ve.did(c.dve.tensor_scalar(rms[:, 0], rms[:, 0], 1.0 / P, EPS, ALU.mult, ALU.add))
        wait(c.act, m)
        m = c.ac.did(c.act.activation(rms[:, 1], rms[:, 0], ACT.Sqrt))
        wait(c.dve, m)
        m = c.ve.did(c.dve.reciprocal(rms[:, 0], rms[:, 1]))
        wait(c.dve, m)
        stats = c.sb(st, "y_stats", [P, TT, 6])
        mv = c.sb(st, "y_mv", [P, TT, 2])
        std = c.sb(st, "y_std", [P, TT, 2])
        scaled, columns = {}, {}
        for t in range(TT):
            scaled[t] = c.ve.did(c.dve.tensor_tensor(o[:, t], o[:, t], rms[:, 0, t, :, None].to_broadcast([P, DHEADS, P]), ALU.mult))
        wait(c.act, ready)
        wait(c.pe, small["o"])
        for t in range(TT):
            wait(c.pe, scaled[t])
            m = four_transposes(c.bank[4 + t], lambda h: o[:, t, h, :])
            wait(c.act, m)
            columns[t] = c.ac.did(c.act.activation(xt[:, :, t * P:(t + 1) * P], heads_of(c.bank[4 + t]), ACT.Identity, scale=g_rms[:, 0:1]))
        for t in range(TT):
            wait(c.pe, columns[t])
            for h in range(DHEADS):
                last = c.pe.matmul(c.bank[t][:], xt[:, h, t * P:(t + 1) * P], w[3][:, h, :], start=h == 0, stop=h == DHEADS - 1)
            m = c.mm.did(last)
            wait(c.dve, m)
            m = c.ve.did(c.dve.tensor_tensor(xn[:, t, :], xn[:, t, :], c.bank[t][:], ALU.add))
            wait(c.dve, m)
            m = c.ve.did(c.dve.bn_stats(stats[:, t, :], xn[:, t, :]))
            wait(c.dve, m)
            c.ve.did(c.dve.bn_aggr(mv[:, t, :], stats[:, t, :]))
        wait(c.dve, c.ve.now())
        m = c.ve.did(c.dve.tensor_scalar(std[:, :, 0], mv[:, :, 1], EPS, None, ALU.add))
        wait(c.act, m)
        m = c.ac.did(c.act.activation(std[:, :, 1], std[:, :, 0], ACT.Sqrt))
        wait(c.dve, m)
        m = c.ve.did(c.dve.reciprocal(std[:, :, 0], std[:, :, 1]))
        wait(c.dve, m, x_ready)
        for t in range(TT):
            c.ve.did(c.dve.tensor_scalar(xn[:, t, :], xn[:, t, :], mv[:, t, 0:1], std[:, t, 0:1], ALU.subtract, ALU.mult))
        for t in range(TT):
            wait(c.dve, c.ve.now(TT - 1))
            c.ve.did(c.dve.tensor_tensor(xn[:, t, :], xn[:, t, :], ln[:, 0, :], ALU.mult))
        for t in range(TT):
            wait(c.dve, c.ve.now(TT - 1))
            c.ve.did(c.dve.tensor_tensor(x[:, t, :], x[:, t, :], xn[:, t, :], ALU.add))
        c.barrier()


def perceiver(nc, A, out, stages=range(1, 8)):
    with ExitStack() as ctx:
        c = Core(nc, ctx)
        scratch = {
            "k": nc.dram_tensor("k_parts", [2, 2, D, KEYS], F32, kind="Internal").ap(),
            "v": nc.dram_tensor("v_heads", [2, HEADS, P, KT, DH], F32, kind="Internal").ap(),
            "q": nc.dram_tensor("q_parts", [2, 2, D, TOK], F32, kind="Internal").ap(),
            "heads": nc.dram_tensor("head_outputs", [D, TOK], F32, kind="Internal").ap(),
        }
        x = c.sb(ctx, "x_rows", [P, TT, D])
        const = c.sb(ctx, "constants", [P, CONST_COLS])
        for name, (lo, hi) in CONST_AT.items():
            c.const[name] = const[:, lo:hi]
        c.ident, c.ones, c.iota, c.upto, c.lower, c.level0, c.fold, c.pick = (
            c.const[n] for n in ("ident", "ones", "iota", "upto", "lower", "level0", "fold", "pick"))
        c.level_t = [c.const["level_t"][:, k * P:(k + 1) * P] for k in range(LEVELS)]
        if 1 in stages:
            project_context(c, A, scratch, x, const)
        if 2 in stages:
            cross_attention(c, A, scratch, x, 0)
        if 3 in stages:
            selective_scan(c, A, x)
        if 4 in stages:
            experts_top1(c, A, x)
        if 5 in stages:
            cross_attention(c, A, scratch, x, 1)
        if 6 in stages:
            delta_rule(c, A, x)
        if 7 in stages:
            experts_top2(c, A, x)
        c.out[0].did(nc.sync.dma_start(out.rearrange("(t p) d -> p t d", p=P), x[:]))
        wait(nc.sync, c.out[0].now())


CONST_AT, CONST_COLS = {}, 0
for _name, _cols in (("ident", P), ("ones", P), ("iota", P), ("upto", P), ("lower", P), ("level0", P),
                     ("level_t", LEVELS * P), ("fold", DH), ("pick", DSTATE * P)):
    CONST_AT[_name] = (CONST_COLS, CONST_COLS + _cols)
    CONST_COLS += _cols



def constants(np):
    i, j = np.arange(P)[:, None], np.arange(P)[None, :]
    level = [(i // (2 << n) == j // (2 << n)) & ((i >> n) % 2 == 1) & ((j >> n) % 2 == 0) for n in range(LEVELS)]
    parts = {
        "ident": i == j, "ones": i + j >= 0, "iota": j + 0 * i, "upto": i <= j, "lower": i > j, "level0": level[0],
        "level_t": np.concatenate([m.T for m in level], 1),
        "fold": i % DH == j[:, :DH],
        "pick": np.concatenate([(i == s) & (j >= 0) for s in range(DSTATE)], 1),
    }
    return np.concatenate([parts[n].astype(np.float32) for n in CONST_AT], 1)


def arrange(np, x, ctx_1024, **w):
    def rows(a, k=None):
        return a.reshape(-1, P, a.shape[-1]).transpose(1, 0, 2)

    def column(a):
        return a.reshape(-1, P).T

    ipw, ipb = w["L1_xattn_in_proj_weight"], w["L1_xattn_in_proj_bias"]
    g, u, dn = w["L1_ffn_gate_w"], w["L1_ffn_up_w"], w["L1_ffn_down_w"]

    def in_pieces(a):
        return a.reshape(EXPERTS, KD, P, FB, 512).transpose(0, 3, 2, 1, 4).reshape(EXPERTS, FB, P, KD * 512)

    def out_pieces(a):
        return a.reshape(EXPERTS, FB, 4, P, D).transpose(0, 1, 3, 2, 4).reshape(EXPERTS, FB, P, 4 * D)

    gu = np.stack([in_pieces(g.transpose(0, 2, 1)), in_pieces(u.transpose(0, 2, 1))], 2).reshape(EXPERTS, 2 * FB, P, KD * 512)
    A = {
        "constants": constants(np),
        "x": x.reshape(TOK, D),
        "ctx": ctx_1024.reshape(NCHUNK, CHUNK, KD, P).transpose(0, 3, 2, 1).reshape(NCHUNK * P, KD * CHUNK),
        "wq": np.stack([rows(w["L0_xattn_W_Q"]), rows(ipw[0:D].T)]),
        "wk": np.stack([rows(w["L0_xattn_W_K"]), rows(ipw[D:2 * D].T)]),
        "wv": np.stack([rows(w["L0_xattn_W_V"]), rows(ipw[2 * D:].T)]),
        "wo": np.stack([rows(w["L0_xattn_W_O"]), rows(w["L1_xattn_out_w"].T)]),
        "bq": np.stack([column(w["L0_xattn_b_Q"]), column(ipb[0:D])]),
        "bk": np.stack([column(w["L0_xattn_b_K"]), column(ipb[D:2 * D])]),
        "bv": np.stack([w["L0_xattn_b_V"], ipb[2 * D:]]),
        "bo": np.stack([w["L0_xattn_b_O"], w["L1_xattn_out_b"]]),
        "w_in": rows(w["L0_attn_W_in"].T),
        "w_out": rows(w["L0_attn_W_out"].T),
        "w_xproj": rows(w["L0_attn_W_xproj"].T),
        "w_dt": w["L0_attn_W_dt"].T,
        "chan": np.concatenate([
            rows(np.concatenate([w["L0_attn_Kx"], w["L0_attn_Kz"]]).reshape(D, 3)),
            rows(np.concatenate([w["L0_attn_b_dt"]] * 2).reshape(D, 1)),
            rows(np.concatenate([w["L0_attn_D"]] * 2).reshape(D, 1)),
            rows(np.concatenate([w["L0_attn_A_log"]] * 2))], 2),
        "moe0_router": rows(w["L0_ffn_wg"]),
        "moe0_w": np.concatenate([in_pieces(w["L0_ffn_W1"]), out_pieces(w["L0_ffn_W2"])], 1).reshape(-1, KD * 512),
        "moe0_b1": w["L0_ffn_b1"].reshape(EXPERTS, FT, P).transpose(0, 2, 1).reshape(EXPERTS * P, FT),
        "moe0_b2": np.repeat(w["L0_ffn_b2"], P, axis=0),
        "d_wq": rows(w["L1_attn_Wq"]), "d_wk": rows(w["L1_attn_Wk"]), "d_wv": rows(w["L1_attn_Wv"]),
        "d_wo": rows(w["L1_attn_Wo"]), "d_wb": rows(w["L1_attn_Wb"]),
        "d_taps": np.stack([rows(w["L1_attn_conv_" + n].T) for n in "qkv"], 1),
        "d_rms": w["L1_attn_g_rms"].reshape(P, 1),
        "d_lng": w["L1_attn_ln_g"], "d_lnb": w["L1_attn_ln_b"],
        "moe1_router": rows(w["L1_ffn_router_w"].T),
        "moe1_router_b": w["L1_ffn_router_b"],
        "moe1_w": np.concatenate([gu, out_pieces(dn.transpose(0, 2, 1))], 1).reshape(-1, KD * 512),
    }
    return {name: np.ascontiguousarray(a) for name, a in A.items()}


def kernel(**inputs):
    import numpy as np
    import concourse.bacc as bacc
    from concourse.bass_utils import run_bass_kernel_spmd

    arrays = arrange(np, **{k: np.asarray(v) for k, v in inputs.items()})
    nc = bacc.Bacc("TRN2", target_bir_lowering=False, num_devices=1)
    aps = {name: nc.dram_tensor("in_" + name, a.shape, mybir.dt.from_np(a.dtype), kind="ExternalInput").ap() for name, a in arrays.items()}
    out = nc.dram_tensor("out", (TOK, D), F32, kind="ExternalOutput").ap()
    perceiver(nc, aps, out)
    result = run_bass_kernel_spmd(nc, [{"in_" + name: a for name, a in arrays.items()}], core_ids=[0])
    return result.results[0]["out"].reshape(1, TOK, D)
```
